# Optimizing a Trainium2 kernel written in Bass

```python
import numpy as np
import jax
import jax.numpy as jnp

def _softmax(x, axis=-1):
    return jax.nn.softmax(x, axis=axis)

def _gelu(x):
    return jax.nn.gelu(x, approximate=True)

def _silu(x):
    return jax.nn.silu(x)

def _sigmoid(x):
    return jax.nn.sigmoid(x)

def _layernorm(x, axis=-1, eps=1e-05):
    m = jnp.mean(x, axis=axis, keepdims=True)
    v = jnp.var(x, axis=axis, keepdims=True)
    return (x - m) / jnp.sqrt(v + eps)

def _scatter_add(tgt, idx, src, axis=0):
    return tgt.at[idx].add(src)

def _segment_sum(src, seg, n):
    return jax.ops.segment_sum(src, seg, n)
kernel_name = 'mk_gps_d1_gnn_r32_8f4f3d'

def setup_inputs(seed: int=0):
    np.random.seed(seed)
    _w = jnp.asarray

    def _rec_inputs():
        import jax
        import jax.numpy as jnp
        _gk = jax.random.key(seed)
        x = -0.0002928 + 1 * jax.random.normal(jax.random.fold_in(_gk, 1), (3125, 256), jnp.float32)
        src = jax.random.randint(jax.random.fold_in(_gk, 2), (50000,), 0, 3125, jnp.int32)
        dst = jax.random.randint(jax.random.fold_in(_gk, 3), (50000,), 0, 3125, jnp.int32)
        _o = jnp.argsort(dst, stable=True)
        src = src[_o]
        dst = dst[_o]
        return (x, src, dst)
    x, src, dst = _rec_inputs()

    def _L0_gnn_setup():
        import jax, jax.numpy as jnp
        import numpy as np
        N_NODES = 512
        N_EDGES = 8192
        D_IN = 256
        D = 256
        H = 512
        E = 64
        TOP_K = 2
        CAP = 1024
        BN_EPS = 1e-05

        def _moe_ff(x, Wg, bg, w1, b1, w2, b2):
            N = x.shape[0]
            logits = x @ Wg + bg
            vals, idx = jax.lax.top_k(logits, TOP_K)
            gates = jax.nn.softmax(vals, axis=-1)
            e_flat = idx.reshape(-1)
            g_flat = gates.reshape(-1)
            tok = jnp.arange(N * TOP_K) // TOP_K
            order = jnp.argsort(e_flat)
            e_s, tok_s, g_s = (e_flat[order], tok[order], g_flat[order])
            counts = jnp.bincount(e_flat, length=E)
            offs = jnp.concatenate([jnp.zeros((1,), counts.dtype), jnp.cumsum(counts)[:-1]])
            rank = jnp.arange(N * TOP_K) - offs[e_s]
            valid = rank < CAP
            slot = jnp.where(valid, e_s * CAP + rank, E * CAP)
            buf = jnp.zeros((E * CAP + 1, D), x.dtype).at[slot].set(x[tok_s])
            h = buf[:E * CAP].reshape(E, CAP, D)
            h1 = jax.nn.gelu(jnp.einsum('ecd,edh->ech', h, w1) + b1[:, None, :], approximate=False)
            h2 = jnp.einsum('ech,ehd->ecd', h1, w2) + b2[:, None, :]
            out_buf = h2.reshape(E * CAP, D)
            y_s = jnp.where(valid[:, None], out_buf[jnp.minimum(slot, E * CAP - 1)], 0.0)
            return jnp.zeros((N, D), x.dtype).at[tok_s].add(g_s[:, None] * y_s)

        def _forward(feats, W_gc, b_gc, W_res, b_res, Wg, bg, w1, b1, w2, b2, gamma, beta, src, dst):
            n = feats.shape[0]
            ones = jnp.ones((src.shape[0],), feats.dtype)
            deg_out = jnp.clip(jax.ops.segment_sum(ones, src, num_segments=n), 1.0)
            deg_in = jnp.clip(jax.ops.segment_sum(ones, dst, num_segments=n), 1.0)
            h = feats * jax.lax.rsqrt(deg_out)[:, None]
            m = jax.ops.segment_sum(h[src], dst, num_segments=n) * jax.lax.rsqrt(deg_in)[:, None]
            gc = m @ W_gc + b_gc
            x = gc + (feats @ W_res + b_res)
            core = _moe_ff(x, Wg, bg, w1, b1, w2, b2)
            y = x + core
            mean = jnp.mean(y, axis=0)
            var = jnp.mean((y - mean) ** 2, axis=0)
            return (y - mean) * jax.lax.rsqrt(var + BN_EPS) * gamma + beta
        key = jax.random.key(seed)
        ks = jax.random.split(key, 16)
        s = lambda d: 1.0 / np.sqrt(d)
        inp = {'feats': jax.random.normal(ks[0], (N_NODES, D_IN), jnp.float32), 'W_gc': jax.random.normal(ks[1], (D_IN, D), jnp.float32) * s(D_IN), 'b_gc': jnp.zeros((D,), jnp.float32), 'W_res': jax.random.normal(ks[2], (D_IN, D), jnp.float32) * s(D_IN), 'b_res': jnp.zeros((D,), jnp.float32), 'Wg': jax.random.normal(ks[3], (D, E), jnp.float32) * s(D), 'bg': jnp.zeros((E,), jnp.float32), 'w1': jax.random.normal(ks[4], (E, D, H), jnp.float32) * s(D), 'b1': jnp.zeros((E, H), jnp.float32), 'w2': jax.random.normal(ks[5], (E, H, D), jnp.float32) * s(H), 'b2': jnp.zeros((E, D), jnp.float32), 'gamma': jnp.ones((D,), jnp.float32), 'beta': jnp.zeros((D,), jnp.float32), 'src': jax.random.randint(ks[6], (N_EDGES,), 0, N_NODES), 'dst': jax.random.randint(ks[7], (N_EDGES,), 0, N_NODES)}
        return inp
    _L0_gnn_all = _L0_gnn_setup()
    _L0_gnn_in = {k: v for k, v in _L0_gnn_all.items() if k in ('W_gc', 'b_gc', 'W_res', 'b_res', 'Wg', 'bg', 'w1', 'b1', 'w2', 'b2', 'gamma', 'beta')}
    del _L0_gnn_all

    def _L0_mix_setup():
        import jax, jax.numpy as jnp
        import numpy as np
        B, N, C = (8, 256, 256)
        HEADS, DH, KR = (8, 32, 4)
        INNER = HEADS * DH
        FF = 4 * C
        EPS = 1e-05

        def layernorm(x, g, b):
            mu = jnp.mean(x, axis=-1, keepdims=True)
            var = jnp.mean((x - mu) ** 2, axis=-1, keepdims=True)
            return (x - mu) * jax.lax.rsqrt(var + EPS) * g + b
        key = jax.random.key(seed)
        ks = jax.random.split(key, 16)
        s = 0.02
        return {'x': jax.random.normal(ks[0], (B, N, C), jnp.float32), 'ln1_g': jnp.ones((C,), jnp.float32), 'ln1_b': jnp.zeros((C,), jnp.float32), 'Wx': jax.random.normal(ks[1], (C, INNER), jnp.float32) * s, 'bx': jnp.zeros((INNER,), jnp.float32), 'Wq': jax.random.normal(ks[2], (DH, KR), jnp.float32) * s, 'Wk': jax.random.normal(ks[3], (DH, KR), jnp.float32) * s, 'Wv': jax.random.normal(ks[4], (DH, DH), jnp.float32) * s, 'Wo': jax.random.normal(ks[5], (INNER, C), jnp.float32) * s, 'bo': jnp.zeros((C,), jnp.float32), 'ln2_g': jnp.ones((C,), jnp.float32), 'ln2_b': jnp.zeros((C,), jnp.float32), 'W1': jax.random.normal(ks[6], (C, FF), jnp.float32) * s, 'b1': jnp.zeros((FF,), jnp.float32), 'W2': jax.random.normal(ks[7], (FF, C), jnp.float32) * s, 'b2': jnp.zeros((C,), jnp.float32)}
    _L0_mix_all = _L0_mix_setup()
    _L0_mix_in = {k: v for k, v in _L0_mix_all.items() if k in ('ln1_g', 'ln1_b', 'Wx', 'bx', 'Wq', 'Wk', 'Wv', 'Wo', 'bo', 'ln2_g', 'ln2_b', 'W1', 'b1', 'W2', 'b2')}
    del _L0_mix_all

    def _L0_ffn_setup():
        import jax, jax.numpy as jnp
        import numpy as np
        B, T, D, H, E = (16, 128, 256, 512, 8)
        key = jax.random.key(seed)
        ks = jax.random.split(key, 5)
        x = jax.random.normal(ks[0], (B, T, D), dtype=jnp.float32)
        gate_w = jax.random.normal(ks[1], (D, E), dtype=jnp.float32) * 0.02
        gate_b = jnp.zeros((E,), dtype=jnp.float32)
        W1 = jax.random.normal(ks[2], (E, D, H), dtype=jnp.float32) * 0.02
        b1 = jnp.zeros((E, H), dtype=jnp.float32)
        W2 = jax.random.normal(ks[3], (E, H, D), dtype=jnp.float32) * 0.02
        b2 = jnp.zeros((E, D), dtype=jnp.float32)
        return {'x': x, 'gate_w': gate_w, 'gate_b': gate_b, 'W1': W1, 'b1': b1, 'W2': W2, 'b2': b2}
    _L0_ffn_all = _L0_ffn_setup()
    _L0_ffn_in = {k: v for k, v in _L0_ffn_all.items() if k in ('gate_w', 'gate_b', 'W1', 'b1', 'W2', 'b2')}
    del _L0_ffn_all
    return {'x': x, 'src': src, 'dst': dst, 'L0_gnn_W_gc': _L0_gnn_in['W_gc'], 'L0_gnn_b_gc': _L0_gnn_in['b_gc'], 'L0_gnn_W_res': _L0_gnn_in['W_res'], 'L0_gnn_b_res': _L0_gnn_in['b_res'], 'L0_gnn_Wg': _L0_gnn_in['Wg'], 'L0_gnn_bg': _L0_gnn_in['bg'], 'L0_gnn_w1': _L0_gnn_in['w1'], 'L0_gnn_b1': _L0_gnn_in['b1'], 'L0_gnn_w2': _L0_gnn_in['w2'], 'L0_gnn_b2': _L0_gnn_in['b2'], 'L0_gnn_gamma': _L0_gnn_in['gamma'], 'L0_gnn_beta': _L0_gnn_in['beta'], 'L0_mix_ln1_g': _L0_mix_in['ln1_g'], 'L0_mix_ln1_b': _L0_mix_in['ln1_b'], 'L0_mix_Wx': _L0_mix_in['Wx'], 'L0_mix_bx': _L0_mix_in['bx'], 'L0_mix_Wq': _L0_mix_in['Wq'], 'L0_mix_Wk': _L0_mix_in['Wk'], 'L0_mix_Wv': _L0_mix_in['Wv'], 'L0_mix_Wo': _L0_mix_in['Wo'], 'L0_mix_bo': _L0_mix_in['bo'], 'L0_mix_ln2_g': _L0_mix_in['ln2_g'], 'L0_mix_ln2_b': _L0_mix_in['ln2_b'], 'L0_mix_W1': _L0_mix_in['W1'], 'L0_mix_b1': _L0_mix_in['b1'], 'L0_mix_W2': _L0_mix_in['W2'], 'L0_mix_b2': _L0_mix_in['b2'], 'L0_ffn_gate_w': _L0_ffn_in['gate_w'], 'L0_ffn_gate_b': _L0_ffn_in['gate_b'], 'L0_ffn_W1': _L0_ffn_in['W1'], 'L0_ffn_b1': _L0_ffn_in['b1'], 'L0_ffn_W2': _L0_ffn_in['W2'], 'L0_ffn_b2': _L0_ffn_in['b2']}

def reference(x, src, dst, L0_gnn_W_gc, L0_gnn_b_gc, L0_gnn_W_res, L0_gnn_b_res, L0_gnn_Wg, L0_gnn_bg, L0_gnn_w1, L0_gnn_b1, L0_gnn_w2, L0_gnn_b2, L0_gnn_gamma, L0_gnn_beta, L0_mix_ln1_g, L0_mix_ln1_b, L0_mix_Wx, L0_mix_bx, L0_mix_Wq, L0_mix_Wk, L0_mix_Wv, L0_mix_Wo, L0_mix_bo, L0_mix_ln2_g, L0_mix_ln2_b, L0_mix_W1, L0_mix_b1, L0_mix_W2, L0_mix_b2, L0_ffn_gate_w, L0_ffn_gate_b, L0_ffn_W1, L0_ffn_b1, L0_ffn_W2, L0_ffn_b2):
    import jax
    import jax.numpy as jnp

    def _L0_gnn_ref(feats, W_gc, b_gc, W_res, b_res, Wg, bg, w1, b1, w2, b2, gamma, beta, src, dst):
        import jax, jax.numpy as jnp
        import numpy as np
        N_NODES = 512
        N_EDGES = 8192
        D_IN = 256
        D = 256
        H = 512
        E = 64
        TOP_K = 2
        CAP = 1024
        BN_EPS = 1e-05

        def _moe_ff(x, Wg, bg, w1, b1, w2, b2):
            N = x.shape[0]
            logits = x @ Wg + bg
            vals, idx = jax.lax.top_k(logits, TOP_K)
            gates = jax.nn.softmax(vals, axis=-1)
            e_flat = idx.reshape(-1)
            g_flat = gates.reshape(-1)
            tok = jnp.arange(N * TOP_K) // TOP_K
            order = jnp.argsort(e_flat)
            e_s, tok_s, g_s = (e_flat[order], tok[order], g_flat[order])
            counts = jnp.bincount(e_flat, length=E)
            offs = jnp.concatenate([jnp.zeros((1,), counts.dtype), jnp.cumsum(counts)[:-1]])
            rank = jnp.arange(N * TOP_K) - offs[e_s]
            valid = rank < CAP
            slot = jnp.where(valid, e_s * CAP + rank, E * CAP)
            buf = jnp.zeros((E * CAP + 1, D), x.dtype).at[slot].set(x[tok_s])
            h = buf[:E * CAP].reshape(E, CAP, D)
            h1 = jax.nn.gelu(jnp.einsum('ecd,edh->ech', h, w1) + b1[:, None, :], approximate=False)
            h2 = jnp.einsum('ech,ehd->ecd', h1, w2) + b2[:, None, :]
            out_buf = h2.reshape(E * CAP, D)
            y_s = jnp.where(valid[:, None], out_buf[jnp.minimum(slot, E * CAP - 1)], 0.0)
            return jnp.zeros((N, D), x.dtype).at[tok_s].add(g_s[:, None] * y_s)

        def _forward(feats, W_gc, b_gc, W_res, b_res, Wg, bg, w1, b1, w2, b2, gamma, beta, src, dst):
            n = feats.shape[0]
            ones = jnp.ones((src.shape[0],), feats.dtype)
            deg_out = jnp.clip(jax.ops.segment_sum(ones, src, num_segments=n), 1.0)
            deg_in = jnp.clip(jax.ops.segment_sum(ones, dst, num_segments=n), 1.0)
            h = feats * jax.lax.rsqrt(deg_out)[:, None]
            m = jax.ops.segment_sum(h[src], dst, num_segments=n) * jax.lax.rsqrt(deg_in)[:, None]
            gc = m @ W_gc + b_gc
            x = gc + (feats @ W_res + b_res)
            core = _moe_ff(x, Wg, bg, w1, b1, w2, b2)
            y = x + core
            mean = jnp.mean(y, axis=0)
            var = jnp.mean((y - mean) ** 2, axis=0)
            return (y - mean) * jax.lax.rsqrt(var + BN_EPS) * gamma + beta
        return _forward(feats, W_gc, b_gc, W_res, b_res, Wg, bg, w1, b1, w2, b2, gamma, beta, src, dst)

    def _L0_mix_ref(x, ln1_g, ln1_b, Wx, bx, Wq, Wk, Wv, Wo, bo, ln2_g, ln2_b, W1, b1, W2, b2):
        import jax, jax.numpy as jnp
        import numpy as np
        B, N, C = (8, 256, 256)
        HEADS, DH, KR = (8, 32, 4)
        INNER = HEADS * DH
        FF = 4 * C
        EPS = 1e-05

        def layernorm(x, g, b):
            mu = jnp.mean(x, axis=-1, keepdims=True)
            var = jnp.mean((x - mu) ** 2, axis=-1, keepdims=True)
            return (x - mu) * jax.lax.rsqrt(var + EPS) * g + b
        b, n, c = x.shape
        h = layernorm(x, ln1_g, ln1_b)
        xm = h @ Wx + bx
        xm = xm.reshape(b, n, HEADS, DH).transpose(0, 2, 1, 3)
        q = jax.nn.softmax(xm @ Wq, axis=-1)
        k = jax.nn.softmax(xm @ Wk, axis=-2)
        v = xm @ Wv
        kv = jnp.einsum('bhnr,bhnd->bhrd', k, v)
        qkv = jnp.einsum('bhnr,bhrd->bhnd', q, kv)
        attn = qkv.transpose(0, 2, 1, 3).reshape(b, n, INNER) @ Wo + bo
        fx = attn + x
        h2 = layernorm(fx, ln2_g, ln2_b)
        m = jax.nn.gelu(h2 @ W1 + b1, approximate=False) @ W2 + b2
        return m + fx

    def _L0_ffn_ref(x, gate_w, gate_b, W1, b1, W2, b2):
        import jax, jax.numpy as jnp
        import numpy as np
        B, T, D, H, E = (16, 128, 256, 512, 8)
        Bb, Tt, Dd = x.shape
        Ee = gate_w.shape[1]
        xf = x.reshape(-1, Dd)
        N = xf.shape[0]
        logits = xf @ gate_w + gate_b
        probs = jax.nn.softmax(logits, axis=-1)
        top2_vals, top2_idx = jax.lax.top_k(probs, 2)
        cw = jnp.zeros((N, Ee), dtype=xf.dtype).at[jnp.arange(N)[:, None], top2_idx].add(top2_vals)

        def step(acc, params):
            w1, bb1, w2, bb2, we = params
            h = jax.nn.gelu(xf @ w1 + bb1, approximate=False)
            y = h @ w2 + bb2
            return (acc + we[:, None] * y, None)
        out, _ = jax.lax.scan(step, jnp.zeros_like(xf), (W1, b1, W2, b2, cw.T))
        return out.reshape(Bb, Tt, Dd)
    xn = _layernorm(x, axis=-1)
    x = x + _L0_gnn_ref(xn, L0_gnn_W_gc, L0_gnn_b_gc, L0_gnn_W_res, L0_gnn_b_res, L0_gnn_Wg, L0_gnn_bg, L0_gnn_w1, L0_gnn_b1, L0_gnn_w2, L0_gnn_b2, L0_gnn_gamma, L0_gnn_beta, src, dst) + _L0_mix_ref(xn[None], L0_mix_ln1_g, L0_mix_ln1_b, L0_mix_Wx, L0_mix_bx, L0_mix_Wq, L0_mix_Wk, L0_mix_Wv, L0_mix_Wo, L0_mix_bo, L0_mix_ln2_g, L0_mix_ln2_b, L0_mix_W1, L0_mix_b1, L0_mix_W2, L0_mix_b2)[0]
    x = x + _L0_ffn_ref(_layernorm(x, axis=-1)[None], L0_ffn_gate_w, L0_ffn_gate_b, L0_ffn_W1, L0_ffn_b1, L0_ffn_W2, L0_ffn_b2)[0]
    return x

_drawn_inputs = setup_inputs


def setup_inputs(seed=0):
    import zlib

    import numpy as np

    out = dict(_drawn_inputs(seed))
    spreads = {'L0_gnn_b_gc': (0.0, 0.273),
     'L0_gnn_b_res': (0.0, 0.1),
     'L0_gnn_bg': (0.0, 0.27),
     'L0_gnn_b1': (0.0, 0.413),
     'L0_gnn_b2': (0.0, 0.284),
     'L0_gnn_gamma': (1.0, 0.2),
     'L0_gnn_beta': (0.0, 0.387),
     'L0_mix_ln1_g': (1.0, 0.6),
     'L0_mix_ln1_b': (0.0, 0.8),
     'L0_mix_bx': (0.0, 0.8),
     'L0_mix_bo': (0.0, 0.346),
     'L0_mix_ln2_g': (1.0, 0.6),
     'L0_mix_ln2_b': (0.0, 2.0),
     'L0_mix_b1': (0.0, 0.479),
     'L0_mix_b2': (0.0, 0.457),
     'L0_ffn_gate_b': (0.0, 0.8),
     'L0_ffn_b1': (0.0, 0.8),
     'L0_ffn_b2': (0.0, 0.701)}
    factors = {'L0_mix_Wx': 8.0,
     'L0_mix_Wq': 8.0,
     'L0_mix_Wk': 8.0,
     'L0_mix_Wv': 8.0,
     'L0_mix_Wo': 8.0,
     'L0_ffn_gate_w': 4.461,
     'L0_ffn_W1': 6.426,
     'L0_ffn_W2': 6.034}
    for name, (base, spread) in spreads.items():
        noise = np.random.default_rng([zlib.crc32(name.encode()), seed]).standard_normal(out[name].shape)
        drawn = base * np.exp(spread * noise) if base else spread * noise
        out[name] = jnp.asarray(drawn.astype(out[name].dtype))
    for name, factor in factors.items():
        out[name] = (out[name] * factor).astype(out[name].dtype)
    return out
```

```python
from contextlib import ExitStack, contextmanager

import concourse.bass as bass
from concourse import mybir

F32, I32, U32, BF16 = mybir.dt.float32, mybir.dt.int32, mybir.dt.uint32, mybir.dt.bfloat16
ALU = mybir.AluOpType
ACT = mybir.ActivationFunctionType
AX = mybir.AxisListType.X
ds = bass.ds

N, D = 3125, 256
NE = 50000
T = 125
NT = N // T
U = 5
NG = NT // U
EC = NE // T
EQ = 100
EJ = EC // EQ
VU = 4
EPAD = VU
HG = 20
DC = D // 128
EPS = 1e-5
MAGIC = float(3 << 22)
HEADS, DH, KR = 8, 32, 4
HR = HEADS * KR
FF = 1024
FC = FF // 128
H = 512
HC = H // 128
B = 128
MU = 4
E_GNN, E_FFN = 64, 8
CAP = 1024
SPLIT = 112


class Bag:
    pass


def most_blocks(experts):
    blocks = (2 * N + experts * (B - 1)) // B
    return -(-blocks // MU) * MU


@contextmanager
def phase(nc, name, semaphores):
    sems = {s: nc.alloc_semaphore(f"{name}_{s}") for s in semaphores.split()}
    with ExitStack() as scope:
        tools = Bag()
        tools.sb = lambda n, shape, dt=F32: scope.enter_context(nc.sbuf_tensor(f"{name}_{n}", shape, dt))
        tools.psum = scope.enter_context(nc.psum_tensor(f"{name}_psum", [128, 8 * 512], F32))[:]
        tools.s = sems
        tools.banks = [tools.psum[:, 512 * n:512 * (n + 1)] for n in range(8)]
        tools.wide = [tools.psum[:, 512 * n:512 * (n + 2)] for n in (3, 5)]
        yield tools
    nc.clear_and_free_semaphores(list(sems.values()))
    nc.all_engine_barrier(sem_only=True)


def rows_of(dram, group):
    return dram.rearrange("(g u p) d -> g p u d", p=T, u=U)[group]


def round_to_whole(nc, out, in_, scale, shift):
    return (lambda: nc.vector.tensor_scalar(out, in_, scale, shift, ALU.mult, ALU.add),
            lambda: nc.vector.tensor_scalar(out, out, MAGIC, MAGIC, ALU.add, ALU.subtract))


def resident(nc, scope):
    sb = lambda n, shape, dt=F32: scope.enter_context(nc.sbuf_tensor(n, shape, dt))
    r = Bag()
    r.acc = sb("acc", [T, NT, D])
    r.nodes = sb("nodes", [T, NT, D])
    r.ident = sb("ident", [128, 128])
    r.ones = sb("ones", [T, T])
    r.zeros = sb("zeros", [128, D + 2], BF16)
    r.tril_f = sb("tril_f", [64, 64])
    r.tril = sb("tril", [T, T], BF16)
    r.ones_b = sb("ones_b", [T, T], BF16)
    r.row = sb("row", [128, 512])
    r.col = sb("col", [128, 1])
    r.eps = sb("eps", [128, 1])
    return r


def constants(nc, r):
    with phase(nc, "constants", "filled shaped") as k:
        s = k.s
        with nc.Block() as block:
            @block.gpsimd
            def _(pool):
                nc.gpsimd.memset(r.ident[:], 0.0)
                nc.gpsimd.memset(r.ones[:], 1.0)
                nc.gpsimd.memset(r.ones_b[:], 1.0)
                nc.gpsimd.memset(r.tril[:], 1.0)
                nc.gpsimd.memset(r.tril_f[:], 1.0)
                nc.gpsimd.memset(r.zeros[:], 0.0)
                nc.gpsimd.memset(r.eps[:], EPS)
                nc.gpsimd.iota(r.row[:], pattern=[[1, 512]], base=0, channel_multiplier=0,
                               allow_small_or_imprecise_dtypes=True)
                nc.gpsimd.iota(r.col[:], pattern=[[0, 1]], base=0, channel_multiplier=1,
                               allow_small_or_imprecise_dtypes=True).then_inc(s["filled"], 1)
                pool.wait_ge(s["filled"], 1)
                nc.gpsimd.affine_select(out=r.ident[:], in_=r.ident[:], compare_op=ALU.not_equal, fill=1.0,
                                        base=0, pattern=[[-1, 128]], channel_multiplier=1).then_inc(s["shaped"], 1)
                nc.gpsimd.affine_select(out=r.tril[:], in_=r.tril[:], compare_op=ALU.is_gt, fill=0.0,
                                        base=0, pattern=[[1, T]], channel_multiplier=-1).then_inc(s["shaped"], 1)
                nc.gpsimd.affine_select(out=r.tril_f[:], in_=r.tril_f[:], compare_op=ALU.is_gt, fill=0.0,
                                        base=0, pattern=[[1, 64]], channel_multiplier=-1).then_inc(s["shaped"], 1)
                pool.wait_ge(s["shaped"], 3)


def prepare(nc, d, r, a):
    names = ("edges_in x_in mix_in rest_in edges_float edge_columns ids ids_step hist_ready hist_free degree degree_root"
             " chunk_range range_bc visit_step visit_row tables blockdiag wx_turned wx_copied folded qk_weights"
             " stats1 moments1 root1 inverse1 xn_ready xn_free h_ready h_stored stats2 moments2 root2 inverse2"
             " hn_ready hn_free xnT_turned hnT_turned hT_ready hT_free qk_ready qk_kept xnT_kept passed")
    with phase(nc, "prepare", names) as k:
        s, sb = k.s, k.sb
        src_n, dst_n = sb("src_n", [EQ, EJ, T], I32), sb("dst_n", [EQ, EJ, T], I32)
        src_f, dst_f = sb("src_f", [EQ, EJ, T]), sb("dst_f", [EQ, EJ, T])
        src_t, src_hi = sb("src_t", [T, EC]), sb("src_hi", [T, EC])
        hi_b, lo_b = sb("hi_b", [T, EC], BF16), sb("lo_b", [T, EC], BF16)
        count_lo, count_hi = sb("count_lo", [T, T, HG], BF16), sb("count_hi", [T, NT, HG], BF16)
        hot_lo = [sb(f"hot_lo{v}", [T, T, HG], BF16) for v in range(2)]
        hot_hi = [sb(f"hot_hi{v}", [T, NT, HG], BF16) for v in range(2)]
        degree = sb("degree", [T, NT])
        reach = sb("reach", [EQ, 2, EJ])
        lo_c, hi_c = sb("lo_c", [NT, EC]), sb("hi_c", [NT, EC])
        visit = sb("visit", [NT, 8])
        blockdiag_qk = sb("blockdiag_qk", [128, DC, 2 * HR])
        bias_rows = sb("bias_rows", [22, 128])
        wx_t = sb("wx_t", [128, DC, D])
        wqk = sb("wqk", [128, DC, 2 * HR])
        bqk = sb("bqk", [T, 2 * HR])
        stats, moments = sb("stats", [T, U, 6]), sb("moments", [T, U, 2])
        root = sb("root", [T, U])
        xn = sb("xn", [T, U, D])
        hn = sb("hn", [T, U, D])
        h_out = sb("h_out", [T, U, D])
        hT = sb("hT", [128, U, DC, T])
        turn_x = [k.banks[u // 2][:, (u % 2) * 256:(u % 2) * 256 + DC * T] for u in range(U)]
        turn_h = [k.banks[3 + u // 2][:, (u % 2) * 256:(u % 2) * 256 + DC * T] for u in range(U)]
        qk_ps = k.banks[6]
        hist = k.banks[7][0:T, 0:NT]

        with nc.Block() as block:
            @block.sync
            def _(sp):
                def load(to, what, sem):
                    sp.dma_start(to, what).then_inc(sem, 16)
                for dst, edges in ((src_n, d["src"]), (dst_n, d["dst"])):
                    load(dst[:], edges.rearrange("(j q e) -> q j e", q=EQ, e=T), s["edges_in"])
                for p0, p1 in ((0, SPLIT), (SPLIT, T)):
                    load(r.acc[p0:p1], d["x"].rearrange("(i p) d -> p i d", p=T)[p0:p1], s["x_in"])
                load(a.wx[:], d["mix_Wx"].rearrange("(c p) n -> p c n", p=128), s["mix_in"])
                for at, what in ((0, d["mix_bx"]), (2, d["mix_ln1_g"]), (4, d["mix_ln1_b"]), (6, d["mix_ln2_g"]), (8, d["mix_ln2_b"]),
                                 (10, d["mix_b1"]), (18, d["gnn_b_gc"]), (20, d["gnn_b_res"])):
                    pieces = what.rearrange("(c p) -> c p", p=128)
                    load(bias_rows[at:at + pieces.shape[0], :], pieces, s["mix_in"])
                sp.wait_ge(s["blockdiag"], 1)
                for c in range(DC):
                    for q in range(128 // DH):
                        at, head = slice(DH * q, DH * (q + 1)), 4 * c + q
                        load(blockdiag_qk[at, c, KR * head:KR * (head + 1)], d["mix_Wq"], s["mix_in"])
                        load(blockdiag_qk[at, c, HR + KR * head:HR + KR * (head + 1)], d["mix_Wk"], s["mix_in"])
                for q in range(128 // DH):
                    load(a.wv[DH * q:DH * (q + 1), DH * q:DH * (q + 1)], d["mix_Wv"], s["rest_in"])
                for p0, p1 in ((0, SPLIT), (SPLIT, T)):
                    load(a.b2_bc[p0:p1], d["mix_b2"].partition_broadcast(p1 - p0), s["rest_in"])
                    load(a.beta_bc[p0:p1], d["gnn_beta"].partition_broadcast(p1 - p0), s["rest_in"])
                    load(a.bg_bc[p0:p1], d["gnn_bg"].partition_broadcast(p1 - p0), s["rest_in"])
                load(a.g1_bc[:], d["mix_ln1_g"].partition_broadcast(HR), s["rest_in"])
                load(a.b1_bc[:], d["mix_ln1_b"].partition_broadcast(HR), s["rest_in"])
                load(a.bx_row[:], d["mix_bx"].rearrange("(o n) -> o n", o=1), s["rest_in"])
                load(a.m_aug[HR:HR + 1, :], d["mix_bo"].rearrange("(o n) -> o n", o=1), s["rest_in"])
                for to, what in ((a.wo, d["mix_Wo"]), (a.w_gc, d["gnn_W_gc"]), (a.w_res, d["gnn_W_res"]), (a.wg, d["gnn_Wg"])):
                    load(to[:], what.rearrange("(c p) n -> p c n", p=128), s["rest_in"])
                rest = 4 + 6 + 4 + 4
                sp.sem_inc(s["h_stored"], 32)
                with sp.Fori(0, NG) as g:
                    sp.wait_ge(s["h_ready"], U * g + U)
                    for p0, p1 in ((0, SPLIT), (SPLIT, T)):
                        sp.dma_start(rows_of(a.h_dram, g)[p0:p1], h_out[p0:p1]).then_inc(s["h_stored"], 16)
                sp.wait_ge(s["h_stored"], 32 * NG + 32)
                sp.wait_ge(s["mix_in"], 16 * (1 + 8 + 4 * 2 * DC))
                sp.wait_ge(s["rest_in"], 16 * rest)
                sp.wait_ge(s["x_in"], 32)
                sp.wait_ge(s["edges_in"], 32)

            @block.gpsimd
            def _(pool):
                nc.gpsimd.memset(blockdiag_qk[:], 0.0)
                nc.gpsimd.memset(a.wv[:], 0.0).then_inc(s["blockdiag"], 1)
                nc.gpsimd.iota(count_lo[:], pattern=[[1, T], [0, HG]], base=0, channel_multiplier=0,
                               allow_small_or_imprecise_dtypes=True)
                nc.gpsimd.iota(count_hi[:], pattern=[[1, NT], [0, HG]], base=0, channel_multiplier=0,
                               allow_small_or_imprecise_dtypes=True).then_inc(s["tables"], 1)
                pool.sem_inc(s["xn_free"], U)
                pool.sem_inc(s["hn_free"], U)
                with pool.Fori(0, NG) as g:
                    for u in range(U):
                        pool.wait_ge(s["xn_ready"], U * g + u + 1)
                        nc.gpsimd.tensor_copy(a.xn[:, ds(U * g + u, 1), :], xn[:, u:u + 1, :]).then_inc(s["xn_free"], 1)
                    for u in range(U):
                        pool.wait_ge(s["hn_ready"], U * g + u + 1)
                        nc.gpsimd.tensor_copy(r.nodes[:, ds(U * g + u, 1), :], hn[:, u:u + 1, :]).then_inc(s["hn_free"], 1)

            @block.vector
            def _(dve):
                steps = [0]

                def then(ins):
                    steps[0] += 1
                    ins.then_inc(s["ids_step"], 1)
                    dve.wait_ge(s["ids_step"], steps[0])

                nc.vector.memset(a.src_idx[:], 0)
                nc.vector.memset(a.visit_tab[:], 0)
                then(nc.vector.memset(a.dst_t[:], -1.0))
                dve.wait_ge(s["edges_in"], 32)
                nc.vector.tensor_copy(src_f[:], src_n[:]).then_inc(s["edges_float"], 1)
                nc.vector.tensor_copy(dst_f[:], dst_n[:]).then_inc(s["edges_float"], 1)
                dve.wait_ge(s["edge_columns"], 2)
                nc.vector.tensor_copy(a.src_idx[:, 0:EC], k.banks[0][0:T, 0:EC])
                nc.vector.tensor_copy(src_t[:], k.banks[0][0:T, 0:EC])
                then(nc.vector.tensor_copy(a.dst_t[:, 0:EC], k.banks[1][0:T, 0:EC]))
                for ins in round_to_whole(nc, src_hi[:], src_t[:], 1.0 / T, -(T // 2) / T):
                    then(ins())
                nc.vector.tensor_copy(hi_b[:], src_hi[:])
                nc.vector.scalar_tensor_tensor(lo_b[:], src_hi[:], -float(T), src_t[:], ALU.mult, ALU.add).then_inc(s["ids"], 1)
                dve.wait_ge(s["ids"], 1)
                dve.wait_ge(s["tables"], 1)
                with dve.Fori(0, EC // HG // 2) as i:
                    for v in range(2):
                        at = ds((2 * i + v) * HG, HG)
                        dve.wait_ge(s["hist_free"], 2 * i + v + 1)
                        nc.vector.tensor_tensor(hot_lo[v][:], count_lo[:], lo_b[:, at].unsqueeze(1).broadcast_to([T, T, HG]), ALU.is_equal)
                        nc.vector.tensor_tensor(hot_hi[v][:], count_hi[:], hi_b[:, at].unsqueeze(1).broadcast_to([T, NT, HG]),
                                                ALU.is_equal).then_inc(s["hist_ready"], 1)
                dve.wait_ge(s["hist_free"], EC // HG + 2 + 1)
                nc.vector.tensor_scalar(degree[:], hist, 1.0, None, ALU.max).then_inc(s["degree"], 1)
                dve.wait_ge(s["degree_root"], 1)
                then(nc.vector.reciprocal(a.rs_out[:], degree[:]))
                nc.vector.tensor_reduce(reach[:, 0, :], dst_f[:], AX, ALU.min)
                then(nc.vector.tensor_reduce(reach[:, 1, :], dst_f[:], AX, ALU.max))
                for ins in round_to_whole(nc, reach[:], reach[:], 1.0 / T, -(T // 2) / T):
                    then(ins())
                nc.vector.tensor_copy(visit[:, 7:8], r.col[0:NT, :]).then_inc(s["chunk_range"], 1)
                dve.wait_ge(s["range_bc"], 1)
                block_no = r.col[0:NT, :]
                nc.vector.tensor_scalar(lo_c[:], k.banks[2][0:NT, 0:EC], block_no, None, ALU.is_le)
                then(nc.vector.tensor_scalar(hi_c[:], k.banks[3][0:NT, 0:EC], block_no, None, ALU.is_ge))
                then(nc.vector.tensor_tensor(lo_c[:], lo_c[:], hi_c[:], ALU.mult))
                then(nc.vector.scalar_tensor_tensor(hi_c[:], r.row[0:NT, 0:EC], -float(EC), lo_c[:], ALU.add, ALU.mult))
                then(nc.vector.tensor_reduce(visit[:, 0:1], hi_c[:], AX, ALU.min))
                then(nc.vector.tensor_scalar(visit[:, 0:1], visit[:, 0:1], float(EC), float(EC - 1), ALU.add, ALU.min))
                then(nc.vector.scalar_tensor_tensor(hi_c[:], r.row[0:NT, 0:EC], 1.0, lo_c[:], ALU.add, ALU.mult))
                then(nc.vector.tensor_reduce(visit[:, 1:2], hi_c[:], AX, ALU.max))
                then(nc.vector.tensor_tensor(visit[:, 1:2], visit[:, 1:2], visit[:, 0:1], ALU.subtract))
                then(nc.vector.tensor_scalar(visit[:, 1:2], visit[:, 1:2], 1.0, None, ALU.max))
                for ins in round_to_whole(nc, visit[:, 2:3], visit[:, 1:2], 1.0 / VU, (VU - 1) / (2.0 * VU)):
                    then(ins())
                nc.vector.tensor_copy(visit[:, 3:4], visit[:, 2:3]).then_inc(s["visit_step"], 1)
                dve.wait_ge(s["visit_row"], 1)
                nc.vector.tensor_copy(visit[:, 4:5], k.banks[4][0:NT, 0:1]).then_inc(s["visit_step"], 1)
                dve.wait_ge(s["visit_row"], 2)
                nc.vector.tensor_copy(a.visit_tab[0:1, 0, 0:NT], k.banks[5][0:1, 0:NT])
                nc.vector.tensor_copy(a.visit_tab[0:1, 1, 0:NT], k.banks[5][0:1, NT:2 * NT])
                nc.vector.tensor_copy(a.visit_tab[0:1, 2, 0:NT], k.banks[5][0:1, 2 * NT:3 * NT])
                dve.wait_ge(s["wx_turned"], 1)
                nc.vector.tensor_copy(a.cols[:], k.banks[0][:, 0:22])
                nc.vector.tensor_copy(wx_t[:], k.banks[6][:, 0:DC * D].rearrange("p (c n) -> p c n", c=DC)).then_inc(s["wx_copied"], 1)
                dve.wait_ge(s["folded"], 1)
                nc.vector.tensor_copy(wqk[:], k.banks[1][:, 0:DC * 2 * HR].rearrange("p (c n) -> p c n", c=DC))
                nc.vector.tensor_copy(bqk[:], k.banks[1][0:T, 256:256 + 2 * HR]).then_inc(s["qk_weights"], 1)
                dve.wait_ge(s["qk_weights"], 1)
                dve.wait_ge(s["x_in"], 32)

                with dve.Fori(0, NG) as g:
                    def norm(tile, stats_sem, moments_sem, root_sem, inverse_sem):
                        for u in range(U):
                            nc.vector.bn_stats(stats[:, u, :], tile(u)).then_inc(stats_sem, 1)
                        dve.wait_ge(stats_sem, U * g + U)
                        dve.sem_inc(s["passed"], 1)
                        for u in range(U):
                            nc.vector.bn_aggr(moments[:, u, :], stats[:, u, :]).then_inc(moments_sem, 1)
                        dve.wait_ge(root_sem, g + 1)
                        nc.vector.reciprocal(root[:], root[:]).then_inc(inverse_sem, 1)
                        dve.wait_ge(inverse_sem, g + 1)

                    norm(lambda u: r.acc[:, ds(U * g + u, 1), :].rearrange("p o d -> p (o d)"), s["stats1"], s["moments1"], s["root1"], s["inverse1"])
                    for u in range(U):
                        dve.wait_ge(s["xn_free"], U * g + u + 1)
                        nc.vector.tensor_scalar(xn[:, u:u + 1, :], r.acc[:, ds(U * g + u, 1), :], moments[:, u, 0:1], root[:, u:u + 1],
                                                ALU.subtract, ALU.mult).then_inc(s["xn_ready"], 1)
                    dve.wait_ge(s["xn_ready"], U * g + U)
                    norm(lambda u: xn[:, u, :], s["stats2"], s["moments2"], s["root2"], s["inverse2"])
                    for u in range(U):
                        dve.wait_ge(s["hn_free"], U * g + u + 1)
                        nc.vector.tensor_scalar(hn[:, u, :], xn[:, u, :], moments[:, u, 0:1], root[:, u:u + 1],
                                                ALU.subtract, ALU.mult).then_inc(s["hn_ready"], 1)
                    dve.wait_ge(s["xnT_turned"], U * g + U)
                    for u in range(U):
                        nc.vector.tensor_copy(a.xnT[:, :, ds((U * g + u) * T, T)],
                                              turn_x[u].rearrange("p (c t) -> p c t", c=DC)).then_inc(s["xnT_kept"], 1)
                    dve.wait_ge(s["qk_ready"], U * g + U)
                    nc.vector.tensor_tensor(a.qk[:, ds(U * g, U), :], qk_ps[0:T, 0:U * 2 * HR].rearrange("p (u n) -> p u n", u=U),
                                            bqk[:].unsqueeze(1).broadcast_to([T, U, 2 * HR]), ALU.add).then_inc(s["qk_kept"], 1)

            @block.scalar
            def _(act):
                act.wait_ge(s["degree"], 1)
                nc.scalar.activation(degree[:], degree[:], ACT.Sqrt).then_inc(s["degree_root"], 1)
                act.sem_inc(s["hT_free"], 1)
                with act.Fori(0, NG) as g:
                    act.wait_ge(s["moments1"], U * g + U)
                    nc.scalar.activation(root[:], moments[:, :, 1], ACT.Sqrt, bias=r.eps[0:T, :]).then_inc(s["root1"], 1)
                    act.wait_ge(s["h_stored"], 32 * g + 32)
                    for u in range(U):
                        act.wait_ge(s["xn_ready"], U * g + u + 1)
                        nc.scalar.activation(h_out[:, u, :], xn[:, u, :], ACT.Copy,
                                             scale=a.rs_out[:, ds(U * g + u, 1)]).then_inc(s["h_ready"], 1)
                    act.wait_ge(s["moments2"], U * g + U)
                    nc.scalar.activation(root[:], moments[:, :, 1], ACT.Sqrt, bias=r.eps[0:T, :]).then_inc(s["root2"], 1)
                    act.wait_ge(s["hnT_turned"], U * g + U)
                    for u in range(U):
                        for c in range(DC):
                            done = nc.scalar.activation(hT[:, u, c, :], turn_h[u][:, c * T:(c + 1) * T], ACT.Identity,
                                                        scale=a.cols[:, 2 + c:3 + c], bias=a.cols[:, 4 + c:5 + c])
                        done.then_inc(s["hT_ready"], 1)

            @block.tensor
            def _(pe):
                for n, (edges, bank) in enumerate(((src_f, k.banks[0]), (dst_f, k.banks[1]))):
                    pe.wait_ge(s["edges_float"], n + 1)
                    for j in range(EJ):
                        done = nc.tensor.transpose(bank[0:T, j * EQ:(j + 1) * EQ], edges[:, j, :], r.ident[0:EQ, 0:EQ])
                    done.then_inc(s["edge_columns"], 1)
                pe.sem_inc(s["hist_free"], 2)
                nc.tensor.matmul(hist, r.zeros[0:T, 0:T], r.zeros[0:T, 0:NT], start=True, stop=False)
                with pe.Fori(0, EC // HG // 2) as i:
                    for v in range(2):
                        pe.wait_ge(s["hist_ready"], 2 * i + v + 1)
                        for j in range(HG):
                            done = nc.tensor.matmul(hist, hot_lo[v][:, :, j], hot_hi[v][:, :, j], start=False, stop=False)
                        done.then_inc(s["hist_free"], 1)
                nc.tensor.matmul(hist, r.zeros[0:T, 0:T], r.zeros[0:T, 0:NT], start=False, stop=True).then_inc(s["hist_free"], 1)
                pe.wait_ge(s["chunk_range"], 1)
                for way in range(2):
                    for j in range(EJ):
                        done = nc.tensor.matmul(k.banks[2 + way][0:NT, j * EQ:(j + 1) * EQ],
                                                reach[:, way, j:j + 1].broadcast_to([EQ, NT]), r.ident[0:EQ, 0:EQ], start=True, stop=True)
                done.then_inc(s["range_bc"], 1)
                pe.wait_ge(s["visit_step"], 1)
                nc.tensor.matmul(k.banks[4][0:NT, 0:1], r.tril_f[0:NT, 0:NT], visit[:, 2:3], start=True, stop=True).then_inc(s["visit_row"], 1)
                pe.wait_ge(s["visit_step"], 2)
                for n, what in enumerate((visit[:, 4:5], visit[:, 0:1], visit[:, 2:3])):
                    done = nc.tensor.matmul(k.banks[5][0:1, n * NT:(n + 1) * NT], what, r.ident[0:NT, 0:NT], start=True, stop=True)
                done.then_inc(s["visit_row"], 1)
                pe.wait_ge(s["mix_in"], 16 * (1 + 8 + 4 * 2 * DC))
                nc.tensor.transpose(k.banks[0][:, 0:22], bias_rows[:], r.ident[0:22, 0:22])
                for n in range(DC):
                    for c in range(DC):
                        done = nc.tensor.transpose(k.banks[6][:, n * D + c * 128:n * D + (c + 1) * 128], a.wx[:, c, n * 128:(n + 1) * 128], r.ident[:])
                done.then_inc(s["wx_turned"], 1)
                pe.wait_ge(s["wx_copied"], 1)
                for c in range(DC):
                    for n in range(DC):
                        nc.tensor.matmul(k.banks[1][:, c * 64:(c + 1) * 64], wx_t[:, n, c * 128:(c + 1) * 128], blockdiag_qk[:, n, :],
                                         start=n == 0, stop=n == DC - 1)
                for n in range(DC):
                    done = nc.tensor.matmul(k.banks[1][0:T, 256:256 + 2 * HR], a.cols[:, n:n + 1].broadcast_to([128, T]), blockdiag_qk[:, n, :],
                                            start=n == 0, stop=n == DC - 1)
                done.then_inc(s["folded"], 1)
                pe.wait_ge(s["qk_weights"], 1)
                with pe.Fori(0, NG) as g:
                    for u in range(U):
                        pe.wait_ge(s["xn_ready"], U * g + u + 1)
                        for c in range(DC):
                            done = nc.tensor.transpose(turn_x[u][:, c * T:(c + 1) * T], xn[:, u, c * 128:(c + 1) * 128], r.ident[0:T, 0:T])
                        done.then_inc(s["xnT_turned"], 1)
                    for u in range(U):
                        pe.wait_ge(s["hn_ready"], U * g + u + 1)
                        for c in range(DC):
                            done = nc.tensor.transpose(turn_h[u][:, c * T:(c + 1) * T], hn[:, u, c * 128:(c + 1) * 128], r.ident[0:T, 0:T])
                        done.then_inc(s["hnT_turned"], 1)
                    for u in range(U):
                        pe.wait_ge(s["hT_ready"], U * g + u + 1)
                        for c in range(DC):
                            done = nc.tensor.matmul(qk_ps[0:T, 64 * u:64 * u + 64], hT[:, u, c, :], wqk[:, c, :], start=c == 0, stop=c == DC - 1)
                        done.then_inc(s["qk_ready"], 1)


def attention_state(nc, d, r, a):
    names = ("step act_step pe_step staged staged_free summed bias_added weights_in")
    with phase(nc, "state", names) as k:
        s, sb = k.s, k.sb
        q_max, q_sum = sb("q_max", [T, NT, HEADS]), sb("q_sum", [T, NT, HEADS])
        k_max, k_sum = sb("k_max", [T, HR]), sb("k_sum", [T, HR])
        k_top = sb("k_top", [HR, 1])
        k_max_bc = sb("k_max_bc", [T, HR])
        ek = [sb(f"ek{v}", [T, U, HR]) for v in range(1)]
        sum_col, inv_col, sum_row = sb("sum_col", [HR, 1]), sb("inv_col", [HR, 1]), sb("sum_row", [1, HR])
        gt = sb("gt", [HR, D])
        gh, xm, kv = (sb(n, [128, DC, HR]) for n in ("gh", "xm", "kv"))
        own = sb("own", [128, DC, HR])
        state = k.banks[0][0:HR, 0:D]
        q_part = a.qk[:, :, 0:HR].rearrange("p i (h r) -> p i h r", h=HEADS)
        k_part = a.qk[:, :, HR:2 * HR]
        by_head = lambda t: t[:].unsqueeze(3).broadcast_to([T, NT, HEADS, KR])

        with nc.Block() as block:
            @block.sync
            def _(sp):
                for to, what in ((a.w1, d["mix_W1"]), (a.w2, d["mix_W2"])):
                    sp.dma_start(to[:], what.rearrange("(c p) n -> p c n", p=128)).then_inc(s["weights_in"], 16)
                sp.wait_ge(s["weights_in"], 32)

            @block.gpsimd
            def _(pool):
                nc.gpsimd.tensor_tensor(a.b2_bc[:], a.b2_bc[:], a.beta_bc[:], ALU.add).then_inc(s["bias_added"], 1)
                pool.wait_ge(s["bias_added"], 1)
                nc.gpsimd.tensor_tensor(r.acc[:], r.acc[:], a.b2_bc[:].unsqueeze(1).broadcast_to([T, NT, D]), ALU.add).then_inc(s["bias_added"], 1)

            @block.vector
            def _(dve):
                steps = [0]

                def then(ins):
                    steps[0] += 1
                    ins.then_inc(s["step"], 1)
                    dve.wait_ge(s["step"], steps[0])

                nc.vector.tensor_reduce(q_max[:], q_part, AX, ALU.max)
                then(nc.vector.tensor_reduce(k_max[:], k_part.rearrange("p i n -> p n i"), AX, ALU.max))
                nc.vector.tensor_tensor(q_part, q_part, by_head(q_max), ALU.subtract)
                dve.wait_ge(s["pe_step"], 1)
                then(nc.vector.tensor_reduce(k_top[:], k.banks[1][0:HR, 0:T], AX, ALU.max))
                dve.wait_ge(s["pe_step"], 2)
                then(nc.vector.tensor_copy(k_max_bc[:], k.banks[2][0:T, 0:HR]))
                then(nc.vector.tensor_tensor(k_part, k_part, k_max_bc[:].unsqueeze(1).broadcast_to([T, NT, HR]), ALU.subtract))
                nc.vector.memset(own[:], 0.0)
                dve.wait_ge(s["act_step"], 1)
                then(nc.vector.tensor_reduce(k_sum[:], k_part.rearrange("p i n -> p n i"), AX, ALU.add))
                with dve.Fori(0, NG) as g:
                    dve.wait_ge(s["staged_free"], g + 1)
                    nc.vector.tensor_copy(ek[0][:], a.qk[:, ds(U * g, U), HR:2 * HR]).then_inc(s["staged"], 1)
                then(nc.vector.tensor_reduce(q_sum[:], q_part, AX, ALU.add))
                then(nc.vector.reciprocal(q_sum[:], q_sum[:]))
                for c in range(DC):
                    for q in range(128 // DH):
                        head = 4 * c + q
                        nc.vector.memset(own[DH * q:DH * (q + 1), c, KR * head:KR * (head + 1)], 1.0)
                then(nc.vector.tensor_tensor(q_part, q_part, by_head(q_sum), ALU.mult))
                dve.wait_ge(s["summed"], 1)
                nc.vector.tensor_copy(sum_col[:], k.banks[1][0:HR, 128:129])
                nc.vector.tensor_copy(sum_row[:], k.banks[1][0:1, 256:256 + HR])
                then(nc.vector.tensor_tensor(gt[:], state, a.g1_bc[:], ALU.mult))
                nc.vector.reciprocal(inv_col[:], sum_col[:])
                then(nc.vector.scalar_tensor_tensor(gt[:], a.b1_bc[:], sum_col[:], gt[:], ALU.mult, ALU.add))
                for n, to in ((3, gh), (4, xm)):
                    dve.wait_ge(s["pe_step"], n)
                    then(nc.vector.tensor_copy(to[:], k.banks[n][:, 0:DC * HR].rearrange("p (c n) -> p c n", c=DC)))
                dve.wait_ge(s["pe_step"], 5)
                then(nc.vector.tensor_tensor(kv[:], k.banks[5][:, 0:DC * HR].rearrange("p (c n) -> p c n", c=DC), own[:], ALU.mult))
                dve.wait_ge(s["pe_step"], 6)
                then(nc.vector.tensor_scalar(a.m_aug[0:HR, :], k.banks[6][0:HR, 0:D], inv_col[:], None, ALU.mult))

            @block.scalar
            def _(act):
                act.wait_ge(s["step"], 4)
                nc.scalar.activation(a.qk[:], a.qk[:], ACT.Exp).then_inc(s["act_step"], 1)

            @block.tensor
            def _(pe):
                pe.wait_ge(s["step"], 1)
                nc.tensor.transpose(k.banks[1][0:HR, 0:T], k_max[:], r.ident[0:T, 0:T]).then_inc(s["pe_step"], 1)
                pe.wait_ge(s["step"], 2)
                nc.tensor.matmul(k.banks[2][0:T, 0:HR], k_top[:].broadcast_to([HR, T]), r.ident[0:HR, 0:HR],
                                 start=True, stop=True).then_inc(s["pe_step"], 1)
                pe.sem_inc(s["staged_free"], 1)
                nc.tensor.matmul(state, r.zeros[0:T, 0:HR], r.zeros[0:T, 0:D], start=True, stop=False)
                with pe.Fori(0, NG) as g:
                    pe.wait_ge(s["staged"], g + 1)
                    for u in range(U):
                        done = nc.tensor.matmul(state, ek[0][:, u, :], r.nodes[:, ds(U * g + u, 1), :].rearrange("p o d -> p (o d)"), start=False, stop=False)
                    done.then_inc(s["staged_free"], 1)
                nc.tensor.matmul(state, r.zeros[0:T, 0:HR], r.zeros[0:T, 0:D], start=False, stop=True)
                nc.tensor.matmul(k.banks[1][0:HR, 128:129], k_sum[:], r.ones[:, 0:1], start=True, stop=True)
                nc.tensor.matmul(k.banks[1][0:1, 256:256 + HR], r.ones[:, 0:1], k_sum[:], start=True, stop=True).then_inc(s["summed"], 1)
                pe.wait_ge(s["step"], 10)
                for c in range(DC):
                    done = nc.tensor.transpose(k.banks[3][:, c * HR:(c + 1) * HR], gt[:, c * 128:(c + 1) * 128], r.ident[0:HR, 0:HR])
                done.then_inc(s["pe_step"], 1)
                pe.wait_ge(s["step"], 11)
                for n in range(DC):
                    out = k.banks[4][:, n * HR:(n + 1) * HR]
                    for c in range(DC):
                        nc.tensor.matmul(out, a.wx[:, c, n * 128:(n + 1) * 128], gh[:, c, :], start=c == 0, stop=False)
                    done = nc.tensor.matmul(out, a.bx_row[0:1, n * 128:(n + 1) * 128], sum_row[0:1, :], start=False, stop=True)
                done.then_inc(s["pe_step"], 1)
                pe.wait_ge(s["step"], 12)
                for n in range(DC):
                    done = nc.tensor.matmul(k.banks[5][:, n * HR:(n + 1) * HR], a.wv[:], xm[:, n, :], start=True, stop=True)
                done.then_inc(s["pe_step"], 1)
                pe.wait_ge(s["step"], 13)
                for n in range(DC):
                    done = nc.tensor.matmul(k.banks[6][0:HR, 0:D], kv[:, n, :], a.wo[:, n, :], start=n == 0, stop=n == DC - 1)
                done.then_inc(s["pe_step"], 1)


def by_parity(eng, step, body):
    parity = eng.snap(step & 1)
    with eng.If(parity == 0):
        body(0)
    with eng.Else():
        body(1)


def chunk_at(first, step):
    return (first + VU * step).with_bounds(min_val=0, max_val=EC - 1)


def graph_and_mix(nc, d, r, a, q, p):
    names = ("idx_ready passed visited hot_ready bias_summed"
             " ones_in sums_ready inv_degree deg_clipped deg_root mean_ready meanT_ready meanT_kept xgT_ready xgT_kept"
             " xg_turned xg_kept xg_stored logits_ready logits_kept"
             " q_staged qT_ready qT_kept attn_ready fx_ready fx_stats fx_moments fx_root fx_inverse h2_ready h2T_ready h2T_kept"
             " up_ready hidden_ready down_ready down_added blanked") + "".join(f" row_in{n}" for n in range(2 * VU))
    with phase(nc, "graph", names) as k:
        s, sb = k.s, k.sb
        gathered = [s[f"row_in{n}"] for n in range(2 * VU)]
        rows = sb("rows", [T, 2 * VU, D + 2])
        hot = [sb(f"hot{v}", [T, VU, T]) for v in range(2)]
        idx = [sb(f"idx{v}", [T, VU], I32) for v in range(2)]
        blank = sb("blank", [B, D])
        base = sb("base", [T, NT])
        bias_gc = sb("bias_gc", [128, DC])
        inv_deg = sb("inv_deg", [T, 1])
        deg_root = sb("deg_root", [T, 1])
        mean = sb("mean", [T, D])
        meanT = sb("meanT", [128, DC, T])
        xgT = sb("xgT", [128, DC, T])
        qs = sb("qs", [T, U, HR + 1])
        qT = sb("qT", [HR + 1, U, T])
        fx = sb("fx", [T, U, D])
        h2T = sb("h2T", [128, DC, U * T])
        hidden_all = sb("hidden", [128, FC * U * T])
        hidden = hidden_all[:].rearrange("p (m t) -> p m t", m=FC)
        h2 = hidden_all[0:T, 0:U * D].rearrange("p (u d) -> p u d", u=U)
        stats, moments, root = sb("stats", [T, U, 6]), sb("moments", [T, U, 2]), sb("root", [T, U])
        sums = k.banks[0][0:T, 0:D + 2]
        meanT_ps, xg_ps = k.banks[1][:, 0:DC * T], k.banks[1][0:T, 256:512]
        xgT_ps, logit_ps = k.banks[2][:, 0:DC * T], k.banks[2][0:T, 256:256 + E_GNN]
        slot = [k.banks[5 + u // 2][:, (u % 2) * 256:(u % 2) * 256 + 256] for u in range(U)]
        wide = [k.wide[0][:], k.wide[1][:]]
        turn_q = [k.banks[3][0:HR + 1, u * T:(u + 1) * T] for u in range(4)] + [k.banks[4][0:HR + 1, 0:T]]
        tile3 = lambda t, i: t[:, ds(i, 1), :].rearrange("p o d -> p (o d)")

        with nc.Block() as block:
            @block.sync
            def _(sp):
                sp.wait_ge(s["ones_in"], 1)
                for layer, used in ((q, 2 * CAP // B), (p, 2 * N // B)):
                    rows_out = layer.outputs.rearrange("(m p) d -> p m d", p=B)[:, used:, :]
                    sp.dma_start(rows_out, blank[:].unsqueeze(1).broadcast_to([B, rows_out.shape[1], D])).then_inc(s["blanked"], 16)
                sp.sem_inc(s["xg_stored"], 32)
                with sp.Fori(0, NG) as g:
                    sp.wait_ge(s["xg_kept"], U * g + U)
                    for p0, p1 in ((0, SPLIT), (SPLIT, T)):
                        sp.dma_start(rows_of(q.tokens, g)[p0:p1], r.nodes[p0:p1, ds(U * g, U), :]).then_inc(s["xg_stored"], 16)
                sp.wait_ge(s["xg_stored"], 32 * NG + 32)
                sp.wait_ge(s["blanked"], 32)

            @block.gpsimd
            def _(pool):
                pool.wait_ge(s["ones_in"], 1)
                with pool.Fori(0, NT) as b:
                    before = pool.value_load(a.visit_tab[0:1, 0, ds(b, 1)], min_val=0, max_val=NT * EC)
                    first = pool.value_load(a.visit_tab[0:1, 1, ds(b, 1)], min_val=0, max_val=EC - 1)
                    steps = pool.value_load(a.visit_tab[0:1, 2, ds(b, 1)], min_val=1, max_val=EC // VU)
                    with pool.Fori(0, steps) as j:
                        v = pool.snap(before + j)
                        pool.wait_ge(s["visited"], v + 1)
                        pool.sem_inc(s["passed"], 1)

                        def fetch(n):
                            nc.gpsimd.tensor_copy(idx[n][:], a.src_idx[:, ds(chunk_at(first, j), VU)]).then_inc(s["idx_ready"], 1)
                            pool.wait_ge(s["idx_ready"], v + 1)
                            pool.sem_inc(s["passed"], 1)
                            for u in range(VU):
                                nc.gpsimd.indirect_dma_start(
                                    out=rows[:, VU * n + u, 0:D], out_offset=None, in_=a.h_dram[:, :],
                                    in_offset=bass.IndirectOffsetOnAxis(ap=idx[n][:, u:u + 1], axis=0)).then_inc(gathered[VU * n + u], 16)
                        by_parity(pool, v, fetch)

            @block.vector
            def _(dve):
                nc.vector.memset(blank[:], 0.0)
                nc.vector.memset(rows[:], 1.0).then_inc(s["ones_in"], 1)
                nc.vector.memset(qs[:], 1.0)
                nc.vector.tensor_scalar(base[:], r.row[0:T, 0:NT], float(T), None, ALU.mult)
                nc.vector.tensor_tensor(bias_gc[:], a.cols[:, 18:20], a.cols[:, 20:22], ALU.add).then_inc(s["ones_in"], 1)
                dve.wait_ge(s["ones_in"], 2)

                with dve.Fori(0, NG) as g:
                    for u in range(U):
                        nc.vector.tensor_copy(qs[:, u, 0:HR], a.qk[:, ds(U * g + u, 1), 0:HR].rearrange("p o n -> p (o n)")).then_inc(s["q_staged"], 1)

                    def hot_of_block(u):
                        b = U * g + u
                        before = dve.value_load(a.visit_tab[0:1, 0, ds(b, 1)], min_val=0, max_val=NT * EC)
                        first = dve.value_load(a.visit_tab[0:1, 1, ds(b, 1)], min_val=0, max_val=EC - 1)
                        steps = dve.value_load(a.visit_tab[0:1, 2, ds(b, 1)], min_val=1, max_val=EC // VU)
                        with dve.Fori(0, steps) as j:
                            v = dve.snap(before + j)
                            dve.wait_ge(s["visited"], v + 1)

                            def mark(n):
                                nc.vector.scalar_tensor_tensor(
                                    hot[n][:], r.row[0:T, 0:T].unsqueeze(1).broadcast_to([T, VU, T]), base[:, ds(b, 1)],
                                    a.dst_t[:, ds(chunk_at(first, j), VU)].unsqueeze(2).broadcast_to([T, VU, T]),
                                    ALU.add, ALU.is_equal).then_inc(s["hot_ready"], 1)
                            by_parity(dve, v, mark)

                    def mean_of_block(u):
                        i = U * g + u
                        dve.wait_ge(s["sums_ready"], i + 1)
                        nc.vector.tensor_scalar(inv_deg[:], sums[:, D:D + 1], 1.0, None, ALU.max).then_inc(s["deg_clipped"], 1)
                        dve.wait_ge(s["deg_root"], i + 1)
                        nc.vector.reciprocal(inv_deg[:], deg_root[:]).then_inc(s["inv_degree"], 1)
                        dve.wait_ge(s["inv_degree"], i + 1)
                        nc.vector.tensor_scalar(mean[:], sums[:, 0:D], inv_deg[:], None, ALU.mult).then_inc(s["mean_ready"], 1)
                        dve.wait_ge(s["meanT_ready"], i + 1)
                        nc.vector.tensor_copy(meanT[:].rearrange("p c t -> p (c t)"), meanT_ps).then_inc(s["meanT_kept"], 1)

                    def tokens_of_block(u):
                        i = U * g + u
                        dve.wait_ge(s["xg_turned"], i + 1)
                        nc.vector.tensor_copy(tile3(r.nodes, i), xg_ps).then_inc(s["xg_kept"], 1)
                        dve.wait_ge(s["logits_ready"], i + 1)
                        nc.vector.tensor_tensor(tile3(q.logits, i), logit_ps, a.bg_bc[:], ALU.add).then_inc(s["logits_kept"], 1)

                    dve.wait_ge(s["qT_ready"], U * g + U)
                    for u in range(U):
                        nc.vector.tensor_copy(qT[:, u, :], turn_q[u]).then_inc(s["qT_kept"], 1)
                    hot_of_block(0)
                    mean_of_block(0)
                    dve.wait_ge(s["attn_ready"], U * g + U)
                    for u in range(U):
                        i = U * g + u
                        nc.vector.tensor_tensor(fx[:, u, :], slot[u][0:T, :], tile3(a.xn, i), ALU.add).then_inc(s["fx_ready"], 1)
                    dve.wait_ge(s["fx_ready"], U * g + U)
                    dve.sem_inc(s["passed"], 1)
                    for u in range(U):
                        nc.vector.bn_stats(stats[:, u, :], fx[:, u, :]).then_inc(s["fx_stats"], 1)
                    dve.wait_ge(s["fx_stats"], U * g + U)
                    dve.sem_inc(s["passed"], 1)
                    for u in range(U):
                        nc.vector.bn_aggr(moments[:, u, :], stats[:, u, :]).then_inc(s["fx_moments"], 1)
                    tokens_of_block(0)
                    dve.wait_ge(s["fx_root"], g + 1)
                    nc.vector.reciprocal(root[:], root[:]).then_inc(s["fx_inverse"], 1)
                    dve.wait_ge(s["fx_inverse"], g + 1)
                    for u in range(U):
                        nc.vector.tensor_scalar(h2[:, u, :], fx[:, u, :], moments[:, u, 0:1], root[:, u:u + 1],
                                                ALU.subtract, ALU.mult).then_inc(s["h2_ready"], 1)
                    for u in range(1, U):
                        hot_of_block(u)
                        mean_of_block(u)
                        tokens_of_block(u)
                    dve.wait_ge(s["down_ready"], U * g + U)
                    for u in range(U):
                        i = U * g + u
                        nc.vector.tensor_tensor(fx[:, u, :], slot[u][0:T, :], fx[:, u, :], ALU.add).then_inc(s["down_added"], 1)
                    for u in range(U):
                        i = U * g + u
                        dve.wait_ge(s["down_added"], i + 1)
                        done = nc.vector.tensor_tensor(tile3(r.acc, i), tile3(r.acc, i), fx[:, u, :], ALU.add)
                    done.then_inc(s["bias_summed"], 1)

            @block.scalar
            def _(act):
                with act.Fori(0, NG) as g:
                    for u in range(U):
                        i = U * g + u
                        act.wait_ge(s["deg_clipped"], i + 1)
                        nc.scalar.activation(deg_root[:], inv_deg[:], ACT.Sqrt).then_inc(s["deg_root"], 1)
                        if u == 1:
                            act.wait_ge(s["h2T_ready"], U * g + U)
                            for w in range(U):
                                for c in range(DC):
                                    done = nc.scalar.activation(h2T[:, c, w * T:(w + 1) * T], slot[w][:, c * T:(c + 1) * T],
                                                                ACT.Identity, scale=a.cols[:, 6 + c:7 + c], bias=a.cols[:, 8 + c:9 + c])
                                done.then_inc(s["h2T_kept"], 1)
                        if u in (2, 3):
                            for m in range(FC // 2 * (u - 2), FC // 2 * (u - 1)):
                                act.wait_ge(s["up_ready"], FC * g + m + 1)
                                nc.scalar.activation(hidden[:, m, :], wide[m % 2][:, 0:U * T], ACT.Gelu,
                                                     bias=a.cols[:, 10 + m:11 + m]).then_inc(s["hidden_ready"], 1)
                        act.wait_ge(s["xgT_ready"], i + 1)
                        for c in range(DC):
                            done = nc.scalar.activation(xgT[:, c, :], xgT_ps[:, c * T:(c + 1) * T], ACT.Identity, bias=bias_gc[:, c:c + 1])
                        done.then_inc(s["xgT_kept"], 1)
                        if u == 0:
                            act.wait_ge(s["fx_moments"], U * g + U)
                            nc.scalar.activation(root[:], moments[:, :, 1], ACT.Sqrt, bias=r.eps[0:T, :]).then_inc(s["fx_root"], 1)

            @block.tensor
            def _(pe):
                pe.wait_ge(s["ones_in"], 2)
                pe.sem_inc(s["visited"], 2)
                with pe.Fori(0, NG) as g:
                    def visit_block(u):
                        b = U * g + u
                        before = pe.value_load(a.visit_tab[0:1, 0, ds(b, 1)], min_val=0, max_val=NT * EC)
                        steps = pe.value_load(a.visit_tab[0:1, 2, ds(b, 1)], min_val=1, max_val=EC // VU)
                        pe.wait_ge(s["hot_ready"], before + 1)
                        nc.tensor.matmul(sums, r.zeros[0:T, 0:T], r.zeros[0:T, 0:D + 2], start=True, stop=False)
                        with pe.Fori(0, steps) as j:
                            v = pe.snap(before + j)
                            pe.wait_ge(s["hot_ready"], v + 1)

                            def add(n):
                                for u in range(VU):
                                    pe.wait_ge(gathered[VU * n + u], ((v >> 1) + 1) * 16)
                                    done = nc.tensor.matmul(sums, hot[n][:, u, :], rows[:, VU * n + u, :], start=False, stop=False)
                                done.then_inc(s["visited"], 1)
                            by_parity(pe, v, add)
                        nc.tensor.matmul(sums, r.zeros[0:T, 0:T], r.zeros[0:T, 0:D + 2], start=False, stop=True).then_inc(s["sums_ready"], 1)

                    def tokens_of_block(u):
                        i = U * g + u
                        pe.wait_ge(s["mean_ready"], i + 1)
                        for c in range(DC):
                            done = nc.tensor.transpose(meanT_ps[:, c * T:(c + 1) * T], mean[:, c * 128:(c + 1) * 128], r.ident[0:T, 0:T])
                        done.then_inc(s["meanT_ready"], 1)
                        for n in range(DC):
                            out = xgT_ps[:, n * T:(n + 1) * T]
                            for c in range(DC):
                                nc.tensor.matmul(out, a.w_res[:, c, n * 128:(n + 1) * 128], a.xnT[:, c, ds(i * T, T)], start=c == 0, stop=False)
                            if n == 0:
                                pe.wait_ge(s["meanT_kept"], i + 1)
                            for c in range(DC):
                                done = nc.tensor.matmul(out, a.w_gc[:, c, n * 128:(n + 1) * 128], meanT[:, c, :], start=False, stop=c == DC - 1)
                        done.then_inc(s["xgT_ready"], 1)
                        pe.wait_ge(s["xgT_kept"], i + 1)
                        for c in range(DC):
                            done = nc.tensor.transpose(xg_ps[:, c * 128:(c + 1) * 128], xgT[:, c, :], r.ident[:])
                        done.then_inc(s["xg_turned"], 1)
                        for c in range(DC):
                            done = nc.tensor.matmul(logit_ps, xgT[:, c, :], a.wg[:, c, :], start=c == 0, stop=c == DC - 1)
                        done.then_inc(s["logits_ready"], 1)

                    def up(chunks):
                        for m in chunks:
                            if m >= 2:
                                pe.wait_ge(s["hidden_ready"], FC * g + m - 1)
                            for lo, hi in ((0, 512), (512, U * T)):
                                for c in range(DC):
                                    done = nc.tensor.matmul(wide[m % 2][:, lo:hi], a.w1[:, c, m * 128:(m + 1) * 128], h2T[:, c, lo:hi],
                                                            start=c == 0, stop=c == DC - 1)
                            done.then_inc(s["up_ready"], 1)

                    for u in range(U):
                        pe.wait_ge(s["q_staged"], U * g + u + 1)
                        pe.sem_inc(s["passed"], 1)
                        nc.tensor.transpose(turn_q[u], qs[:, u, :], r.ident[0:T, 0:T]).then_inc(s["qT_ready"], 1)
                    visit_block(0)
                    for u in range(U):
                        pe.wait_ge(s["qT_kept"], U * g + u + 1)
                        nc.tensor.matmul(slot[u][0:T, :], qT[:, u, :], a.m_aug[:], start=True, stop=True).then_inc(s["attn_ready"], 1)
                    tokens_of_block(0)
                    visit_block(1)
                    for u in range(U):
                        pe.wait_ge(s["h2_ready"], U * g + u + 1)
                        for c in range(DC):
                            done = nc.tensor.transpose(slot[u][:, c * T:(c + 1) * T], h2[:, u, c * 128:(c + 1) * 128], r.ident[0:T, 0:T])
                        done.then_inc(s["h2T_ready"], 1)
                    tokens_of_block(1)
                    visit_block(2)
                    pe.wait_ge(s["h2T_kept"], U * g + U)
                    up(range(0, FC // 2))
                    tokens_of_block(2)
                    visit_block(3)
                    up(range(FC // 2, FC))
                    tokens_of_block(3)
                    visit_block(4)
                    pe.wait_ge(s["hidden_ready"], FC * g + FC)
                    for u in range(U):
                        for m in range(FC):
                            done = nc.tensor.matmul(slot[u][0:T, :], hidden[:, m, u * T:(u + 1) * T], a.w2[:, m, :], start=m == 0, stop=m == FC - 1)
                        done.then_inc(s["down_ready"], 1)
                    tokens_of_block(4)


def route(nc, name, r, q, experts, cap, dense):
    names = "passed step act_step pe_step staged top_found id_found chosen marked placed halves_ready halves_free"
    blocks = most_blocks(experts)
    E = experts
    with phase(nc, name, names) as k:
        s, sb = k.s, k.sb
        top = sb("top", [T, NT, 2])
        logits_s, top_s, top_id_s = sb("logits_s", [T, U, E]), sb("top_s", [T, U, 8]), sb("top_id_s", [T, U, 8], U32)
        choice = sb("choice", [T, NT, 2])
        hot = [sb(f"hot{v}", [T, NT, E], BF16) for v in range(2)]
        both = sb("both", [T, NT, E], BF16)
        run = [sb(f"run{v}", [T, NT, E], BF16) for v in range(2)]
        rank, part = sb("rank", [T, NT, E]), sb("part", [T, NT, E])
        start_bc = sb("start_bc", [T, E])
        col = sb("col", [E, 8])
        ended = sb("ended", [E, blocks + MU])
        place = sb("place", [T, NT, 2])
        first, order, fits, slot = (sb(n, [T, NT, 2]) for n in ("first", "order", "fits", "slot"))
        slot_hi, slot_lo = sb("slot_hi", [T, 2 * NT]), sb("slot_lo", [T, 2 * NT])
        token = sb("token", [T, NT])
        line = sb("line", [1, blocks + MU])
        hot_lo = sb("hot_lo", [T, 2 * U, B])
        hot_hi = sb("hot_hi", [T, 2 * U, blocks])
        big = sb("big", [T, NT])
        ranks = k.psum[0:T, 0:NT * E]
        table = k.banks[4][:, 0:blocks]
        flat = lambda t: t[:].rearrange("p i e -> p (i e)")
        over = lambda t: t.unsqueeze(2).broadcast_to([T, NT, E])
        pick = lambda t, n: t[:, :, n:n + 1].broadcast_to([T, NT, E])

        with nc.Block() as block:
            @block.vector
            def _(dve):
                steps = [0]

                def then(ins):
                    steps[0] += 1
                    ins.then_inc(s["step"], 1)
                    dve.wait_ge(s["step"], steps[0])

                if dense:
                    then(nc.vector.tensor_reduce(big[:], q.logits[:], AX, ALU.max))
                    then(nc.vector.tensor_tensor(q.logits[:], q.logits[:], over(big[:]), ALU.subtract))
                    dve.wait_ge(s["act_step"], 1)
                    then(nc.vector.tensor_reduce(big[:], q.logits[:], AX, ALU.add))
                    then(nc.vector.reciprocal(big[:], big[:]))
                    then(nc.vector.tensor_tensor(q.logits[:], q.logits[:], over(big[:]), ALU.mult))
                with dve.Fori(0, NG) as g:
                    nc.vector.tensor_copy(logits_s[:], q.logits[:, ds(U * g, U), :]).then_inc(s["staged"], 1)
                    dve.wait_ge(s["staged"], g + 1)
                    dve.sem_inc(s["passed"], 1)
                    for u in range(U):
                        nc.vector.max(top_s[:, u, :], logits_s[:, u, :]).then_inc(s["top_found"], 1)
                    dve.wait_ge(s["top_found"], U * g + U)
                    dve.sem_inc(s["passed"], 1)
                    for u in range(U):
                        nc.vector.max_index(top_id_s[:, u, :], top_s[:, u, :], logits_s[:, u, :]).then_inc(s["id_found"], 1)
                    dve.wait_ge(s["id_found"], U * g + U)
                    nc.vector.tensor_copy(top[:, ds(U * g, U), :], top_s[:, :, 0:2])
                    nc.vector.tensor_copy(choice[:, ds(U * g, U), :], top_id_s[:, :, 0:2]).then_inc(s["chosen"], 1)
                dve.wait_ge(s["chosen"], NG)
                row = r.row[0:T, 0:E].unsqueeze(1).broadcast_to([T, NT, E])
                for n in range(2):
                    then(nc.vector.tensor_tensor(hot[n][:], row, pick(choice, n), ALU.is_equal))
                then(nc.vector.tensor_tensor(both[:], hot[0][:], hot[1][:], ALU.add))
                now = both
                for n, reach in enumerate((1, 2, 4, 8, 16)):
                    new = run[n % 2]
                    nc.vector.tensor_copy(new[:, 0:reach, :], now[:, 0:reach, :])
                    then(nc.vector.tensor_tensor(new[:, reach:, :], now[:, reach:, :], now[:, 0:NT - reach, :], ALU.add))
                    now = new
                nc.vector.tensor_scalar(token[:], r.row[0:T, 0:NT], float(T), r.col[0:T, :], ALU.mult, ALU.add).then_inc(s["marked"], 1)
                if dense:
                    nc.vector.tensor_copy(q.gates[:], top[:, :, 0:2])
                else:
                    then(nc.vector.tensor_tensor(q.gates[:, :, 1:2], top[:, :, 1:2], top[:, :, 0:1], ALU.subtract))
                    gate_step = steps[0]
                    dve.wait_ge(s["act_step"], 1)
                    then(nc.vector.tensor_scalar(q.gates[:, :, 0:1], q.gates[:, :, 1:2], 1.0, None, ALU.add))
                    then(nc.vector.reciprocal(q.gates[:, :, 0:1], q.gates[:, :, 0:1]))
                    then(nc.vector.tensor_tensor(q.gates[:, :, 1:2], q.gates[:, :, 1:2], q.gates[:, :, 0:1], ALU.mult))
                    q.gate_step = gate_step
                dve.wait_ge(s["pe_step"], 1)
                then(nc.vector.tensor_scalar(col[:, 0:1], k.banks[5][0:E, 0:1], float(cap), None, ALU.min))
                for ins in round_to_whole(nc, col[:, 1:2], col[:, 0:1], 1.0 / B, (B - 1) / (2.0 * B)):
                    then(ins())
                nc.vector.tensor_copy(col[:, 7:8], col[:, 1:2]).then_inc(s["placed"], 1)
                dve.wait_ge(s["pe_step"], 2)
                then(nc.vector.tensor_copy(col[:, 2:3], k.banks[5][0:E, 8:9]))
                then(nc.vector.tensor_tensor(col[:, 3:4], col[:, 2:3], col[:, 1:2], ALU.add))
                nc.vector.tensor_scalar(ended[:], r.row[0:E, 0:blocks + MU], col[:, 3:4], None, ALU.is_ge).then_inc(s["placed"], 1)
                dve.wait_ge(s["pe_step"], 3)
                then(nc.vector.tensor_copy(start_bc[:], k.banks[6][0:T, 0:E]))
                then(nc.vector.scalar_tensor_tensor(rank[:], start_bc[:].unsqueeze(1).broadcast_to([T, NT, E]), 8192.0,
                                                    ranks.rearrange("p (i e) -> p i e", e=E), ALU.mult, ALU.add))
                for n in range(2):
                    then(nc.vector.tensor_tensor(part[:], rank[:], hot[n][:], ALU.mult))
                    then(nc.vector.tensor_reduce(place[:, :, n], part[:], AX, ALU.add))
                for ins in round_to_whole(nc, first[:], place[:], 1.0 / 8192, -4095.5 / 8192):
                    then(ins())
                then(nc.vector.scalar_tensor_tensor(order[:], first[:], -8192.0, place[:], ALU.mult, ALU.add))
                then(nc.vector.tensor_scalar(fits[:], order[:], float(cap), None, ALU.is_lt))
                then(nc.vector.scalar_tensor_tensor(slot[:], first[:], float(B), order[:], ALU.mult, ALU.add))
                then(nc.vector.scalar_tensor_tensor(slot[:], slot[:], 1.0, fits[:], ALU.add, ALU.mult))
                then(nc.vector.tensor_scalar(slot[:], slot[:], -1.0, None, ALU.add))
                nc.vector.tensor_tensor(q.gates[:], q.gates[:], fits[:], ALU.mult)
                nc.vector.tensor_scalar(q.slots[:], slot[:], 0.0, None, ALU.max)
                for ins in round_to_whole(nc, slot_hi[:], slot[:].rearrange("p i n -> p (i n)"), 1.0 / B, -(B / 2 - 0.5) / B):
                    then(ins())
                then(nc.vector.scalar_tensor_tensor(slot_lo[:], slot_hi[:], -float(B), slot[:].rearrange("p i n -> p (i n)"), ALU.mult, ALU.add))
                with dve.Fori(0, NG) as g:
                    for u in range(U):
                        for n in range(2):
                            w = 2 * u + n
                            at = ds(2 * U * g + w, 1)
                            dve.wait_ge(s["halves_free"], 2 * U * g + w + 1)
                            nc.vector.tensor_scalar(hot_lo[:, w, :], r.row[0:T, 0:B], slot_lo[:, at], None, ALU.is_equal)
                            nc.vector.tensor_scalar(hot_hi[:, w, :], r.row[0:T, 0:blocks], slot_hi[:, at], token[:, ds(U * g + u, 1)],
                                                    ALU.is_equal, ALU.mult).then_inc(s["halves_ready"], 1)
                then(nc.vector.tensor_tensor(part[:], hot[0][:], pick(q.gates, 0), ALU.mult))
                then(nc.vector.tensor_tensor(rank[:], hot[1][:], pick(q.gates, 1), ALU.mult))
                then(nc.vector.tensor_tensor(q.logits[:], part[:], rank[:], ALU.add))
                dve.wait_ge(s["pe_step"], 4)
                nc.vector.memset(q.token_of[:], 0)
                then(nc.vector.tensor_scalar(line[:], k.banks[7][0:1, 0:blocks + MU], float(E - 1), None, ALU.min))
                then(nc.vector.tensor_copy(q.expert_of[:], line[:]))
                then(nc.vector.tensor_copy(q.token_of[:, 0:blocks], table))
                for ins in round_to_whole(nc, line[:, 0:1], k.banks[6][0:1, 64:65], 1.0 / MU, (MU - 1) / (2.0 * MU)):
                    then(ins())
                then(nc.vector.tensor_copy(q.steps[:], line[:, 0:1]))

            @block.scalar
            def _(act):
                if dense:
                    act.wait_ge(s["step"], 2)
                    nc.scalar.activation(q.logits[:], q.logits[:], ACT.Exp).then_inc(s["act_step"], 1)
                else:
                    act.wait_ge(s["step"], q.gate_step)
                    nc.scalar.activation(q.gates[:, :, 1:2], q.gates[:, :, 1:2], ACT.Exp).then_inc(s["act_step"], 1)

            @block.tensor
            def _(pe):
                pe.sem_inc(s["halves_free"], 2 * U)
                pe.wait_ge(s["marked"], 1)
                counts = run[0]
                per = 512 // E
                for t0 in range(0, NT, per):
                    t1 = min(t0 + per, NT)
                    nc.tensor.matmul(ranks[:, t0 * E:t1 * E], r.tril[:], flat(both)[:, t0 * E:t1 * E], start=True, stop=False)
                    a0 = max(t0, 1)
                    nc.tensor.matmul(ranks[:, a0 * E:t1 * E], r.ones_b[:], flat(counts)[:, (a0 - 1) * E:(t1 - 1) * E], start=False, stop=True)
                nc.tensor.matmul(k.banks[5][0:E, 0:1], counts[:, NT - 1, :], r.ones_b[:, 0:1], start=True, stop=True).then_inc(s["pe_step"], 1)
                pe.wait_ge(s["placed"], 1)
                nc.tensor.matmul(k.banks[5][0:E, 8:9], r.tril_f[0:E, 0:E], col[:, 1:2], start=True, stop=True).then_inc(s["pe_step"], 1)
                pe.wait_ge(s["placed"], 2)
                nc.tensor.matmul(k.banks[6][0:T, 0:E], col[:, 2:3].broadcast_to([E, T]), r.ident[0:E, 0:E], start=True, stop=True)
                nc.tensor.matmul(k.banks[6][0:1, 64:65], r.ones[0:E, 0:1], col[:, 1:2], start=True, stop=True)
                nc.tensor.matmul(k.banks[7][0:1, 0:blocks + MU], r.ones[0:E, 0:1], ended[:], start=True, stop=True).then_inc(s["pe_step"], 1)
                nc.tensor.matmul(table, r.zeros[0:T, 0:B], r.zeros[0:T, 0:blocks], start=True, stop=False)
                with pe.Fori(0, NG) as g:
                    for w in range(2 * U):
                        pe.wait_ge(s["halves_ready"], 2 * U * g + w + 1)
                        nc.tensor.matmul(table, hot_lo[:, w, :], hot_hi[:, w, :], start=False, stop=False).then_inc(s["halves_free"], 1)
                nc.tensor.matmul(table, r.zeros[0:T, 0:B], r.zeros[0:T, 0:blocks], start=False, stop=True).then_inc(s["pe_step"], 1)


def run_experts(nc, name, r, q, experts, w1, w2, b1):
    names = ("b1_in b1_turned b1_kept x_turned xT_kept up_ready hidden_ready down_ready y_kept idx_ready passed"
             + "".join(f" x_in{n} w1_in{n} w2_in{n}" for n in range(MU)) + " y_stored0 y_stored1")
    E = experts
    with phase(nc, name, names) as k:
        s, sb = k.s, k.sb
        x_in, w1_in, w2_in = ([s[f"{w}{n}"] for n in range(MU)] for w in ("x_in", "w1_in", "w2_in"))
        y_stored = [s["y_stored0"], s["y_stored1"]]
        w1s, w2s = sb("w1s", [128, MU, DC, H]), sb("w2s", [128, MU, HC, D])
        idx = sb("idx", [B, MU], I32)
        x = sb("x", [B, MU, D])
        xT = sb("xT", [128, 2, DC, B])
        hidden = sb("hidden", [128, 2, HC, B])
        y = sb("y", [B, 2, D])
        b1_rows, b1T = sb("b1_rows", [E, H]), sb("b1T", [128, HC, E])
        xT_ps, up_ps, down_ps = k.banks[0:2], k.banks[2:4], k.banks[4:6]
        w1_rows, w2_rows = w1.rearrange("e (c p) h -> e p c h", p=128), w2.rearrange("e (c p) h -> e p c h", p=128)
        expert = lambda eng, m: eng.value_load(q.expert_of[0:1, ds(m, 1)], min_val=0, max_val=E - 1)
        loop_steps = lambda eng: eng.value_load(q.steps[0:1, 0:1], min_val=1, max_val=most_blocks(E) // MU)
        y_rows = q.outputs.rearrange("(m p) d -> m p d", p=B)

        with nc.Block() as block:
            @block.sync
            def _(sp):
                sp.dma_start(b1_rows[:], b1).then_inc(s["b1_in"], 16)

                def load(m, n):
                    e = expert(sp, m)
                    sp.wait_ge(s["up_ready"], m + 1)
                    sp.dma_start(w1s[:, n], w1_rows[ds(e, 1)].rearrange("o p c h -> p (o c) h")).then_inc(w1_in[n], 16)
                    sp.wait_ge(s["down_ready"], m + 1)
                    sp.dma_start(w2s[:, n], w2_rows[ds(e, 1)].rearrange("o p c h -> p (o c) h")).then_inc(w2_in[n], 16)
                load(0, 0)
                with sp.Fori(0, loop_steps(sp)) as i:
                    for u in range(MU):
                        load(MU * i + u + 1, (u + 1) % MU)
                n = loop_steps(sp)
                for w in (w1_in, w2_in):
                    for u in range(MU):
                        sp.wait_ge(w[u], 16 * n + (16 if u == 0 else 0))
                sp.sem_inc(s["passed"], 1)
                sp.wait_ge(s["b1_in"], 16)

            @block.gpsimd
            def _(pool):
                def gather(m, n):
                    pool.wait_ge(s["x_turned"], m + 1)
                    pool.sem_inc(s["passed"], 1)
                    nc.gpsimd.tensor_copy(idx[:, n:n + 1], q.token_of[:, ds(m, 1)]).then_inc(s["idx_ready"], 1)
                    pool.wait_ge(s["idx_ready"], m + 1)
                    pool.sem_inc(s["passed"], 1)
                    nc.gpsimd.indirect_dma_start(out=x[:, n, :], out_offset=None, in_=q.tokens[:, :],
                                                 in_offset=bass.IndirectOffsetOnAxis(ap=idx[:, n:n + 1], axis=0)).then_inc(x_in[n], 16)
                gather(0, 0)
                with pool.Fori(0, loop_steps(pool)) as i:
                    for u in range(MU):
                        gather(MU * i + u + 1, (u + 1) % MU)

            @block.vector
            def _(dve):
                dve.wait_ge(s["b1_turned"], 1)
                nc.vector.tensor_copy(b1T[:], k.banks[7][:, 0:HC * E].rearrange("p (c e) -> p c e", c=HC)).then_inc(s["b1_kept"], 1)
                dve.sem_inc(s["xT_kept"], 2)
                dve.sem_inc(s["y_kept"], 2)

                def keep_x(m, v):
                    dve.wait_ge(s["x_turned"], m + 1 + MU)
                    dve.wait_ge(s["up_ready"], m + MU - 1)
                    nc.vector.tensor_copy(xT[:, v], xT_ps[v][:, 0:DC * B].rearrange("p (c t) -> p c t", c=DC)).then_inc(s["xT_kept"], 1)

                def keep_y(m, v, uses):
                    dve.wait_ge(s["down_ready"], m + 1 + MU)
                    dve.wait_ge(y_stored[v], 16 * uses + 16)
                    nc.vector.tensor_copy(y[:, v, :], down_ps[v][:, 0:D]).then_inc(s["y_kept"], 1)
                keep_x(0, 0)
                with dve.Fori(0, loop_steps(dve)) as i:
                    for u in range(MU):
                        keep_x(MU * i + u + 1, (u + 1) % 2)
                        keep_y(MU * i + u, u % 2, MU // 2 * i + u // 2)

            @block.scalar
            def _(act):
                act.sem_inc(s["hidden_ready"], 2)
                act.sem_inc(y_stored[0], 16)
                act.sem_inc(y_stored[1], 16)
                act.wait_ge(s["b1_kept"], 1)

                def activate(m, v):
                    e = expert(act, m)
                    act.wait_ge(s["up_ready"], m + 1 + MU)
                    act.wait_ge(s["down_ready"], m + MU - 1)
                    for j in range(HC):
                        done = nc.scalar.activation(hidden[:, v, j, :], up_ps[v][:, j * B:(j + 1) * B], ACT.Gelu,
                                                    bias=b1T[:, j, ds(e, 1)])
                    done.then_inc(s["hidden_ready"], 1)
                activate(0, 0)
                with act.Fori(0, loop_steps(act)) as i:
                    for u in range(MU):
                        activate(MU * i + u + 1, (u + 1) % 2)
                        act.wait_ge(s["y_kept"], MU * i + u + 1 + 2)
                        act.dma_start(y_rows[ds(MU * i + u, 1)].rearrange("o p d -> p (o d)"), y[:, u % 2, :]).then_inc(y_stored[u % 2], 16)
                n = loop_steps(act)
                for v in range(2):
                    act.wait_ge(y_stored[v], MU // 2 * 16 * n + 16)
                act.sem_inc(s["passed"], 1)

            @block.tensor
            def _(pe):
                pe.wait_ge(s["b1_in"], 16)
                for c in range(HC):
                    done = nc.tensor.transpose(k.banks[7][:, c * E:(c + 1) * E], b1_rows[:, c * 128:(c + 1) * 128], r.ident[0:E, 0:E])
                done.then_inc(s["b1_turned"], 1)
                for primed in (s["x_turned"], s["up_ready"], s["down_ready"]):
                    pe.sem_inc(primed, MU)

                def up(m, v, n, landed):
                    pe.wait_ge(x_in[n], landed)
                    pe.wait_ge(s["xT_kept"], m + 1)
                    for c in range(DC):
                        done = nc.tensor.transpose(xT_ps[v][:, c * B:(c + 1) * B], x[:, n, c * 128:(c + 1) * 128], r.ident[:])
                    done.then_inc(s["x_turned"], 1)
                    pe.wait_ge(w1_in[n], landed)
                    pe.wait_ge(s["hidden_ready"], m + 1)
                    pe.wait_ge(s["xT_kept"], m + 3)
                    for j in range(HC):
                        for c in range(DC):
                            done = nc.tensor.matmul(up_ps[v][:, j * B:(j + 1) * B], w1s[:, n, c, j * 128:(j + 1) * 128], xT[:, v, c, :],
                                                    start=c == 0, stop=c == DC - 1)
                    done.then_inc(s["up_ready"], 1)

                def down(m, v, n, landed):
                    pe.wait_ge(w2_in[n], landed)
                    pe.wait_ge(s["y_kept"], m + 1)
                    pe.wait_ge(s["hidden_ready"], m + 3)
                    for j in range(HC):
                        done = nc.tensor.matmul(down_ps[v][:, 0:D], hidden[:, v, j, :], w2s[:, n, j, :], start=j == 0, stop=j == HC - 1)
                    done.then_inc(s["down_ready"], 1)
                up(0, 0, 0, 16)
                with pe.Fori(0, loop_steps(pe)) as i:
                    for u in range(MU):
                        up(MU * i + u + 1, (u + 1) % 2, (u + 1) % MU, 16 * i + (32 if u == MU - 1 else 16))
                        down(MU * i + u, u % 2, u, 16 * i + 16)


def combine(nc, name, r, q, experts, b2, out):
    names = ("b2_in idx_ready passed joined joined1 joined2 joined3 gates_staged gates_turned gatesT_kept bias_ready summed out_stored"
             + "".join(f" y_in{n}" for n in range(2 * U)))
    E = experts
    with phase(nc, name, names) as k:
        s, sb = k.s, k.sb
        y_in = [s[f"y_in{n}"] for n in range(2 * U)]
        b2s = sb("b2", [E, D])
        idx = sb("idx", [T, 2 * U], I32)
        y = sb("y", [T, 2 * U, D])
        total = sb("total", [T, U, D])
        gates_s, gatesT = sb("gates_s", [T, U, E]), sb("gatesT", [E, U, T])
        turned = [k.banks[u // 4][0:E, (u % 4) * T:(u % 4 + 1) * T] for u in range(U)]
        bias = [k.banks[2 + u // 2][0:T, (u % 2) * 256:(u % 2) * 256 + 256] for u in range(U)]
        sums = k.banks[7][0:T, 0:D]
        home = r.nodes if out is None else r.acc
        tile3 = lambda t, i: t[:, ds(i, 1), :].rearrange("p o d -> p (o d)")
        slots = q.slots[:].rearrange("p i n -> p (i n)")
        gates = q.gates[:].rearrange("p i n -> p (i n)")
        with nc.Block() as block:
            @block.sync
            def _(sp):
                sp.dma_start(b2s[:], b2).then_inc(s["b2_in"], 16)
                if out is not None:
                    with sp.Fori(0, NG) as g:
                        sp.wait_ge(s["joined3"], U * g + U)
                        for p0, p1 in ((0, SPLIT), (SPLIT, T)):
                            sp.dma_start(rows_of(out, g)[p0:p1], home[p0:p1, ds(U * g, U), :]).then_inc(s["out_stored"], 16)
                    sp.wait_ge(s["out_stored"], 32 * NG)
                sp.wait_ge(s["b2_in"], 16)

            @block.gpsimd
            def _(pool):
                with pool.Fori(0, NG) as g:
                    for u in range(U):
                        i = U * g + u
                        pool.wait_ge(s["joined"], i + 1)
                        nc.gpsimd.tensor_copy(idx[:, 2 * u:2 * u + 2], slots[:, ds(2 * i, 2)]).then_inc(s["idx_ready"], 1)
                        pool.wait_ge(s["idx_ready"], i + 1)
                        pool.sem_inc(s["passed"], 1)
                        for n in range(2):
                            w = 2 * u + n
                            nc.gpsimd.indirect_dma_start(out=y[:, w, :], out_offset=None, in_=q.outputs[:, :],
                                                         in_offset=bass.IndirectOffsetOnAxis(ap=idx[:, w:w + 1], axis=0)).then_inc(y_in[w], 16)

            @block.vector
            def _(dve):
                dve.sem_inc(s["joined"], U)
                with dve.Fori(0, NG) as g:
                    for u in range(U):
                        nc.vector.tensor_copy(gates_s[:, u, :], tile3(q.logits, U * g + u)).then_inc(s["gates_staged"], 1)
                    dve.wait_ge(s["bias_ready"], U * g + U)
                    for u in range(U):
                        i = U * g + u
                        nc.vector.tensor_tensor(total[:, u, :], bias[u], tile3(home, i), ALU.add).then_inc(s["joined1"], 1)
                    for u in range(U):
                        i = U * g + u
                        dve.wait_ge(s["joined1"], i + 1)
                        dve.wait_ge(y_in[2 * u], 16 * g + 16)
                        nc.vector.scalar_tensor_tensor(total[:, u, :], y[:, 2 * u, :], gates[:, ds(2 * i, 1)], total[:, u, :],
                                                       ALU.mult, ALU.add).then_inc(s["joined2"], 1)
                    for u in range(U):
                        i = U * g + u
                        dve.wait_ge(s["joined2"], i + 1)
                        dve.wait_ge(y_in[2 * u + 1], 16 * g + 16)
                        nc.vector.scalar_tensor_tensor(tile3(home, i), y[:, 2 * u + 1, :], gates[:, ds(2 * i + 1, 1)], total[:, u, :],
                                                       ALU.mult, ALU.add).then_inc(s["joined3"], 1)
                    for u in range(U):
                        dve.wait_ge(s["joined3"], U * g + u + 1)
                        dve.sem_inc(s["joined"], 1)

            @block.scalar
            def _(act):
                with act.Fori(0, NG) as g:
                    act.wait_ge(s["gates_turned"], U * g + U)
                    for u in range(U):
                        nc.scalar.activation(gatesT[:, u, :], turned[u], ACT.Copy).then_inc(s["gatesT_kept"], 1)

            @block.tensor
            def _(pe):
                pe.wait_ge(s["b2_in"], 16)
                if out is None:
                    nc.tensor.matmul(sums, r.zeros[0:T, 0:T], r.zeros[0:T, 0:D], start=True, stop=False)
                with pe.Fori(0, NG) as g:
                    for u in range(U):
                        pe.wait_ge(s["gates_staged"], U * g + u + 1)
                        pe.sem_inc(s["passed"], 1)
                        nc.tensor.transpose(turned[u], gates_s[:, u, :], r.ident[0:T, 0:T]).then_inc(s["gates_turned"], 1)
                    for u in range(U):
                        pe.wait_ge(s["gatesT_kept"], U * g + u + 1)
                        nc.tensor.matmul(bias[u], gatesT[:, u, :], b2s[:], start=True, stop=True).then_inc(s["bias_ready"], 1)
                    if out is None:
                        for u in range(U):
                            pe.wait_ge(s["joined3"], U * g + u + 1)
                            nc.tensor.matmul(sums, r.ones[:], tile3(r.nodes, U * g + u), start=False, stop=False)
                if out is None:
                    nc.tensor.matmul(sums, r.zeros[0:T, 0:T], r.zeros[0:T, 0:D], start=False, stop=True).then_inc(s["summed"], 1)
                    pe.wait_ge(s["summed"], 1)
            if out is None:
                @block.vector
                def _(dve):
                    dve.wait_ge(s["summed"], 1)
                    nc.vector.tensor_scalar(q.mean[:], sums, 1.0 / N, None, ALU.mult).then_inc(s["joined1"], 1)
                    dve.wait_ge(s["joined1"], NT + 1)


def batch_norm(nc, d, r, q, p):
    names = ("passed loaded centred squared squares_free squared_sum scaled step roots"
             " product sum_ready sum_stats sum_moments sum_root sum_inverse x_ready x_stored xT_ready xT_kept logits_ready logits_kept")
    with phase(nc, "norm", names) as k:
        s, sb = k.s, k.sb
        gamma, spread = sb("gamma", [T, D]), sb("spread", [T, D])
        gate_w, gate_b = sb("gate_w", [128, DC, E_FFN]), sb("gate_b", [T, E_FFN])
        squares = sb("squares", [T, U, D])
        stats, moments, root = sb("stats", [T, U, 6]), sb("moments", [T, U, 2]), sb("root", [T, U])
        x = sb("x", [T, U, D])
        xT = sb("xT", [128, U, DC, T])
        sums = k.banks[7][0:T, 0:D]
        turned = [k.banks[u // 2][:, (u % 2) * 256:(u % 2) * 256 + DC * T] for u in range(U)]
        logit_ps = k.banks[3][0:T, 0:U * E_FFN]
        tile3 = lambda t, i: t[:, ds(i, 1), :].rearrange("p o d -> p (o d)")
        with nc.Block() as block:
            @block.sync
            def _(sp):
                for p0, p1 in ((0, SPLIT), (SPLIT, T)):
                    sp.dma_start(gamma[p0:p1], d["gnn_gamma"].partition_broadcast(p1 - p0)).then_inc(s["loaded"], 16)
                    sp.dma_start(gate_b[p0:p1], d["ffn_gate_b"].partition_broadcast(p1 - p0)).then_inc(s["loaded"], 16)
                sp.dma_start(gate_w[:], d["ffn_gate_w"].rearrange("(c p) n -> p c n", p=128)).then_inc(s["loaded"], 16)
                sp.sem_inc(s["x_stored"], 32)
                with sp.Fori(0, NG) as g:
                    sp.wait_ge(s["x_ready"], U * g + U)
                    for p0, p1 in ((0, SPLIT), (SPLIT, T)):
                        sp.dma_start(rows_of(p.tokens, g)[p0:p1], x[p0:p1]).then_inc(s["x_stored"], 16)
                sp.wait_ge(s["x_stored"], 32 * NG + 32)
                sp.wait_ge(s["loaded"], 80)

            @block.vector
            def _(dve):
                with dve.Fori(0, NG) as g:
                    for u in range(U):
                        nc.vector.tensor_tensor(tile3(r.nodes, U * g + u), tile3(r.nodes, U * g + u), q.mean[:], ALU.subtract).then_inc(s["centred"], 1)
                dve.wait_ge(s["squared_sum"], 1)
                nc.vector.tensor_scalar(spread[:], sums, 1.0 / N, None, ALU.mult).then_inc(s["step"], 1)
                dve.wait_ge(s["roots"], 1)
                nc.vector.reciprocal(spread[:], spread[:]).then_inc(s["step"], 1)
                dve.wait_ge(s["step"], 2)
                dve.wait_ge(s["loaded"], 80)
                nc.vector.tensor_tensor(spread[:], spread[:], gamma[:], ALU.mult).then_inc(s["step"], 1)
                dve.wait_ge(s["step"], 3)
                with dve.Fori(0, NG) as g:
                    for u in range(U):
                        nc.vector.tensor_tensor(tile3(r.nodes, U * g + u), tile3(r.nodes, U * g + u), spread[:], ALU.mult).then_inc(s["product"], 1)
                    for u in range(U):
                        i = U * g + u
                        dve.wait_ge(s["product"], i + 1)
                        nc.vector.tensor_tensor(tile3(r.acc, i), tile3(r.acc, i), tile3(r.nodes, i), ALU.add).then_inc(s["sum_ready"], 1)
                    dve.wait_ge(s["sum_ready"], U * g + U)
                    dve.sem_inc(s["passed"], 1)
                    for u in range(U):
                        nc.vector.bn_stats(stats[:, u, :], tile3(r.acc, U * g + u)).then_inc(s["sum_stats"], 1)
                    dve.wait_ge(s["sum_stats"], U * g + U)
                    dve.sem_inc(s["passed"], 1)
                    for u in range(U):
                        nc.vector.bn_aggr(moments[:, u, :], stats[:, u, :]).then_inc(s["sum_moments"], 1)
                    dve.wait_ge(s["sum_root"], g + 1)
                    nc.vector.reciprocal(root[:], root[:]).then_inc(s["sum_inverse"], 1)
                    dve.wait_ge(s["sum_inverse"], g + 1)
                    dve.wait_ge(s["x_stored"], 32 * g + 32)
                    for u in range(U):
                        i = U * g + u
                        nc.vector.tensor_scalar(x[:, u, :], tile3(r.acc, i), moments[:, u, 0:1], root[:, u:u + 1],
                                                ALU.subtract, ALU.mult).then_inc(s["x_ready"], 1)
                    dve.wait_ge(s["logits_ready"], U * g + U)
                    nc.vector.tensor_tensor(p.logits[:, ds(U * g, U), :], logit_ps.rearrange("p (u n) -> p u n", u=U),
                                            gate_b[:].unsqueeze(1).broadcast_to([T, U, E_FFN]), ALU.add).then_inc(s["logits_kept"], 1)

            @block.scalar
            def _(act):
                with act.Fori(0, NG) as g:
                    for u in range(U):
                        i = U * g + u
                        act.wait_ge(s["centred"], i + 1)
                        act.wait_ge(s["squares_free"], i + 1)
                        nc.scalar.activation(squares[:, u, :], tile3(r.nodes, i), ACT.Square).then_inc(s["squared"], 1)
                act.wait_ge(s["step"], 1)
                nc.scalar.activation(spread[:], spread[:], ACT.Sqrt, bias=r.eps[0:T, :]).then_inc(s["roots"], 1)
                with act.Fori(0, NG) as g:
                    act.wait_ge(s["sum_moments"], U * g + U)
                    nc.scalar.activation(root[:], moments[:, :, 1], ACT.Sqrt, bias=r.eps[0:T, :]).then_inc(s["sum_root"], 1)
                    act.wait_ge(s["xT_ready"], U * g + U)
                    for u in range(U):
                        nc.scalar.activation(xT[:, u], turned[u].rearrange("p (c t) -> p c t", c=DC), ACT.Copy).then_inc(s["xT_kept"], 1)

            @block.tensor
            def _(pe):
                pe.sem_inc(s["squares_free"], U)
                nc.tensor.matmul(sums, r.zeros[0:T, 0:T], r.zeros[0:T, 0:D], start=True, stop=False)
                with pe.Fori(0, NG) as g:
                    for u in range(U):
                        pe.wait_ge(s["squared"], U * g + u + 1)
                        nc.tensor.matmul(sums, r.ones[:], squares[:, u, :], start=False, stop=False).then_inc(s["squares_free"], 1)
                nc.tensor.matmul(sums, r.zeros[0:T, 0:T], r.zeros[0:T, 0:D], start=False, stop=True).then_inc(s["squared_sum"], 1)
                pe.wait_ge(s["loaded"], 80)
                with pe.Fori(0, NG) as g:
                    for u in range(U):
                        pe.wait_ge(s["x_ready"], U * g + u + 1)
                        for c in range(DC):
                            done = nc.tensor.transpose(turned[u][:, c * T:(c + 1) * T], x[:, u, c * 128:(c + 1) * 128], r.ident[0:T, 0:T])
                        done.then_inc(s["xT_ready"], 1)
                    for u in range(U):
                        pe.wait_ge(s["xT_kept"], U * g + u + 1)
                        for c in range(DC):
                            done = nc.tensor.matmul(logit_ps[:, u * E_FFN:(u + 1) * E_FFN], xT[:, u, c, :], gate_w[:, c, :], start=c == 0, stop=c == DC - 1)
                        done.then_inc(s["logits_ready"], 1)


def program(nc, d, out):
    with ExitStack() as scope:
        r = resident(nc, scope)
        constants(nc, r)
        sb = lambda where, n, shape, dt=F32: where.enter_context(nc.sbuf_tensor(n, shape, dt))

        def layer(where, name, experts):
            blocks = most_blocks(experts)
            kept = Bag()
            kept.logits = sb(where, f"{name}_logits", [T, NT, experts])
            kept.gates = sb(where, f"{name}_gates", [T, NT, 2])
            kept.slots = sb(where, f"{name}_slots", [T, NT, 2], I32)
            kept.token_of = sb(where, f"{name}_token_of", [B, blocks + MU], I32)
            kept.expert_of = sb(where, f"{name}_expert_of", [1, blocks + MU], I32)
            kept.steps = sb(where, f"{name}_steps", [1, 1], I32)
            kept.tokens = nc.dram_tensor(f"{name}_tokens", (N, D), F32, kind="Internal").ap()
            kept.outputs = nc.dram_tensor(f"{name}_outputs", (blocks * B, D), F32, kind="Internal").ap()
            return kept
        with ExitStack() as graph_scope:
            q = layer(graph_scope, "graph", E_GNN)
            p = layer(graph_scope, "dense", E_FFN)
            q.mean = sb(graph_scope, "column_mean", [T, D])
            with ExitStack() as mix_scope:
                m = lambda n, shape, dt=F32: sb(mix_scope, n, shape, dt)
                a = Bag()
                a.xn, a.xnT, a.qk = m("xn", [T, NT, D]), m("xnT", [128, DC, N]), m("qk", [T, NT, 2 * HR])
                a.src_idx, a.dst_t = m("src_idx", [T, EC + EPAD], I32), m("dst_t", [T, EC + EPAD])
                a.visit_tab, a.rs_out = m("visit_tab", [1, 3, NT], I32), m("rs_out", [T, NT])
                a.wx, a.wv, a.wo = m("wx", [128, DC, D]), m("wv", [128, 128]), m("wo", [128, DC, D])
                a.w_gc, a.w_res, a.wg = m("w_gc", [128, DC, D]), m("w_res", [128, DC, D]), m("wg", [128, DC, E_GNN])
                a.cols = m("cols", [128, 22])
                a.bx_row, a.g1_bc, a.b1_bc = m("bx_row", [1, D]), m("g1_bc", [HR, D]), m("b1_bc", [HR, D])
                a.b2_bc, a.bg_bc, a.beta_bc = m("b2_bc", [T, D]), m("bg_bc", [T, E_GNN]), m("beta_bc", [T, D])
                a.m_aug = m("m_aug", [HR + 1, D])
                a.h_dram = nc.dram_tensor("scaled_nodes", (N, D), F32, kind="Internal").ap()
                prepare(nc, d, r, a)
                a.w1, a.w2 = m("w1", [128, DC, FF]), m("w2", [128, FC, D])
                attention_state(nc, d, r, a)
                graph_and_mix(nc, d, r, a, q, p)
            route(nc, "graph_route", r, q, E_GNN, CAP, dense=False)
            run_experts(nc, "graph_experts", r, q, E_GNN, d["gnn_w1"], d["gnn_w2"], d["gnn_b1"])
            combine(nc, "graph_combine", r, q, E_GNN, d["gnn_b2"], None)
            batch_norm(nc, d, r, q, p)
            route(nc, "dense_route", r, p, E_FFN, 2 * N, dense=True)
            run_experts(nc, "dense_experts", r, p, E_FFN, d["ffn_W1"], d["ffn_W2"], d["ffn_b1"])
            combine(nc, "dense_combine", r, p, E_FFN, d["ffn_b2"], out)


_INS = ["x", "src", "dst", "gnn_W_gc", "gnn_b_gc", "gnn_W_res", "gnn_b_res", "gnn_Wg", "gnn_bg", "gnn_w1", "gnn_b1", "gnn_w2", "gnn_b2",
        "gnn_gamma", "gnn_beta", "mix_ln1_g", "mix_ln1_b", "mix_Wx", "mix_bx", "mix_Wq", "mix_Wk", "mix_Wv", "mix_Wo", "mix_bo",
        "mix_ln2_g", "mix_ln2_b", "mix_W1", "mix_b1", "mix_W2", "mix_b2",
        "ffn_gate_w", "ffn_gate_b", "ffn_W1", "ffn_b1", "ffn_W2", "ffn_b2"]


def kernel(**inputs):
    import numpy as _np
    import concourse.bacc as _bacc
    from concourse import mybir as _mybir
    from concourse.bass_utils import run_bass_kernel_spmd as _run

    nc = _bacc.Bacc("TRN2", target_bir_lowering=False, num_devices=1)
    arrays, args = {}, {}
    for name in _INS:
        a = _np.ascontiguousarray(inputs[name if name in inputs else "L0_" + name])
        arrays[f"in_{name}"] = a
        args[name] = nc.dram_tensor(f"in_{name}", a.shape, _mybir.dt.from_np(a.dtype), kind="ExternalInput").ap()
    out = nc.dram_tensor("out_0", (N, D), F32, kind="ExternalOutput").ap()
    program(nc, args, out)
    return _run(nc, [arrays], core_ids=[0]).results[0]["out_0"]
```

```python
from contextlib import ExitStack, contextmanager

import concourse.bass as bass
from concourse import mybir

F32, I32, U32, BF16 = mybir.dt.float32, mybir.dt.int32, mybir.dt.uint32, mybir.dt.bfloat16
ALU = mybir.AluOpType
ACT = mybir.ActivationFunctionType
AX = mybir.AxisListType.X
ds = bass.ds

N, D = 3125, 256
NE = 50000
T = 125
NT = N // T
U = 5
NG = NT // U
EC = NE // T
EQ = 100
EJ = EC // EQ
VU = 4
SETS = 4
EPAD = VU
HG = 20
DC = D // 128
EPS = 1e-5
MAGIC = float(3 << 22)
HEADS, DH, KR = 8, 32, 4
HR = HEADS * KR
FF = 1024
FC = FF // 128
H = 512
HC = H // 128
B = 128
E_GNN, E_FFN = 64, 8
CAP = 1024
SPLIT = 112


class Bag:
    pass


class Cut:

    def __init__(self, experts, wide, unroll):
        self.experts, self.wide, self.unroll = experts, wide, unroll
        slots = B * wide
        loads = (2 * N + experts * (slots - 1)) // slots
        self.steps = -(-loads // unroll)
        self.loads = self.steps * unroll
        self.blocks = self.loads * wide


CUTS = {E_GNN: Cut(E_GNN, wide=1, unroll=4), E_FFN: Cut(E_FFN, wide=2, unroll=2)}


@contextmanager
def phase(nc, name, semaphores):
    sems = {s: nc.alloc_semaphore(f"{name}_{s}") for s in semaphores.split()}
    with ExitStack() as scope:
        tools = Bag()
        tools.sb = lambda n, shape, dt=F32: scope.enter_context(nc.sbuf_tensor(f"{name}_{n}", shape, dt))
        tools.psum = scope.enter_context(nc.psum_tensor(f"{name}_psum", [128, 8 * 512], F32))[:]
        tools.s = sems
        tools.banks = [tools.psum[:, 512 * n:512 * (n + 1)] for n in range(8)]
        tools.wide = [tools.psum[:, 512 * n:512 * (n + 2)] for n in (3, 5)]
        yield tools
    nc.clear_and_free_semaphores(list(sems.values()))
    nc.all_engine_barrier(sem_only=True)


def rows_of(dram, group):
    return dram.rearrange("(g u p) d -> g p u d", p=T, u=U)[group]


def round_to_whole(nc, out, in_, scale, shift):
    return (lambda: nc.vector.tensor_scalar(out, in_, scale, shift, ALU.mult, ALU.add),
            lambda: nc.vector.tensor_scalar(out, out, MAGIC, MAGIC, ALU.add, ALU.subtract))


def resident(nc, scope):
    sb = lambda n, shape, dt=F32: scope.enter_context(nc.sbuf_tensor(n, shape, dt))
    r = Bag()
    r.acc = sb("acc", [T, NT, D])
    r.nodes = sb("nodes", [T, NT, D])
    r.ident = sb("ident", [128, 128])
    r.ones = sb("ones", [T, T])
    r.zeros = sb("zeros", [128, D + 2], BF16)
    r.tril_f = sb("tril_f", [64, 64])
    r.tril = sb("tril", [T, T], BF16)
    r.ones_b = sb("ones_b", [T, T], BF16)
    r.row = sb("row", [128, 512])
    r.col = sb("col", [128, 1])
    r.eps = sb("eps", [128, 1])
    return r


def constants(nc, r):
    with phase(nc, "constants", "filled shaped") as k:
        s = k.s
        with nc.Block() as block:
            @block.gpsimd
            def _(pool):
                nc.gpsimd.memset(r.ident[:], 0.0)
                nc.gpsimd.memset(r.ones[:], 1.0)
                nc.gpsimd.memset(r.ones_b[:], 1.0)
                nc.gpsimd.memset(r.tril[:], 1.0)
                nc.gpsimd.memset(r.tril_f[:], 1.0)
                nc.gpsimd.memset(r.zeros[:], 0.0)
                nc.gpsimd.memset(r.eps[:], EPS)
                nc.gpsimd.iota(r.row[:], pattern=[[1, 512]], base=0, channel_multiplier=0,
                               allow_small_or_imprecise_dtypes=True)
                nc.gpsimd.iota(r.col[:], pattern=[[0, 1]], base=0, channel_multiplier=1,
                               allow_small_or_imprecise_dtypes=True).then_inc(s["filled"], 1)
                pool.wait_ge(s["filled"], 1)
                nc.gpsimd.affine_select(out=r.ident[:], in_=r.ident[:], compare_op=ALU.not_equal, fill=1.0,
                                        base=0, pattern=[[-1, 128]], channel_multiplier=1).then_inc(s["shaped"], 1)
                nc.gpsimd.affine_select(out=r.tril[:], in_=r.tril[:], compare_op=ALU.is_gt, fill=0.0,
                                        base=0, pattern=[[1, T]], channel_multiplier=-1).then_inc(s["shaped"], 1)
                nc.gpsimd.affine_select(out=r.tril_f[:], in_=r.tril_f[:], compare_op=ALU.is_gt, fill=0.0,
                                        base=0, pattern=[[1, 64]], channel_multiplier=-1).then_inc(s["shaped"], 1)
                pool.wait_ge(s["shaped"], 3)


def prepare(nc, d, r, a, layers):
    names = ("edges_in x_in mix_in rest_in edges_float edge_columns ids ids_step hist_ready hist_free degree degree_root"
             " chunk_range range_bc visit_step visit_row tables blockdiag wx_turned wx_copied folded qk_weights"
             " stats1 moments1 root1 inverse1 xn_ready xn_free h_ready h_stored stats2 moments2 root2 inverse2"
             " hn_ready hn_free xnT_turned hnT_turned hT_ready hT_free qk_ready qk_kept xnT_kept passed blanked")
    with phase(nc, "prepare", names) as k:
        s, sb = k.s, k.sb
        src_n, dst_n = sb("src_n", [EQ, EJ, T], I32), sb("dst_n", [EQ, EJ, T], I32)
        src_f, dst_f = sb("src_f", [EQ, EJ, T]), sb("dst_f", [EQ, EJ, T])
        src_t, src_hi = sb("src_t", [T, EC]), sb("src_hi", [T, EC])
        hi_b, lo_b = sb("hi_b", [T, EC], BF16), sb("lo_b", [T, EC], BF16)
        count_lo, count_hi = sb("count_lo", [T, T, HG], BF16), sb("count_hi", [T, NT, HG], BF16)
        hot_lo = [sb(f"hot_lo{v}", [T, T, HG], BF16) for v in range(2)]
        hot_hi = [sb(f"hot_hi{v}", [T, NT, HG], BF16) for v in range(2)]
        degree = sb("degree", [T, NT])
        reach = sb("reach", [EQ, 2, EJ])
        lo_c, hi_c = sb("lo_c", [NT, EC]), sb("hi_c", [NT, EC])
        visit = sb("visit", [NT, 8])
        blockdiag_qk = sb("blockdiag_qk", [128, DC, 2 * HR])
        bias_rows = sb("bias_rows", [22, 128])
        wx_t = sb("wx_t", [128, DC, D])
        wqk = sb("wqk", [128, DC, 2 * HR])
        bqk = sb("bqk", [T, 2 * HR])
        stats, moments = sb("stats", [T, U, 6]), sb("moments", [T, U, 2])
        root = sb("root", [T, U])
        xn = sb("xn", [T, U, D])
        hn = sb("hn", [T, U, D])
        h_out = sb("h_out", [T, U, D])
        hT = sb("hT", [128, U, DC, T])
        blank = sb("blank", [B, D])
        turn_x = [k.banks[u // 2][:, (u % 2) * 256:(u % 2) * 256 + DC * T] for u in range(U)]
        turn_h = [k.banks[3 + u // 2][:, (u % 2) * 256:(u % 2) * 256 + DC * T] for u in range(U)]
        qk_ps = k.banks[6]
        hist = k.banks[7][0:T, 0:NT]

        with nc.Block() as block:
            @block.sync
            def _(sp):
                def load(to, what, sem):
                    sp.dma_start(to, what).then_inc(sem, 16)
                for dst, edges in ((src_n, d["src"]), (dst_n, d["dst"])):
                    load(dst[:], edges.rearrange("(j q e) -> q j e", q=EQ, e=T), s["edges_in"])
                for p0, p1 in ((0, SPLIT), (SPLIT, T)):
                    load(r.acc[p0:p1], d["x"].rearrange("(i p) d -> p i d", p=T)[p0:p1], s["x_in"])
                load(a.wx[:], d["mix_Wx"].rearrange("(c p) n -> p c n", p=128), s["mix_in"])
                for at, what in ((0, d["mix_bx"]), (2, d["mix_ln1_g"]), (4, d["mix_ln1_b"]), (6, d["mix_ln2_g"]), (8, d["mix_ln2_b"]),
                                 (10, d["mix_b1"]), (18, d["gnn_b_gc"]), (20, d["gnn_b_res"])):
                    pieces = what.rearrange("(c p) -> c p", p=128)
                    load(bias_rows[at:at + pieces.shape[0], :], pieces, s["mix_in"])
                sp.wait_ge(s["blockdiag"], 1)
                for c in range(DC):
                    for q in range(128 // DH):
                        at, head = slice(DH * q, DH * (q + 1)), 4 * c + q
                        load(blockdiag_qk[at, c, KR * head:KR * (head + 1)], d["mix_Wq"], s["mix_in"])
                        load(blockdiag_qk[at, c, HR + KR * head:HR + KR * (head + 1)], d["mix_Wk"], s["mix_in"])
                for q in range(128 // DH):
                    load(a.wv[DH * q:DH * (q + 1), DH * q:DH * (q + 1)], d["mix_Wv"], s["rest_in"])
                for p0, p1 in ((0, SPLIT), (SPLIT, T)):
                    load(a.b2_bc[p0:p1], d["mix_b2"].partition_broadcast(p1 - p0), s["rest_in"])
                    load(a.beta_bc[p0:p1], d["gnn_beta"].partition_broadcast(p1 - p0), s["rest_in"])
                    load(a.bg_bc[p0:p1], d["gnn_bg"].partition_broadcast(p1 - p0), s["rest_in"])
                load(a.g1_bc[:], d["mix_ln1_g"].partition_broadcast(HR), s["rest_in"])
                load(a.b1_bc[:], d["mix_ln1_b"].partition_broadcast(HR), s["rest_in"])
                load(a.bx_row[:], d["mix_bx"].rearrange("(o n) -> o n", o=1), s["rest_in"])
                load(a.m_aug[HR:HR + 1, :], d["mix_bo"].rearrange("(o n) -> o n", o=1), s["rest_in"])
                for to, what in ((a.wo, d["mix_Wo"]), (a.w_gc, d["gnn_W_gc"]), (a.w_res, d["gnn_W_res"]), (a.wg, d["gnn_Wg"])):
                    load(to[:], what.rearrange("(c p) n -> p c n", p=128), s["rest_in"])
                rest = 4 + 6 + 4 + 4
                for layer, used in zip(layers, (2 * CAP // B, 2 * N // B)):
                    rows_out = layer.outputs.rearrange("(m p) d -> p m d", p=B)[:, used:, :]
                    sp.dma_start(rows_out, blank[:].unsqueeze(1).broadcast_to([B, rows_out.shape[1], D])).then_inc(s["blanked"], 16)
                sp.sem_inc(s["h_stored"], 32)
                with sp.Fori(0, NG) as g:
                    sp.wait_ge(s["h_ready"], U * g + U)
                    for p0, p1 in ((0, SPLIT), (SPLIT, T)):
                        sp.dma_start(rows_of(a.h_dram, g)[p0:p1], h_out[p0:p1]).then_inc(s["h_stored"], 16)
                sp.wait_ge(s["h_stored"], 32 * NG + 32)
                sp.wait_ge(s["blanked"], 32)
                sp.wait_ge(s["mix_in"], 16 * (1 + 8 + 4 * 2 * DC))
                sp.wait_ge(s["rest_in"], 16 * rest)
                sp.wait_ge(s["x_in"], 32)
                sp.wait_ge(s["edges_in"], 32)

            @block.gpsimd
            def _(pool):
                nc.gpsimd.memset(blank[:], 0.0)
                nc.gpsimd.memset(blockdiag_qk[:], 0.0)
                nc.gpsimd.memset(a.wv[:], 0.0).then_inc(s["blockdiag"], 1)
                nc.gpsimd.iota(count_lo[:], pattern=[[1, T], [0, HG]], base=0, channel_multiplier=0,
                               allow_small_or_imprecise_dtypes=True)
                nc.gpsimd.iota(count_hi[:], pattern=[[1, NT], [0, HG]], base=0, channel_multiplier=0,
                               allow_small_or_imprecise_dtypes=True).then_inc(s["tables"], 1)
                pool.sem_inc(s["xn_free"], U)
                pool.sem_inc(s["hn_free"], U)
                with pool.Fori(0, NG) as g:
                    for u in range(U):
                        pool.wait_ge(s["xn_ready"], U * g + u + 1)
                        nc.gpsimd.tensor_copy(r.nodes[:, ds(U * g + u, 1), :], xn[:, u:u + 1, :]).then_inc(s["xn_free"], 1)
                    for u in range(U):
                        pool.wait_ge(s["hn_ready"], U * g + u + 1)
                        nc.gpsimd.tensor_copy(a.hn[:, ds(U * g + u, 1), :], hn[:, u:u + 1, :]).then_inc(s["hn_free"], 1)

            @block.vector
            def _(dve):
                steps = [0]

                def then(ins):
                    steps[0] += 1
                    ins.then_inc(s["ids_step"], 1)
                    dve.wait_ge(s["ids_step"], steps[0])

                nc.vector.memset(a.src_idx[:], 0)
                nc.vector.memset(a.visit_tab[:], 0)
                then(nc.vector.memset(a.dst_t[:], -1.0))
                dve.wait_ge(s["edges_in"], 32)
                nc.vector.tensor_copy(src_f[:], src_n[:]).then_inc(s["edges_float"], 1)
                nc.vector.tensor_copy(dst_f[:], dst_n[:]).then_inc(s["edges_float"], 1)
                dve.wait_ge(s["edge_columns"], 2)
                nc.vector.tensor_copy(a.src_idx[:, 0:EC], k.banks[0][0:T, 0:EC])
                nc.vector.tensor_copy(src_t[:], k.banks[0][0:T, 0:EC])
                then(nc.vector.tensor_copy(a.dst_t[:, 0:EC], k.banks[1][0:T, 0:EC]))
                for ins in round_to_whole(nc, src_hi[:], src_t[:], 1.0 / T, -(T // 2) / T):
                    then(ins())
                nc.vector.tensor_copy(hi_b[:], src_hi[:])
                nc.vector.scalar_tensor_tensor(lo_b[:], src_hi[:], -float(T), src_t[:], ALU.mult, ALU.add).then_inc(s["ids"], 1)
                dve.wait_ge(s["ids"], 1)
                dve.wait_ge(s["tables"], 1)
                with dve.Fori(0, EC // HG // 2) as i:
                    for v in range(2):
                        at = ds((2 * i + v) * HG, HG)
                        dve.wait_ge(s["hist_free"], 2 * i + v + 1)
                        nc.vector.tensor_tensor(hot_lo[v][:], count_lo[:], lo_b[:, at].unsqueeze(1).broadcast_to([T, T, HG]), ALU.is_equal)
                        nc.vector.tensor_tensor(hot_hi[v][:], count_hi[:], hi_b[:, at].unsqueeze(1).broadcast_to([T, NT, HG]),
                                                ALU.is_equal).then_inc(s["hist_ready"], 1)
                dve.wait_ge(s["hist_free"], EC // HG + 2 + 1)
                nc.vector.tensor_scalar(degree[:], hist, 1.0, None, ALU.max).then_inc(s["degree"], 1)
                dve.wait_ge(s["degree_root"], 1)
                then(nc.vector.reciprocal(a.rs_out[:], degree[:]))
                nc.vector.tensor_reduce(reach[:, 0, :], dst_f[:], AX, ALU.min)
                then(nc.vector.tensor_reduce(reach[:, 1, :], dst_f[:], AX, ALU.max))
                for ins in round_to_whole(nc, reach[:], reach[:], 1.0 / T, -(T // 2) / T):
                    then(ins())
                nc.vector.tensor_copy(visit[:, 7:8], r.col[0:NT, :]).then_inc(s["chunk_range"], 1)
                dve.wait_ge(s["range_bc"], 1)
                block_no = r.col[0:NT, :]
                nc.vector.tensor_scalar(lo_c[:], k.banks[2][0:NT, 0:EC], block_no, None, ALU.is_le)
                then(nc.vector.tensor_scalar(hi_c[:], k.banks[3][0:NT, 0:EC], block_no, None, ALU.is_ge))
                then(nc.vector.tensor_tensor(lo_c[:], lo_c[:], hi_c[:], ALU.mult))
                then(nc.vector.scalar_tensor_tensor(hi_c[:], r.row[0:NT, 0:EC], -float(EC), lo_c[:], ALU.add, ALU.mult))
                then(nc.vector.tensor_reduce(visit[:, 0:1], hi_c[:], AX, ALU.min))
                then(nc.vector.tensor_scalar(visit[:, 0:1], visit[:, 0:1], float(EC), float(EC - 1), ALU.add, ALU.min))
                then(nc.vector.scalar_tensor_tensor(hi_c[:], r.row[0:NT, 0:EC], 1.0, lo_c[:], ALU.add, ALU.mult))
                then(nc.vector.tensor_reduce(visit[:, 1:2], hi_c[:], AX, ALU.max))
                then(nc.vector.tensor_tensor(visit[:, 1:2], visit[:, 1:2], visit[:, 0:1], ALU.subtract))
                then(nc.vector.tensor_scalar(visit[:, 1:2], visit[:, 1:2], 1.0, None, ALU.max))
                for ins in round_to_whole(nc, visit[:, 2:3], visit[:, 1:2], 1.0 / VU, (VU - 1) / (2.0 * VU)):
                    then(ins())
                nc.vector.tensor_copy(visit[:, 3:4], visit[:, 2:3]).then_inc(s["visit_step"], 1)
                dve.wait_ge(s["visit_row"], 1)
                nc.vector.tensor_copy(visit[:, 4:5], k.banks[4][0:NT, 0:1]).then_inc(s["visit_step"], 1)
                dve.wait_ge(s["visit_row"], 2)
                nc.vector.tensor_copy(a.visit_tab[0:1, 0, 0:NT], k.banks[5][0:1, 0:NT])
                nc.vector.tensor_copy(a.visit_tab[0:1, 1, 0:NT], k.banks[5][0:1, NT:2 * NT])
                nc.vector.tensor_copy(a.visit_tab[0:1, 2, 0:NT], k.banks[5][0:1, 2 * NT:3 * NT])
                dve.wait_ge(s["wx_turned"], 1)
                nc.vector.tensor_copy(a.cols[:], k.banks[0][:, 0:22])
                nc.vector.tensor_copy(wx_t[:], k.banks[6][:, 0:DC * D].rearrange("p (c n) -> p c n", c=DC)).then_inc(s["wx_copied"], 1)
                dve.wait_ge(s["folded"], 1)
                nc.vector.tensor_copy(wqk[:], k.banks[1][:, 0:DC * 2 * HR].rearrange("p (c n) -> p c n", c=DC))
                nc.vector.tensor_copy(bqk[:], k.banks[1][0:T, 256:256 + 2 * HR]).then_inc(s["qk_weights"], 1)
                dve.wait_ge(s["qk_weights"], 1)
                dve.wait_ge(s["x_in"], 32)

                def norm(g, tile, stats_sem, moments_sem, root_sem, inverse_sem):
                    for u in range(U):
                        nc.vector.bn_stats(stats[:, u, :], tile(u)).then_inc(stats_sem, 1)
                    dve.wait_ge(stats_sem, U * g + U)
                    dve.sem_inc(s["passed"], 1)
                    for u in range(U):
                        nc.vector.bn_aggr(moments[:, u, :], stats[:, u, :]).then_inc(moments_sem, 1)
                    dve.wait_ge(root_sem, g + 1)
                    nc.vector.reciprocal(root[:], root[:]).then_inc(inverse_sem, 1)
                    dve.wait_ge(inverse_sem, g + 1)

                def first_norm(g):
                    norm(g, lambda u: r.acc[:, ds(U * g + u, 1), :].rearrange("p o d -> p (o d)"), s["stats1"], s["moments1"], s["root1"], s["inverse1"])
                    dve.wait_ge(s["hnT_turned"], U * g + 1)
                    for u in range(U):
                        dve.wait_ge(s["xn_free"], U * g + u + 1)
                        nc.vector.tensor_scalar(xn[:, u:u + 1, :], r.acc[:, ds(U * g + u, 1), :], moments[:, u, 0:1], root[:, u:u + 1],
                                                ALU.subtract, ALU.mult).then_inc(s["xn_ready"], 1)

                def second_norm(g):
                    dve.wait_ge(s["xn_ready"], U * g + U)
                    norm(g, lambda u: xn[:, u, :], s["stats2"], s["moments2"], s["root2"], s["inverse2"])
                    for u in range(U):
                        dve.wait_ge(s["hn_free"], U * g + u + 1)
                        nc.vector.tensor_scalar(hn[:, u, :], xn[:, u, :], moments[:, u, 0:1], root[:, u:u + 1],
                                                ALU.subtract, ALU.mult).then_inc(s["hn_ready"], 1)

                def keep_turned(g):
                    dve.wait_ge(s["xnT_turned"], U * g + U)
                    for u in range(U):
                        nc.vector.tensor_copy(a.xnT[:, :, ds((U * g + u) * T, T)],
                                              turn_x[u].rearrange("p (c t) -> p c t", c=DC)).then_inc(s["xnT_kept"], 1)
                    dve.wait_ge(s["qk_ready"], U * g + U)
                    nc.vector.tensor_tensor(a.qk[:, ds(U * g, U), :], qk_ps[0:T, 0:U * 2 * HR].rearrange("p (u n) -> p u n", u=U),
                                            bqk[:].unsqueeze(1).broadcast_to([T, U, 2 * HR]), ALU.add).then_inc(s["qk_kept"], 1)

                first_norm(0)
                second_norm(0)
                with dve.Fori(1, NG) as g:
                    first_norm(g)
                    keep_turned(g - 1)
                    second_norm(g)
                keep_turned(NG - 1)

            @block.scalar
            def _(act):
                act.wait_ge(s["degree"], 1)
                nc.scalar.activation(degree[:], degree[:], ACT.Sqrt).then_inc(s["degree_root"], 1)
                act.sem_inc(s["hT_free"], 1)
                with act.Fori(0, NG) as g:
                    act.wait_ge(s["moments1"], U * g + U)
                    nc.scalar.activation(root[:], moments[:, :, 1], ACT.Sqrt, bias=r.eps[0:T, :]).then_inc(s["root1"], 1)
                    act.wait_ge(s["h_stored"], 32 * g + 32)
                    for u in range(U):
                        act.wait_ge(s["xn_ready"], U * g + u + 1)
                        nc.scalar.activation(h_out[:, u, :], xn[:, u, :], ACT.Copy,
                                             scale=a.rs_out[:, ds(U * g + u, 1)]).then_inc(s["h_ready"], 1)
                    act.wait_ge(s["moments2"], U * g + U)
                    nc.scalar.activation(root[:], moments[:, :, 1], ACT.Sqrt, bias=r.eps[0:T, :]).then_inc(s["root2"], 1)
                    act.wait_ge(s["hnT_turned"], U * g + U + 1)
                    for u in range(U):
                        for c in range(DC):
                            done = nc.scalar.activation(hT[:, u, c, :], turn_h[u][:, c * T:(c + 1) * T], ACT.Identity,
                                                        scale=a.cols[:, 2 + c:3 + c], bias=a.cols[:, 4 + c:5 + c])
                        done.then_inc(s["hT_ready"], 1)

            @block.tensor
            def _(pe):
                for n, (edges, bank) in enumerate(((src_f, k.banks[0]), (dst_f, k.banks[1]))):
                    pe.wait_ge(s["edges_float"], n + 1)
                    for j in range(EJ):
                        done = nc.tensor.transpose(bank[0:T, j * EQ:(j + 1) * EQ], edges[:, j, :], r.ident[0:EQ, 0:EQ])
                    done.then_inc(s["edge_columns"], 1)
                pe.sem_inc(s["hist_free"], 2)
                nc.tensor.matmul(hist, r.zeros[0:T, 0:T], r.zeros[0:T, 0:NT], start=True, stop=False)
                with pe.Fori(0, EC // HG // 2) as i:
                    for v in range(2):
                        pe.wait_ge(s["hist_ready"], 2 * i + v + 1)
                        for j in range(HG):
                            done = nc.tensor.matmul(hist, hot_lo[v][:, :, j], hot_hi[v][:, :, j], start=False, stop=False)
                        done.then_inc(s["hist_free"], 1)
                nc.tensor.matmul(hist, r.zeros[0:T, 0:T], r.zeros[0:T, 0:NT], start=False, stop=True).then_inc(s["hist_free"], 1)
                pe.wait_ge(s["chunk_range"], 1)
                for way in range(2):
                    for j in range(EJ):
                        done = nc.tensor.matmul(k.banks[2 + way][0:NT, j * EQ:(j + 1) * EQ],
                                                reach[:, way, j:j + 1].broadcast_to([EQ, NT]), r.ident[0:EQ, 0:EQ], start=True, stop=True)
                done.then_inc(s["range_bc"], 1)
                pe.wait_ge(s["visit_step"], 1)
                nc.tensor.matmul(k.banks[4][0:NT, 0:1], r.tril_f[0:NT, 0:NT], visit[:, 2:3], start=True, stop=True).then_inc(s["visit_row"], 1)
                pe.wait_ge(s["visit_step"], 2)
                for n, what in enumerate((visit[:, 4:5], visit[:, 0:1], visit[:, 2:3])):
                    done = nc.tensor.matmul(k.banks[5][0:1, n * NT:(n + 1) * NT], what, r.ident[0:NT, 0:NT], start=True, stop=True)
                done.then_inc(s["visit_row"], 1)
                pe.wait_ge(s["mix_in"], 16 * (1 + 8 + 4 * 2 * DC))
                nc.tensor.transpose(k.banks[0][:, 0:22], bias_rows[:], r.ident[0:22, 0:22])
                for n in range(DC):
                    for c in range(DC):
                        done = nc.tensor.transpose(k.banks[6][:, n * D + c * 128:n * D + (c + 1) * 128], a.wx[:, c, n * 128:(n + 1) * 128], r.ident[:])
                done.then_inc(s["wx_turned"], 1)
                pe.wait_ge(s["wx_copied"], 1)
                for c in range(DC):
                    for n in range(DC):
                        nc.tensor.matmul(k.banks[1][:, c * 64:(c + 1) * 64], wx_t[:, n, c * 128:(c + 1) * 128], blockdiag_qk[:, n, :],
                                         start=n == 0, stop=n == DC - 1)
                for n in range(DC):
                    done = nc.tensor.matmul(k.banks[1][0:T, 256:256 + 2 * HR], a.cols[:, n:n + 1].broadcast_to([128, T]), blockdiag_qk[:, n, :],
                                            start=n == 0, stop=n == DC - 1)
                done.then_inc(s["folded"], 1)
                pe.wait_ge(s["qk_weights"], 1)
                pe.sem_inc(s["xnT_kept"], U)
                pe.sem_inc(s["qk_kept"], 1)
                pe.sem_inc(s["hnT_turned"], 1)
                with pe.Fori(0, NG) as g:
                    pe.wait_ge(s["xnT_kept"], U * g + U)
                    pe.sem_inc(s["passed"], 1)
                    for u in range(U):
                        pe.wait_ge(s["xn_ready"], U * g + u + 1)
                        for c in range(DC):
                            done = nc.tensor.transpose(turn_x[u][:, c * T:(c + 1) * T], xn[:, u, c * 128:(c + 1) * 128], r.ident[0:T, 0:T])
                        done.then_inc(s["xnT_turned"], 1)
                    for u in range(U):
                        pe.wait_ge(s["hn_ready"], U * g + u + 1)
                        for c in range(DC):
                            done = nc.tensor.transpose(turn_h[u][:, c * T:(c + 1) * T], hn[:, u, c * 128:(c + 1) * 128], r.ident[0:T, 0:T])
                        done.then_inc(s["hnT_turned"], 1)
                    pe.wait_ge(s["qk_kept"], g + 1)
                    pe.sem_inc(s["passed"], 1)
                    for u in range(U):
                        pe.wait_ge(s["hT_ready"], U * g + u + 1)
                        for c in range(DC):
                            done = nc.tensor.matmul(qk_ps[0:T, 64 * u:64 * u + 64], hT[:, u, c, :], wqk[:, c, :], start=c == 0, stop=c == DC - 1)
                        done.then_inc(s["qk_ready"], 1)


def attention_state(nc, d, r, a):
    names = ("step act_step pe_step staged staged_free summed bias_added weights_in")
    with phase(nc, "state", names) as k:
        s, sb = k.s, k.sb
        q_max, q_sum = sb("q_max", [T, NT, HEADS]), sb("q_sum", [T, NT, HEADS])
        k_max, k_sum = sb("k_max", [T, HR]), sb("k_sum", [T, HR])
        k_top = sb("k_top", [HR, 1])
        k_max_bc = sb("k_max_bc", [T, HR])
        ek = [sb(f"ek{v}", [T, U, HR]) for v in range(1)]
        sum_col, inv_col, sum_row = sb("sum_col", [HR, 1]), sb("inv_col", [HR, 1]), sb("sum_row", [1, HR])
        gt = sb("gt", [HR, D])
        gh, xm, kv = (sb(n, [128, DC, HR]) for n in ("gh", "xm", "kv"))
        own = sb("own", [128, DC, HR])
        state = k.banks[0][0:HR, 0:D]
        q_part = a.qk[:, :, 0:HR].rearrange("p i (h r) -> p i h r", h=HEADS)
        k_part = a.qk[:, :, HR:2 * HR]
        by_head = lambda t: t[:].unsqueeze(3).broadcast_to([T, NT, HEADS, KR])

        with nc.Block() as block:
            @block.sync
            def _(sp):
                for to, what in ((a.w1, d["mix_W1"]), (a.w2, d["mix_W2"])):
                    sp.dma_start(to[:], what.rearrange("(c p) n -> p c n", p=128)).then_inc(s["weights_in"], 16)
                sp.wait_ge(s["weights_in"], 32)

            @block.gpsimd
            def _(pool):
                nc.gpsimd.tensor_tensor(a.b2_bc[:], a.b2_bc[:], a.beta_bc[:], ALU.add).then_inc(s["bias_added"], 1)
                pool.wait_ge(s["bias_added"], 1)
                nc.gpsimd.tensor_tensor(r.acc[:], r.acc[:], a.b2_bc[:].unsqueeze(1).broadcast_to([T, NT, D]), ALU.add).then_inc(s["bias_added"], 1)

            @block.vector
            def _(dve):
                steps = [0]

                def then(ins):
                    steps[0] += 1
                    ins.then_inc(s["step"], 1)
                    dve.wait_ge(s["step"], steps[0])

                nc.vector.tensor_reduce(q_max[:], q_part, AX, ALU.max)
                then(nc.vector.tensor_reduce(k_max[:], k_part.rearrange("p i n -> p n i"), AX, ALU.max))
                nc.vector.tensor_tensor(q_part, q_part, by_head(q_max), ALU.subtract)
                dve.wait_ge(s["pe_step"], 1)
                then(nc.vector.tensor_reduce(k_top[:], k.banks[1][0:HR, 0:T], AX, ALU.max))
                dve.wait_ge(s["pe_step"], 2)
                then(nc.vector.tensor_copy(k_max_bc[:], k.banks[2][0:T, 0:HR]))
                then(nc.vector.tensor_tensor(k_part, k_part, k_max_bc[:].unsqueeze(1).broadcast_to([T, NT, HR]), ALU.subtract))
                nc.vector.memset(own[:], 0.0)
                dve.wait_ge(s["act_step"], 1)
                then(nc.vector.tensor_reduce(k_sum[:], k_part.rearrange("p i n -> p n i"), AX, ALU.add))
                with dve.Fori(0, NG) as g:
                    dve.wait_ge(s["staged_free"], g + 1)
                    nc.vector.tensor_copy(ek[0][:], a.qk[:, ds(U * g, U), HR:2 * HR]).then_inc(s["staged"], 1)
                then(nc.vector.tensor_reduce(q_sum[:], q_part, AX, ALU.add))
                then(nc.vector.reciprocal(q_sum[:], q_sum[:]))
                for c in range(DC):
                    for q in range(128 // DH):
                        head = 4 * c + q
                        nc.vector.memset(own[DH * q:DH * (q + 1), c, KR * head:KR * (head + 1)], 1.0)
                then(nc.vector.tensor_tensor(q_part, q_part, by_head(q_sum), ALU.mult))
                dve.wait_ge(s["summed"], 1)
                nc.vector.tensor_copy(sum_col[:], k.banks[1][0:HR, 128:129])
                nc.vector.tensor_copy(sum_row[:], k.banks[1][0:1, 256:256 + HR])
                then(nc.vector.tensor_tensor(gt[:], state, a.g1_bc[:], ALU.mult))
                nc.vector.reciprocal(inv_col[:], sum_col[:])
                then(nc.vector.scalar_tensor_tensor(gt[:], a.b1_bc[:], sum_col[:], gt[:], ALU.mult, ALU.add))
                for n, to in ((3, gh), (4, xm)):
                    dve.wait_ge(s["pe_step"], n)
                    then(nc.vector.tensor_copy(to[:], k.banks[n][:, 0:DC * HR].rearrange("p (c n) -> p c n", c=DC)))
                dve.wait_ge(s["pe_step"], 5)
                then(nc.vector.tensor_tensor(kv[:], k.banks[5][:, 0:DC * HR].rearrange("p (c n) -> p c n", c=DC), own[:], ALU.mult))
                dve.wait_ge(s["pe_step"], 6)
                then(nc.vector.tensor_scalar(a.m_aug[0:HR, :], k.banks[6][0:HR, 0:D], inv_col[:], None, ALU.mult))

            @block.scalar
            def _(act):
                act.wait_ge(s["step"], 4)
                nc.scalar.activation(a.qk[:], a.qk[:], ACT.Exp).then_inc(s["act_step"], 1)

            @block.tensor
            def _(pe):
                pe.wait_ge(s["step"], 1)
                nc.tensor.transpose(k.banks[1][0:HR, 0:T], k_max[:], r.ident[0:T, 0:T]).then_inc(s["pe_step"], 1)
                pe.wait_ge(s["step"], 2)
                nc.tensor.matmul(k.banks[2][0:T, 0:HR], k_top[:].broadcast_to([HR, T]), r.ident[0:HR, 0:HR],
                                 start=True, stop=True).then_inc(s["pe_step"], 1)
                pe.sem_inc(s["staged_free"], 1)
                nc.tensor.matmul(state, r.zeros[0:T, 0:HR], r.zeros[0:T, 0:D], start=True, stop=False)
                with pe.Fori(0, NG) as g:
                    pe.wait_ge(s["staged"], g + 1)
                    for u in range(U):
                        done = nc.tensor.matmul(state, ek[0][:, u, :], a.hn[:, ds(U * g + u, 1), :].rearrange("p o d -> p (o d)"), start=False, stop=False)
                    done.then_inc(s["staged_free"], 1)
                nc.tensor.matmul(state, r.zeros[0:T, 0:HR], r.zeros[0:T, 0:D], start=False, stop=True)
                nc.tensor.matmul(k.banks[1][0:HR, 128:129], k_sum[:], r.ones[:, 0:1], start=True, stop=True)
                nc.tensor.matmul(k.banks[1][0:1, 256:256 + HR], r.ones[:, 0:1], k_sum[:], start=True, stop=True).then_inc(s["summed"], 1)
                pe.wait_ge(s["step"], 10)
                for c in range(DC):
                    done = nc.tensor.transpose(k.banks[3][:, c * HR:(c + 1) * HR], gt[:, c * 128:(c + 1) * 128], r.ident[0:HR, 0:HR])
                done.then_inc(s["pe_step"], 1)
                pe.wait_ge(s["step"], 11)
                for n in range(DC):
                    out = k.banks[4][:, n * HR:(n + 1) * HR]
                    for c in range(DC):
                        nc.tensor.matmul(out, a.wx[:, c, n * 128:(n + 1) * 128], gh[:, c, :], start=c == 0, stop=False)
                    done = nc.tensor.matmul(out, a.bx_row[0:1, n * 128:(n + 1) * 128], sum_row[0:1, :], start=False, stop=True)
                done.then_inc(s["pe_step"], 1)
                pe.wait_ge(s["step"], 12)
                for n in range(DC):
                    done = nc.tensor.matmul(k.banks[5][:, n * HR:(n + 1) * HR], a.wv[:], xm[:, n, :], start=True, stop=True)
                done.then_inc(s["pe_step"], 1)
                pe.wait_ge(s["step"], 13)
                for n in range(DC):
                    done = nc.tensor.matmul(k.banks[6][0:HR, 0:D], kv[:, n, :], a.wo[:, n, :], start=n == 0, stop=n == DC - 1)
                done.then_inc(s["pe_step"], 1)


def by_set(eng, step, body):
    odd, high = eng.snap(step & 1), eng.snap(step & 2)
    with eng.If(high == 0):
        with eng.If(odd == 0):
            body(0)
        with eng.Else():
            body(1)
    with eng.Else():
        with eng.If(odd == 0):
            body(2)
        with eng.Else():
            body(3)


def chunk_at(first, step):
    return (first + VU * step).with_bounds(min_val=0, max_val=EC - 1)


def graph_and_mix(nc, d, r, a, q, p):
    names = ("idx_ready passed visited hot_ready bias_summed"
             " ones_in sums_ready inv_degree deg_clipped deg_root mean_ready meanT_ready meanT_kept xgT_ready xgT_kept"
             " xg_kept xg_stored logits_ready logits_kept"
             " q_staged qT_ready qT_kept attn_ready fx_ready fx_stats fx_moments fx_root fx_inverse h2_ready h2T_ready h2T_kept"
             " up_ready hidden_ready down_ready down_added") + "".join(f" row_in{n}" for n in range(SETS * VU))
    with phase(nc, "graph", names) as k:
        s, sb = k.s, k.sb
        gathered = [s[f"row_in{n}"] for n in range(SETS * VU)]
        spare = a.hn[:].rearrange("p i d -> p (i d)")
        rows_at = SETS * VU * (D + 2)
        rows = spare[:, 0:rows_at].rearrange("p (n d) -> p n d", n=SETS * VU)
        hot = [spare[:, rows_at + n * VU * T:rows_at + (n + 1) * VU * T].rearrange("p (u t) -> p u t", u=VU) for n in range(SETS)]
        idx = [sb(f"idx{n}", [T, VU], I32) for n in range(SETS)]
        base = sb("base", [T, NT])
        bias_gc = sb("bias_gc", [128, DC])
        inv_deg = sb("inv_deg", [T, 1])
        deg_root = sb("deg_root", [T, 1])
        mean = sb("mean", [T, D])
        meanT = sb("meanT", [128, DC, T])
        xgT = sb("xgT", [128, DC, T])
        qs = sb("qs", [T, U, HR + 1])
        qT = sb("qT", [HR + 1, U, T])
        fx = sb("fx", [T, U, D])
        h2T = sb("h2T", [128, DC, U * T])
        hidden_all = sb("hidden", [128, FC * U * T])
        hidden = hidden_all[:].rearrange("p (m t) -> p m t", m=FC)
        h2 = hidden_all[0:T, 0:U * D].rearrange("p (u d) -> p u d", u=U)
        stats, moments, root = sb("stats", [T, U, 6]), sb("moments", [T, U, 2]), sb("root", [T, U])
        sums = [k.banks[n][0:T, 0:D + 2] for n in range(2)]
        meanT_ps, xg_ps = k.banks[2][:, 0:DC * T], k.banks[2][0:T, 0:D]
        xgT_ps, logit_ps = k.banks[2][:, 256:256 + DC * T], k.banks[2][0:T, 256:256 + E_GNN]
        slot = [k.banks[5 + u // 2][:, (u % 2) * 256:(u % 2) * 256 + 256] for u in range(U)]
        wide = [k.wide[0][:], k.wide[1][:]]
        turn_q = [k.banks[3][0:HR + 1, u * T:(u + 1) * T] for u in range(4)] + [k.banks[4][0:HR + 1, 0:T]]
        tile3 = lambda t, i: t[:, ds(i, 1), :].rearrange("p o d -> p (o d)")

        with nc.Block() as block:
            @block.sync
            def _(sp):
                sp.sem_inc(s["xg_stored"], 32)
                with sp.Fori(0, NG) as g:
                    sp.wait_ge(s["xg_kept"], U * g + U)
                    for p0, p1 in ((0, SPLIT), (SPLIT, T)):
                        sp.dma_start(rows_of(q.tokens, g)[p0:p1], r.nodes[p0:p1, ds(U * g, U), :]).then_inc(s["xg_stored"], 16)
                sp.wait_ge(s["xg_stored"], 32 * NG + 32)

            @block.gpsimd
            def _(pool):
                pool.wait_ge(s["ones_in"], 1)
                with pool.Fori(0, NT) as b:
                    before = pool.value_load(a.visit_tab[0:1, 0, ds(b, 1)], min_val=0, max_val=NT * EC)
                    first = pool.value_load(a.visit_tab[0:1, 1, ds(b, 1)], min_val=0, max_val=EC - 1)
                    steps = pool.value_load(a.visit_tab[0:1, 2, ds(b, 1)], min_val=1, max_val=EC // VU)
                    with pool.Fori(0, steps) as j:
                        v = pool.snap(before + j)
                        pool.wait_ge(s["visited"], v + 1)
                        pool.sem_inc(s["passed"], 1)

                        def fetch(n):
                            nc.gpsimd.tensor_copy(idx[n][:], a.src_idx[:, ds(chunk_at(first, j), VU)]).then_inc(s["idx_ready"], 1)
                            pool.wait_ge(s["idx_ready"], v + 1)
                            pool.sem_inc(s["passed"], 1)
                            for u in range(VU):
                                nc.gpsimd.indirect_dma_start(
                                    out=rows[:, VU * n + u, 0:D], out_offset=None, in_=a.h_dram[:, :],
                                    in_offset=bass.IndirectOffsetOnAxis(ap=idx[n][:, u:u + 1], axis=0)).then_inc(gathered[VU * n + u], 16)
                        by_set(pool, v, fetch)

            @block.vector
            def _(dve):
                nc.vector.memset(rows, 1.0).then_inc(s["ones_in"], 1)
                nc.vector.memset(qs[:], 1.0)
                nc.vector.tensor_scalar(base[:], r.row[0:T, 0:NT], float(T), None, ALU.mult)
                nc.vector.tensor_tensor(bias_gc[:], a.cols[:, 18:20], a.cols[:, 20:22], ALU.add).then_inc(s["ones_in"], 1)
                dve.wait_ge(s["ones_in"], 2)
                dve.sem_inc(s["bias_summed"], 1)

                def hot_of_block(g, u):
                    b = U * g + u
                    before = dve.value_load(a.visit_tab[0:1, 0, ds(b, 1)], min_val=0, max_val=NT * EC)
                    first = dve.value_load(a.visit_tab[0:1, 1, ds(b, 1)], min_val=0, max_val=EC - 1)
                    steps = dve.value_load(a.visit_tab[0:1, 2, ds(b, 1)], min_val=1, max_val=EC // VU)
                    with dve.Fori(0, steps) as j:
                        v = dve.snap(before + j)
                        dve.wait_ge(s["visited"], v + 1)

                        def mark(n):
                            nc.vector.scalar_tensor_tensor(
                                hot[n], r.row[0:T, 0:T].unsqueeze(1).broadcast_to([T, VU, T]), base[:, ds(b, 1)],
                                a.dst_t[:, ds(chunk_at(first, j), VU)].unsqueeze(2).broadcast_to([T, VU, T]),
                                ALU.add, ALU.is_equal).then_inc(s["hot_ready"], 1)
                        by_set(dve, v, mark)

                def mean_of_block(g, u):
                    i = U * g + u
                    dve.wait_ge(s["sums_ready"], i + 1)
                    nc.vector.tensor_scalar(inv_deg[:], sums[u % 2][:, D:D + 1], 1.0, None, ALU.max).then_inc(s["deg_clipped"], 1)
                    dve.wait_ge(s["deg_root"], i + 1)
                    nc.vector.reciprocal(inv_deg[:], deg_root[:]).then_inc(s["inv_degree"], 1)
                    dve.wait_ge(s["inv_degree"], i + 1)
                    nc.vector.tensor_scalar(mean[:], sums[u % 2][:, 0:D], inv_deg[:], None, ALU.mult).then_inc(s["mean_ready"], 1)

                def turned_mean_of_block(g, u):
                    i = U * g + u
                    dve.wait_ge(s["meanT_ready"], i + 1)
                    nc.vector.tensor_copy(meanT[:].rearrange("p c t -> p (c t)"), meanT_ps).then_inc(s["meanT_kept"], 1)

                def tokens_of_block(g, u):
                    i = U * g + u
                    dve.wait_ge(s["logits_ready"], i + 1)
                    dve.sem_inc(s["passed"], 1)
                    nc.vector.tensor_copy(tile3(r.nodes, i), xg_ps).then_inc(s["xg_kept"], 1)
                    nc.vector.tensor_tensor(tile3(q.logits, i), logit_ps, a.bg_bc[:], ALU.add).then_inc(s["logits_kept"], 1)

                def stage_q(g):
                    for u in range(U):
                        nc.vector.tensor_copy(qs[:, u, 0:HR], a.qk[:, ds(U * g + u, 1), 0:HR].rearrange("p o n -> p (o n)")).then_inc(s["q_staged"], 1)

                def first_block(g):
                    dve.wait_ge(s["qT_ready"], U * g + U)
                    for u in range(U):
                        nc.vector.tensor_copy(qT[:, u, :], turn_q[u]).then_inc(s["qT_kept"], 1)
                    hot_of_block(g, 0)

                def other_blocks(g, following):
                    hot_of_block(g, 1)
                    mean_of_block(g, 0)
                    dve.wait_ge(s["attn_ready"], U * g + U)
                    for u in range(U):
                        i = U * g + u
                        nc.vector.tensor_tensor(fx[:, u, :], slot[u][0:T, :], tile3(r.nodes, i), ALU.add).then_inc(s["fx_ready"], 1)
                    dve.wait_ge(s["fx_ready"], U * g + U)
                    dve.sem_inc(s["passed"], 1)
                    for u in range(U):
                        nc.vector.bn_stats(stats[:, u, :], fx[:, u, :]).then_inc(s["fx_stats"], 1)
                    dve.wait_ge(s["fx_stats"], U * g + U)
                    dve.sem_inc(s["passed"], 1)
                    for u in range(U):
                        nc.vector.bn_aggr(moments[:, u, :], stats[:, u, :]).then_inc(s["fx_moments"], 1)
                    dve.wait_ge(s["fx_root"], g + 1)
                    nc.vector.reciprocal(root[:], root[:]).then_inc(s["fx_inverse"], 1)
                    dve.wait_ge(s["fx_inverse"], g + 1)
                    for u in range(U):
                        nc.vector.tensor_scalar(h2[:, u, :], fx[:, u, :], moments[:, u, 0:1], root[:, u:u + 1],
                                                ALU.subtract, ALU.mult).then_inc(s["h2_ready"], 1)
                    turned_mean_of_block(g, 0)
                    for u in range(2, U):
                        hot_of_block(g, u)
                        tokens_of_block(g, u - 2)
                        mean_of_block(g, u - 1)
                        turned_mean_of_block(g, u - 1)
                    if following is not None:
                        stage_q(following)
                    tokens_of_block(g, U - 2)
                    mean_of_block(g, U - 1)
                    turned_mean_of_block(g, U - 1)
                    tokens_of_block(g, U - 1)
                    if following is not None:
                        first_block(following)
                    dve.wait_ge(s["down_ready"], U * g + U)
                    for u in range(U):
                        i = U * g + u
                        nc.vector.tensor_tensor(fx[:, u, :], slot[u][0:T, :], fx[:, u, :], ALU.add).then_inc(s["down_added"], 1)
                    for u in range(U):
                        i = U * g + u
                        dve.wait_ge(s["down_added"], i + 1)
                        done = nc.vector.tensor_tensor(tile3(r.acc, i), tile3(r.acc, i), fx[:, u, :], ALU.add)
                    done.then_inc(s["bias_summed"], 1)

                stage_q(0)
                first_block(0)
                with dve.Fori(0, NG - 1) as g:
                    other_blocks(g, g + 1)
                other_blocks(NG - 1, None)

            @block.scalar
            def _(act):
                with act.Fori(0, NG) as g:
                    def degree_root(u):
                        act.wait_ge(s["deg_clipped"], U * g + u + 1)
                        nc.scalar.activation(deg_root[:], inv_deg[:], ACT.Sqrt).then_inc(s["deg_root"], 1)

                    def tokens_of_block(u):
                        act.wait_ge(s["xgT_ready"], U * g + u + 1)
                        for c in range(DC):
                            done = nc.scalar.activation(xgT[:, c, :], xgT_ps[:, c * T:(c + 1) * T], ACT.Identity, bias=bias_gc[:, c:c + 1])
                        done.then_inc(s["xgT_kept"], 1)

                    def hidden_chunks(chunks):
                        for m in chunks:
                            act.wait_ge(s["up_ready"], FC * g + m + 1)
                            nc.scalar.activation(hidden[:, m, :], wide[m % 2][:, 0:U * T], ACT.Gelu,
                                                 bias=a.cols[:, 10 + m:11 + m]).then_inc(s["hidden_ready"], 1)

                    degree_root(0)
                    act.wait_ge(s["fx_moments"], U * g + U)
                    nc.scalar.activation(root[:], moments[:, :, 1], ACT.Sqrt, bias=r.eps[0:T, :]).then_inc(s["fx_root"], 1)
                    act.wait_ge(s["h2T_ready"], U * g + U)
                    for w in range(U):
                        for c in range(DC):
                            done = nc.scalar.activation(h2T[:, c, w * T:(w + 1) * T], slot[w][:, c * T:(c + 1) * T],
                                                        ACT.Identity, scale=a.cols[:, 6 + c:7 + c], bias=a.cols[:, 8 + c:9 + c])
                        done.then_inc(s["h2T_kept"], 1)
                    tokens_of_block(0)
                    for u in (1, 2):
                        degree_root(u)
                        hidden_chunks(range(4 * u - 4, 4 * u - 2))
                        tokens_of_block(u)
                        hidden_chunks(range(4 * u - 2, 4 * u))
                    for u in (3, 4):
                        degree_root(u)
                        tokens_of_block(u)

            @block.tensor
            def _(pe):
                pe.wait_ge(s["ones_in"], 2)
                pe.sem_inc(s["visited"], SETS)
                def visit_block(g, u):
                    b = U * g + u
                    before = pe.value_load(a.visit_tab[0:1, 0, ds(b, 1)], min_val=0, max_val=NT * EC)
                    steps = pe.value_load(a.visit_tab[0:1, 2, ds(b, 1)], min_val=1, max_val=EC // VU)
                    pe.wait_ge(s["hot_ready"], before + 1)
                    nc.tensor.matmul(sums[u % 2], r.zeros[0:T, 0:T], r.zeros[0:T, 0:D + 2], start=True, stop=False)
                    with pe.Fori(0, steps) as j:
                        v = pe.snap(before + j)
                        pe.wait_ge(s["hot_ready"], v + 1)

                        def add(n):
                            for c in range(VU):
                                pe.wait_ge(gathered[VU * n + c], ((v >> 2) + 1) * 16)
                                done = nc.tensor.matmul(sums[u % 2], hot[n][:, c, :], rows[:, VU * n + c, :], start=False, stop=False)
                            done.then_inc(s["visited"], 1)
                        by_set(pe, v, add)
                    nc.tensor.matmul(sums[u % 2], r.zeros[0:T, 0:T], r.zeros[0:T, 0:D + 2], start=False, stop=True).then_inc(s["sums_ready"], 1)

                def turn_mean(g, u):
                    pe.wait_ge(s["mean_ready"], U * g + u + 1)
                    for c in range(DC):
                        done = nc.tensor.transpose(meanT_ps[:, c * T:(c + 1) * T], mean[:, c * 128:(c + 1) * 128], r.ident[0:T, 0:T])
                    done.then_inc(s["meanT_ready"], 1)

                def tokens_turned(g, u):
                    i = U * g + u
                    pe.wait_ge(s["meanT_kept"], i + 1)
                    for n in range(DC):
                        out = xgT_ps[:, n * T:(n + 1) * T]
                        for c in range(DC):
                            nc.tensor.matmul(out, a.w_res[:, c, n * 128:(n + 1) * 128], a.xnT[:, c, ds(i * T, T)], start=c == 0, stop=False)
                        for c in range(DC):
                            done = nc.tensor.matmul(out, a.w_gc[:, c, n * 128:(n + 1) * 128], meanT[:, c, :], start=False, stop=c == DC - 1)
                    done.then_inc(s["xgT_ready"], 1)

                def tokens_and_logits(g, u):
                    pe.wait_ge(s["xgT_kept"], U * g + u + 1)
                    for c in range(DC):
                        nc.tensor.transpose(xg_ps[:, c * 128:(c + 1) * 128], xgT[:, c, :], r.ident[:])
                    for c in range(DC):
                        done = nc.tensor.matmul(logit_ps, xgT[:, c, :], a.wg[:, c, :], start=c == 0, stop=c == DC - 1)
                    done.then_inc(s["logits_ready"], 1)

                def up(g, chunks):
                    for m in chunks:
                        if m >= 2:
                            pe.wait_ge(s["hidden_ready"], FC * g + m - 1)
                        for lo, hi in ((0, 512), (512, U * T)):
                            for c in range(DC):
                                done = nc.tensor.matmul(wide[m % 2][:, lo:hi], a.w1[:, c, m * 128:(m + 1) * 128], h2T[:, c, lo:hi],
                                                        start=c == 0, stop=c == DC - 1)
                        done.then_inc(s["up_ready"], 1)

                def down(g, tiles):
                    for u in tiles:
                        for m in range(FC):
                            done = nc.tensor.matmul(slot[u][0:T, :], hidden[:, m, u * T:(u + 1) * T], a.w2[:, m, :], start=m == 0, stop=m == FC - 1)
                        done.then_inc(s["down_ready"], 1)

                def turn_q_of(g):
                    for u in range(U):
                        pe.wait_ge(s["q_staged"], U * g + u + 1)
                        pe.sem_inc(s["passed"], 1)
                        nc.tensor.transpose(turn_q[u], qs[:, u, :], r.ident[0:T, 0:T]).then_inc(s["qT_ready"], 1)

                def attention(g):
                    pe.wait_ge(s["bias_summed"], g + 1)
                    pe.sem_inc(s["passed"], 1)
                    for u in range(U):
                        pe.wait_ge(s["qT_kept"], U * g + u + 1)
                        nc.tensor.matmul(slot[u][0:T, :], qT[:, u, :], a.m_aug[:], start=True, stop=True).then_inc(s["attn_ready"], 1)

                def other_blocks(g, following):
                    visit_block(g, 1)
                    turn_mean(g, 0)
                    for u in range(U):
                        pe.wait_ge(s["h2_ready"], U * g + u + 1)
                        for c in range(DC):
                            done = nc.tensor.transpose(slot[u][:, c * T:(c + 1) * T], h2[:, u, c * 128:(c + 1) * 128], r.ident[0:T, 0:T])
                        done.then_inc(s["h2T_ready"], 1)
                    tokens_turned(g, 0)
                    tokens_and_logits(g, 0)
                    for u in (1, 2):
                        visit_block(g, u + 1)
                        turn_mean(g, u)
                        if u == 1:
                            pe.wait_ge(s["h2T_kept"], U * g + U)
                        up(g, range(4 * u - 4, 4 * u - 2))
                        tokens_turned(g, u)
                        up(g, range(4 * u - 2, 4 * u))
                        tokens_and_logits(g, u)
                    visit_block(g, 4)
                    turn_mean(g, 3)
                    pe.wait_ge(s["hidden_ready"], FC * g + FC)
                    down(g, [0])
                    tokens_turned(g, 3)
                    down(g, [1])
                    tokens_and_logits(g, 3)
                    turn_mean(g, 4)
                    if following is not None:
                        turn_q_of(following)
                    tokens_turned(g, 4)
                    tokens_and_logits(g, 4)
                    if following is not None:
                        visit_block(following, 0)
                    down(g, range(2, U))
                    if following is not None:
                        attention(following)

                turn_q_of(0)
                visit_block(0, 0)
                attention(0)
                with pe.Fori(0, NG - 1) as g:
                    other_blocks(g, g + 1)
                other_blocks(NG - 1, None)


def route(nc, name, r, q, experts, cap, dense):
    names = "passed step act_step pe_step staged top_found id_found chosen marked placed halves_ready halves_free"
    cut = CUTS[experts]
    blocks, wide = cut.blocks, cut.wide
    loads = cut.loads + cut.unroll
    E = experts
    with phase(nc, name, names) as k:
        s, sb = k.s, k.sb
        top = sb("top", [T, NT, 2])
        logits_s, top_s, top_id_s = sb("logits_s", [T, U, E]), sb("top_s", [T, U, 8]), sb("top_id_s", [T, U, 8], U32)
        choice = sb("choice", [T, NT, 2])
        hot = [sb(f"hot{v}", [T, NT, E], BF16) for v in range(2)]
        both = sb("both", [T, NT, E], BF16)
        run = [sb(f"run{v}", [T, NT, E], BF16) for v in range(2)]
        rank, part = sb("rank", [T, NT, E]), sb("part", [T, NT, E])
        start_bc = sb("start_bc", [T, E])
        col = sb("col", [E, 8])
        ended = sb("ended", [E, loads])
        place = sb("place", [T, NT, 2])
        first, order, fits, slot = (sb(n, [T, NT, 2]) for n in ("first", "order", "fits", "slot"))
        slot_hi, slot_lo = sb("slot_hi", [T, 2 * NT]), sb("slot_lo", [T, 2 * NT])
        token = sb("token", [T, NT])
        line = sb("line", [1, loads])
        hot_lo = sb("hot_lo", [T, 2 * U, B])
        hot_hi = sb("hot_hi", [T, 2 * U, blocks])
        big = sb("big", [T, NT])
        ranks = k.psum[0:T, 0:NT * E]
        table = k.banks[4][:, 0:blocks]
        flat = lambda t: t[:].rearrange("p i e -> p (i e)")
        over = lambda t: t.unsqueeze(2).broadcast_to([T, NT, E])
        pick = lambda t, n: t[:, :, n:n + 1].broadcast_to([T, NT, E])

        with nc.Block() as block:
            @block.vector
            def _(dve):
                steps = [0]

                def then(ins):
                    steps[0] += 1
                    ins.then_inc(s["step"], 1)
                    dve.wait_ge(s["step"], steps[0])

                if dense:
                    then(nc.vector.tensor_reduce(big[:], q.logits[:], AX, ALU.max))
                    then(nc.vector.tensor_tensor(q.logits[:], q.logits[:], over(big[:]), ALU.subtract))
                    dve.wait_ge(s["act_step"], 1)
                    then(nc.vector.tensor_reduce(big[:], q.logits[:], AX, ALU.add))
                    then(nc.vector.reciprocal(big[:], big[:]))
                    then(nc.vector.tensor_tensor(q.logits[:], q.logits[:], over(big[:]), ALU.mult))
                with dve.Fori(0, NG) as g:
                    nc.vector.tensor_copy(logits_s[:], q.logits[:, ds(U * g, U), :]).then_inc(s["staged"], 1)
                    dve.wait_ge(s["staged"], g + 1)
                    dve.sem_inc(s["passed"], 1)
                    for u in range(U):
                        nc.vector.max(top_s[:, u, :], logits_s[:, u, :]).then_inc(s["top_found"], 1)
                    dve.wait_ge(s["top_found"], U * g + U)
                    dve.sem_inc(s["passed"], 1)
                    for u in range(U):
                        nc.vector.max_index(top_id_s[:, u, :], top_s[:, u, :], logits_s[:, u, :]).then_inc(s["id_found"], 1)
                    dve.wait_ge(s["id_found"], U * g + U)
                    nc.vector.tensor_copy(top[:, ds(U * g, U), :], top_s[:, :, 0:2])
                    nc.vector.tensor_copy(choice[:, ds(U * g, U), :], top_id_s[:, :, 0:2]).then_inc(s["chosen"], 1)
                dve.wait_ge(s["chosen"], NG)
                row = r.row[0:T, 0:E].unsqueeze(1).broadcast_to([T, NT, E])
                for n in range(2):
                    then(nc.vector.tensor_tensor(hot[n][:], row, pick(choice, n), ALU.is_equal))
                then(nc.vector.tensor_tensor(both[:], hot[0][:], hot[1][:], ALU.add))
                now = both
                for n, reach in enumerate((1, 2, 4, 8, 16)):
                    new = run[n % 2]
                    nc.vector.tensor_copy(new[:, 0:reach, :], now[:, 0:reach, :])
                    then(nc.vector.tensor_tensor(new[:, reach:, :], now[:, reach:, :], now[:, 0:NT - reach, :], ALU.add))
                    now = new
                nc.vector.tensor_scalar(token[:], r.row[0:T, 0:NT], float(T), r.col[0:T, :], ALU.mult, ALU.add).then_inc(s["marked"], 1)
                if dense:
                    nc.vector.tensor_copy(q.gates[:], top[:, :, 0:2])
                else:
                    then(nc.vector.tensor_tensor(q.gates[:, :, 1:2], top[:, :, 1:2], top[:, :, 0:1], ALU.subtract))
                    gate_step = steps[0]
                    dve.wait_ge(s["act_step"], 1)
                    then(nc.vector.tensor_scalar(q.gates[:, :, 0:1], q.gates[:, :, 1:2], 1.0, None, ALU.add))
                    then(nc.vector.reciprocal(q.gates[:, :, 0:1], q.gates[:, :, 0:1]))
                    then(nc.vector.tensor_tensor(q.gates[:, :, 1:2], q.gates[:, :, 1:2], q.gates[:, :, 0:1], ALU.mult))
                    q.gate_step = gate_step
                dve.wait_ge(s["pe_step"], 1)
                then(nc.vector.tensor_scalar(col[:, 0:1], k.banks[5][0:E, 0:1], float(cap), None, ALU.min))
                for ins in round_to_whole(nc, col[:, 1:2], col[:, 0:1], 1.0 / (B * wide), (B * wide - 1) / (2.0 * B * wide)):
                    then(ins())
                nc.vector.tensor_copy(col[:, 7:8], col[:, 1:2]).then_inc(s["placed"], 1)
                dve.wait_ge(s["pe_step"], 2)
                then(nc.vector.tensor_copy(col[:, 2:3], k.banks[5][0:E, 8:9]))
                then(nc.vector.tensor_tensor(col[:, 3:4], col[:, 2:3], col[:, 1:2], ALU.add))
                nc.vector.tensor_scalar(ended[:], r.row[0:E, 0:loads], col[:, 3:4], None, ALU.is_ge).then_inc(s["placed"], 1)
                dve.wait_ge(s["pe_step"], 3)
                then(nc.vector.tensor_copy(start_bc[:], k.banks[6][0:T, 0:E]))
                then(nc.vector.scalar_tensor_tensor(rank[:], start_bc[:].unsqueeze(1).broadcast_to([T, NT, E]), 8192.0,
                                                    ranks.rearrange("p (i e) -> p i e", e=E), ALU.mult, ALU.add))
                for n in range(2):
                    then(nc.vector.tensor_tensor(part[:], rank[:], hot[n][:], ALU.mult))
                    then(nc.vector.tensor_reduce(place[:, :, n], part[:], AX, ALU.add))
                for ins in round_to_whole(nc, first[:], place[:], 1.0 / 8192, -4095.5 / 8192):
                    then(ins())
                then(nc.vector.scalar_tensor_tensor(order[:], first[:], -8192.0, place[:], ALU.mult, ALU.add))
                then(nc.vector.tensor_scalar(fits[:], order[:], float(cap), None, ALU.is_lt))
                then(nc.vector.scalar_tensor_tensor(slot[:], first[:], float(B * wide), order[:], ALU.mult, ALU.add))
                then(nc.vector.scalar_tensor_tensor(slot[:], slot[:], 1.0, fits[:], ALU.add, ALU.mult))
                then(nc.vector.tensor_scalar(slot[:], slot[:], -1.0, None, ALU.add))
                nc.vector.tensor_tensor(q.gates[:], q.gates[:], fits[:], ALU.mult)
                nc.vector.tensor_scalar(q.slots[:], slot[:], 0.0, None, ALU.max)
                for ins in round_to_whole(nc, slot_hi[:], slot[:].rearrange("p i n -> p (i n)"), 1.0 / B, -(B / 2 - 0.5) / B):
                    then(ins())
                then(nc.vector.scalar_tensor_tensor(slot_lo[:], slot_hi[:], -float(B), slot[:].rearrange("p i n -> p (i n)"), ALU.mult, ALU.add))
                with dve.Fori(0, NG) as g:
                    for u in range(U):
                        for n in range(2):
                            w = 2 * u + n
                            at = ds(2 * U * g + w, 1)
                            dve.wait_ge(s["halves_free"], 2 * U * g + w + 1)
                            nc.vector.tensor_scalar(hot_lo[:, w, :], r.row[0:T, 0:B], slot_lo[:, at], None, ALU.is_equal)
                            nc.vector.tensor_scalar(hot_hi[:, w, :], r.row[0:T, 0:blocks], slot_hi[:, at], token[:, ds(U * g + u, 1)],
                                                    ALU.is_equal, ALU.mult).then_inc(s["halves_ready"], 1)
                then(nc.vector.tensor_tensor(part[:], hot[0][:], pick(q.gates, 0), ALU.mult))
                then(nc.vector.tensor_tensor(rank[:], hot[1][:], pick(q.gates, 1), ALU.mult))
                then(nc.vector.tensor_tensor(q.logits[:], part[:], rank[:], ALU.add))
                dve.wait_ge(s["pe_step"], 4)
                nc.vector.memset(q.token_of[:], 0)
                then(nc.vector.tensor_scalar(line[:], k.banks[7][0:1, 0:loads], float(E - 1), None, ALU.min))
                then(nc.vector.tensor_copy(q.expert_of[:], line[:]))
                then(nc.vector.tensor_copy(q.token_of[:, 0:blocks], table))
                for ins in round_to_whole(nc, line[:, 0:1], k.banks[6][0:1, 64:65], 1.0 / cut.unroll, (cut.unroll - 1) / (2.0 * cut.unroll)):
                    then(ins())
                then(nc.vector.tensor_copy(q.steps[:], line[:, 0:1]))

            @block.scalar
            def _(act):
                if dense:
                    act.wait_ge(s["step"], 2)
                    nc.scalar.activation(q.logits[:], q.logits[:], ACT.Exp).then_inc(s["act_step"], 1)
                else:
                    act.wait_ge(s["step"], q.gate_step)
                    nc.scalar.activation(q.gates[:, :, 1:2], q.gates[:, :, 1:2], ACT.Exp).then_inc(s["act_step"], 1)

            @block.tensor
            def _(pe):
                pe.sem_inc(s["halves_free"], 2 * U)
                pe.wait_ge(s["marked"], 1)
                counts = run[0]
                per = 512 // E
                for t0 in range(0, NT, per):
                    t1 = min(t0 + per, NT)
                    nc.tensor.matmul(ranks[:, t0 * E:t1 * E], r.tril[:], flat(both)[:, t0 * E:t1 * E], start=True, stop=False)
                    a0 = max(t0, 1)
                    nc.tensor.matmul(ranks[:, a0 * E:t1 * E], r.ones_b[:], flat(counts)[:, (a0 - 1) * E:(t1 - 1) * E], start=False, stop=True)
                nc.tensor.matmul(k.banks[5][0:E, 0:1], counts[:, NT - 1, :], r.ones_b[:, 0:1], start=True, stop=True).then_inc(s["pe_step"], 1)
                pe.wait_ge(s["placed"], 1)
                nc.tensor.matmul(k.banks[5][0:E, 8:9], r.tril_f[0:E, 0:E], col[:, 1:2], start=True, stop=True).then_inc(s["pe_step"], 1)
                pe.wait_ge(s["placed"], 2)
                nc.tensor.matmul(k.banks[6][0:T, 0:E], col[:, 2:3].broadcast_to([E, T]), r.ident[0:E, 0:E], start=True, stop=True)
                nc.tensor.matmul(k.banks[6][0:1, 64:65], r.ones[0:E, 0:1], col[:, 1:2], start=True, stop=True)
                nc.tensor.matmul(k.banks[7][0:1, 0:loads], r.ones[0:E, 0:1], ended[:], start=True, stop=True).then_inc(s["pe_step"], 1)
                nc.tensor.matmul(table, r.zeros[0:T, 0:B], r.zeros[0:T, 0:blocks], start=True, stop=False)
                with pe.Fori(0, NG) as g:
                    for w in range(2 * U):
                        pe.wait_ge(s["halves_ready"], 2 * U * g + w + 1)
                        nc.tensor.matmul(table, hot_lo[:, w, :], hot_hi[:, w, :], start=False, stop=False).then_inc(s["halves_free"], 1)
                nc.tensor.matmul(table, r.zeros[0:T, 0:B], r.zeros[0:T, 0:blocks], start=False, stop=True).then_inc(s["pe_step"], 1)


def run_experts(nc, name, r, q, experts, w1, w2, b1):
    cut = CUTS[experts]
    E, MU, W = experts, cut.unroll, cut.wide
    names = ("b1_in b1_turned b1_kept x_turned xT_kept up_ready hidden_ready down_ready y_kept idx_ready passed"
             + "".join(f" x_in{n} w1_in{n} w2_in{n}" for n in range(MU)) + " y_stored0 y_stored1")
    with phase(nc, name, names) as k:
        s, sb = k.s, k.sb
        x_in, w1_in, w2_in = ([s[f"{w}{n}"] for n in range(MU)] for w in ("x_in", "w1_in", "w2_in"))
        y_stored = [s["y_stored0"], s["y_stored1"]]
        w1s, w2s = sb("w1s", [128, MU, DC, H]), sb("w2s", [128, MU, HC, D])
        idx = sb("idx", [B, MU * W], I32)
        x = sb("x", [B, MU * W, D])
        xT = sb("xT", [128, 2, DC, W * B])
        hidden = sb("hidden", [128, 2, HC, W * B])
        y = sb("y", [B, 2, W, D])
        b1_rows, b1T = sb("b1_rows", [E, H]), sb("b1T", [128, HC, E])
        xT_ps = [k.banks[v][:, 0:DC * W * B] for v in range(2)]
        up_ps = [k.psum[:, 512 * (2 + 2 * v):512 * (2 + 2 * v) + HC * W * B] for v in range(2)]
        down_ps = [k.banks[6 + v][:, 0:W * D] for v in range(2)]
        w1_rows, w2_rows = w1.rearrange("e (c p) h -> e p c h", p=128), w2.rearrange("e (c p) h -> e p c h", p=128)
        expert = lambda eng, m: eng.value_load(q.expert_of[0:1, ds(m, 1)], min_val=0, max_val=E - 1)
        loop_steps = lambda eng: eng.value_load(q.steps[0:1, 0:1], min_val=1, max_val=cut.steps)
        y_rows = q.outputs.rearrange("(m w p) d -> m p w d", p=B, w=W)

        with nc.Block() as block:
            @block.sync
            def _(sp):
                sp.dma_start(b1_rows[:], b1).then_inc(s["b1_in"], 16)

                def load(m, n):
                    e = expert(sp, m)
                    sp.wait_ge(s["up_ready"], m + 1)
                    sp.dma_start(w1s[:, n], w1_rows[ds(e, 1)].rearrange("o p c h -> p (o c) h")).then_inc(w1_in[n], 16)
                    sp.wait_ge(s["down_ready"], m + 1)
                    sp.dma_start(w2s[:, n], w2_rows[ds(e, 1)].rearrange("o p c h -> p (o c) h")).then_inc(w2_in[n], 16)
                load(0, 0)
                with sp.Fori(0, loop_steps(sp)) as i:
                    for u in range(MU):
                        load(MU * i + u + 1, (u + 1) % MU)
                n = loop_steps(sp)
                for w in (w1_in, w2_in):
                    for u in range(MU):
                        sp.wait_ge(w[u], 16 * n + (16 if u == 0 else 0))
                sp.sem_inc(s["passed"], 1)
                sp.wait_ge(s["b1_in"], 16)

            @block.gpsimd
            def _(pool):
                def gather(m, n):
                    pool.wait_ge(s["x_turned"], m + 1)
                    pool.sem_inc(s["passed"], 1)
                    nc.gpsimd.tensor_copy(idx[:, W * n:W * n + W], q.token_of[:, ds(W * m, W)]).then_inc(s["idx_ready"], 1)
                    pool.wait_ge(s["idx_ready"], m + 1)
                    pool.sem_inc(s["passed"], 1)
                    for w in range(W * n, W * n + W):
                        nc.gpsimd.indirect_dma_start(out=x[:, w, :], out_offset=None, in_=q.tokens[:, :],
                                                     in_offset=bass.IndirectOffsetOnAxis(ap=idx[:, w:w + 1], axis=0)).then_inc(x_in[n], 16)
                gather(0, 0)
                gather(1, 1)
                with pool.Fori(0, loop_steps(pool)) as i:
                    for u in range(MU):
                        gather(MU * i + u + 2, (u + 2) % MU)

            @block.vector
            def _(dve):
                dve.wait_ge(s["b1_turned"], 1)
                nc.vector.tensor_copy(b1T[:], k.banks[7][:, 0:HC * E].rearrange("p (c e) -> p c e", c=HC)).then_inc(s["b1_kept"], 1)
                dve.wait_ge(s["b1_kept"], 1)
                dve.sem_inc(s["xT_kept"], 2)
                dve.sem_inc(s["y_kept"], 2)

                def keep_x(m, v):
                    dve.wait_ge(s["x_turned"], m + 1 + MU)
                    dve.wait_ge(s["up_ready"], m + MU - 1)
                    nc.vector.tensor_copy(xT[:, v], xT_ps[v].rearrange("p (c t) -> p c t", c=DC)).then_inc(s["xT_kept"], 1)

                def keep_y(m, v, uses):
                    dve.wait_ge(s["down_ready"], m + 1 + MU)
                    dve.wait_ge(y_stored[v], 16 * uses + 16)
                    nc.vector.tensor_copy(y[:, v].rearrange("p w d -> p (w d)"), down_ps[v]).then_inc(s["y_kept"], 1)
                keep_x(0, 0)
                keep_x(1, 1)
                with dve.Fori(0, loop_steps(dve)) as i:
                    for u in range(MU):
                        keep_x(MU * i + u + 2, u % 2)
                        keep_y(MU * i + u, u % 2, MU // 2 * i + u // 2)

            @block.scalar
            def _(act):
                act.sem_inc(s["hidden_ready"], 2)
                act.sem_inc(y_stored[0], 16)
                act.sem_inc(y_stored[1], 16)
                act.wait_ge(s["b1_kept"], 1)

                def activate(m, v):
                    e = expert(act, m)
                    act.wait_ge(s["up_ready"], m + 1 + MU)
                    act.wait_ge(s["down_ready"], m + MU - 1)
                    for j in range(HC):
                        done = nc.scalar.activation(hidden[:, v, j, :], up_ps[v][:, j * W * B:(j + 1) * W * B], ACT.Gelu,
                                                    bias=b1T[:, j, ds(e, 1)])
                    done.then_inc(s["hidden_ready"], 1)
                activate(0, 0)
                with act.Fori(0, loop_steps(act)) as i:
                    for u in range(MU):
                        activate(MU * i + u + 1, (u + 1) % 2)
                        act.wait_ge(s["y_kept"], MU * i + u + 1 + 2)
                        act.dma_start(y_rows[ds(MU * i + u, 1)].rearrange("o p w d -> p (o w) d"), y[:, u % 2]).then_inc(y_stored[u % 2], 16)
                n = loop_steps(act)
                for v in range(2):
                    act.wait_ge(y_stored[v], MU // 2 * 16 * n + 16)
                act.sem_inc(s["passed"], 1)

            @block.tensor
            def _(pe):
                pe.wait_ge(s["b1_in"], 16)
                for c in range(HC):
                    done = nc.tensor.transpose(k.banks[7][:, c * E:(c + 1) * E], b1_rows[:, c * 128:(c + 1) * 128], r.ident[0:E, 0:E])
                done.then_inc(s["b1_turned"], 1)
                for primed in (s["x_turned"], s["up_ready"], s["down_ready"]):
                    pe.sem_inc(primed, MU)

                def turn(m, v, n, landed):
                    pe.wait_ge(x_in[n], landed)
                    pe.wait_ge(s["xT_kept"], m + 1)
                    for c in range(DC):
                        for w in range(W):
                            done = nc.tensor.transpose(xT_ps[v][:, (c * W + w) * B:(c * W + w + 1) * B],
                                                       x[:, W * n + w, c * 128:(c + 1) * 128], r.ident[:])
                    done.then_inc(s["x_turned"], 1)

                def up(m, v, n, landed):
                    pe.wait_ge(w1_in[n], landed)
                    pe.wait_ge(s["hidden_ready"], m + 1)
                    pe.wait_ge(s["xT_kept"], m + 3)
                    for j in range(HC):
                        for c in range(DC):
                            done = nc.tensor.matmul(up_ps[v][:, j * W * B:(j + 1) * W * B], w1s[:, n, c, j * 128:(j + 1) * 128], xT[:, v, c, :],
                                                    start=c == 0, stop=c == DC - 1)
                    done.then_inc(s["up_ready"], 1)

                def down(m, v, n, landed):
                    pe.wait_ge(w2_in[n], landed)
                    pe.wait_ge(s["y_kept"], m + 1)
                    pe.wait_ge(s["hidden_ready"], m + 3)
                    for w in range(W):
                        for j in range(HC):
                            done = nc.tensor.matmul(down_ps[v][:, w * D:(w + 1) * D], hidden[:, v, j, w * B:(w + 1) * B], w2s[:, n, j, :],
                                                    start=j == 0, stop=j == HC - 1)
                    done.then_inc(s["down_ready"], 1)
                turn(0, 0, 0, 16 * W)
                turn(1, 1, 1, 16 * W)
                up(0, 0, 0, 16)
                with pe.Fori(0, loop_steps(pe)) as i:
                    for u in range(MU):
                        turn(MU * i + u + 2, u % 2, (u + 2) % MU, 16 * W * i + 16 * W * (1 + (u + 2) // MU))
                        up(MU * i + u + 1, (u + 1) % 2, (u + 1) % MU, 16 * i + 16 * (1 + (u + 1) // MU))
                        down(MU * i + u, u % 2, u, 16 * i + 16)


def combine(nc, name, r, q, experts, b2, out):
    names = ("b2_in idx_ready passed joined joined1 joined2 joined3 gates_staged gates_turned gatesT_kept bias_ready summed out_stored"
             + "".join(f" y_in{n}" for n in range(2 * U)))
    E = experts
    with phase(nc, name, names) as k:
        s, sb = k.s, k.sb
        y_in = [s[f"y_in{n}"] for n in range(2 * U)]
        b2s = sb("b2", [E, D])
        idx = sb("idx", [T, 2 * U], I32)
        y = sb("y", [T, 2 * U, D])
        total = sb("total", [T, U, D])
        gates_s, gatesT = sb("gates_s", [T, U, E]), sb("gatesT", [E, U, T])
        turned = [k.banks[u // 4][0:E, (u % 4) * T:(u % 4 + 1) * T] for u in range(U)]
        bias = [k.banks[2 + u // 2][0:T, (u % 2) * 256:(u % 2) * 256 + 256] for u in range(U)]
        sums = k.banks[7][0:T, 0:D]
        home = r.nodes if out is None else r.acc
        tile3 = lambda t, i: t[:, ds(i, 1), :].rearrange("p o d -> p (o d)")
        slots = q.slots[:].rearrange("p i n -> p (i n)")
        gates = q.gates[:].rearrange("p i n -> p (i n)")
        with nc.Block() as block:
            @block.sync
            def _(sp):
                sp.dma_start(b2s[:], b2).then_inc(s["b2_in"], 16)
                if out is not None:
                    with sp.Fori(0, NG) as g:
                        sp.wait_ge(s["joined3"], U * g + U)
                        for p0, p1 in ((0, SPLIT), (SPLIT, T)):
                            sp.dma_start(rows_of(out, g)[p0:p1], home[p0:p1, ds(U * g, U), :]).then_inc(s["out_stored"], 16)
                    sp.wait_ge(s["out_stored"], 32 * NG)
                sp.wait_ge(s["b2_in"], 16)

            @block.gpsimd
            def _(pool):
                with pool.Fori(0, NG) as g:
                    for u in range(U):
                        i = U * g + u
                        pool.wait_ge(s["joined"], i + 1)
                        nc.gpsimd.tensor_copy(idx[:, 2 * u:2 * u + 2], slots[:, ds(2 * i, 2)]).then_inc(s["idx_ready"], 1)
                        pool.wait_ge(s["idx_ready"], i + 1)
                        pool.sem_inc(s["passed"], 1)
                        for n in range(2):
                            w = 2 * u + n
                            nc.gpsimd.indirect_dma_start(out=y[:, w, :], out_offset=None, in_=q.outputs[:, :],
                                                         in_offset=bass.IndirectOffsetOnAxis(ap=idx[:, w:w + 1], axis=0)).then_inc(y_in[w], 16)

            @block.vector
            def _(dve):
                dve.sem_inc(s["joined"], U)
                with dve.Fori(0, NG) as g:
                    for u in range(U):
                        nc.vector.tensor_copy(gates_s[:, u, :], tile3(q.logits, U * g + u)).then_inc(s["gates_staged"], 1)
                    dve.wait_ge(s["bias_ready"], U * g + U)
                    for u in range(U):
                        i = U * g + u
                        nc.vector.tensor_tensor(total[:, u, :], bias[u], tile3(home, i), ALU.add).then_inc(s["joined1"], 1)
                    for u in range(U):
                        i = U * g + u
                        dve.wait_ge(s["joined1"], i + 1)
                        dve.wait_ge(y_in[2 * u], 16 * g + 16)
                        nc.vector.scalar_tensor_tensor(total[:, u, :], y[:, 2 * u, :], gates[:, ds(2 * i, 1)], total[:, u, :],
                                                       ALU.mult, ALU.add).then_inc(s["joined2"], 1)
                    for u in range(U):
                        i = U * g + u
                        dve.wait_ge(s["joined2"], i + 1)
                        dve.wait_ge(y_in[2 * u + 1], 16 * g + 16)
                        nc.vector.scalar_tensor_tensor(tile3(home, i), y[:, 2 * u + 1, :], gates[:, ds(2 * i + 1, 1)], total[:, u, :],
                                                       ALU.mult, ALU.add).then_inc(s["joined3"], 1)
                    for u in range(U):
                        dve.wait_ge(s["joined3"], U * g + u + 1)
                        dve.sem_inc(s["joined"], 1)

            @block.scalar
            def _(act):
                with act.Fori(0, NG) as g:
                    act.wait_ge(s["gates_turned"], U * g + U)
                    for u in range(U):
                        nc.scalar.activation(gatesT[:, u, :], turned[u], ACT.Copy).then_inc(s["gatesT_kept"], 1)

            @block.tensor
            def _(pe):
                pe.wait_ge(s["b2_in"], 16)
                if out is None:
                    nc.tensor.matmul(sums, r.zeros[0:T, 0:T], r.zeros[0:T, 0:D], start=True, stop=False)
                with pe.Fori(0, NG) as g:
                    for u in range(U):
                        pe.wait_ge(s["gates_staged"], U * g + u + 1)
                        pe.sem_inc(s["passed"], 1)
                        nc.tensor.transpose(turned[u], gates_s[:, u, :], r.ident[0:T, 0:T]).then_inc(s["gates_turned"], 1)
                    for u in range(U):
                        pe.wait_ge(s["gatesT_kept"], U * g + u + 1)
                        nc.tensor.matmul(bias[u], gatesT[:, u, :], b2s[:], start=True, stop=True).then_inc(s["bias_ready"], 1)
                    if out is None:
                        for u in range(U):
                            pe.wait_ge(s["joined3"], U * g + u + 1)
                            nc.tensor.matmul(sums, r.ones[:], tile3(r.nodes, U * g + u), start=False, stop=False)
                if out is None:
                    nc.tensor.matmul(sums, r.zeros[0:T, 0:T], r.zeros[0:T, 0:D], start=False, stop=True).then_inc(s["summed"], 1)
                    pe.wait_ge(s["summed"], 1)
            if out is None:
                @block.vector
                def _(dve):
                    dve.wait_ge(s["summed"], 1)
                    nc.vector.tensor_scalar(q.mean[:], sums, 1.0 / N, None, ALU.mult).then_inc(s["joined1"], 1)
                    dve.wait_ge(s["joined1"], NT + 1)


def batch_norm(nc, d, r, q, p):
    names = ("passed loaded centred squared squares_free squared_sum scaled step roots"
             " product sum_ready sum_stats sum_moments sum_root sum_inverse x_ready x_stored xT_ready xT_kept logits_ready logits_kept")
    with phase(nc, "norm", names) as k:
        s, sb = k.s, k.sb
        gamma, spread = sb("gamma", [T, D]), sb("spread", [T, D])
        gate_w, gate_b = sb("gate_w", [128, DC, E_FFN]), sb("gate_b", [T, E_FFN])
        squares = sb("squares", [T, U, D])
        stats, moments, root = sb("stats", [T, U, 6]), sb("moments", [T, U, 2]), sb("root", [T, U])
        x = sb("x", [T, U, D])
        xT = sb("xT", [128, U, DC, T])
        sums = k.banks[7][0:T, 0:D]
        turned = [k.banks[u // 2][:, (u % 2) * 256:(u % 2) * 256 + DC * T] for u in range(U)]
        logit_ps = k.banks[3][0:T, 0:U * E_FFN]
        tile3 = lambda t, i: t[:, ds(i, 1), :].rearrange("p o d -> p (o d)")
        with nc.Block() as block:
            @block.sync
            def _(sp):
                for p0, p1 in ((0, SPLIT), (SPLIT, T)):
                    sp.dma_start(gamma[p0:p1], d["gnn_gamma"].partition_broadcast(p1 - p0)).then_inc(s["loaded"], 16)
                    sp.dma_start(gate_b[p0:p1], d["ffn_gate_b"].partition_broadcast(p1 - p0)).then_inc(s["loaded"], 16)
                sp.dma_start(gate_w[:], d["ffn_gate_w"].rearrange("(c p) n -> p c n", p=128)).then_inc(s["loaded"], 16)
                sp.sem_inc(s["x_stored"], 32)
                with sp.Fori(0, NG) as g:
                    sp.wait_ge(s["x_ready"], U * g + U)
                    for p0, p1 in ((0, SPLIT), (SPLIT, T)):
                        sp.dma_start(rows_of(p.tokens, g)[p0:p1], x[p0:p1]).then_inc(s["x_stored"], 16)
                sp.wait_ge(s["x_stored"], 32 * NG + 32)
                sp.wait_ge(s["loaded"], 80)

            @block.vector
            def _(dve):
                with dve.Fori(0, NG) as g:
                    for u in range(U):
                        nc.vector.tensor_tensor(tile3(r.nodes, U * g + u), tile3(r.nodes, U * g + u), q.mean[:], ALU.subtract).then_inc(s["centred"], 1)
                dve.wait_ge(s["squared_sum"], 1)
                nc.vector.tensor_scalar(spread[:], sums, 1.0 / N, None, ALU.mult).then_inc(s["step"], 1)
                dve.wait_ge(s["roots"], 1)
                nc.vector.reciprocal(spread[:], spread[:]).then_inc(s["step"], 1)
                dve.wait_ge(s["step"], 2)
                dve.wait_ge(s["loaded"], 80)
                nc.vector.tensor_tensor(spread[:], spread[:], gamma[:], ALU.mult).then_inc(s["step"], 1)
                dve.wait_ge(s["step"], 3)
                with dve.Fori(0, NG) as g:
                    for u in range(U):
                        nc.vector.tensor_tensor(tile3(r.nodes, U * g + u), tile3(r.nodes, U * g + u), spread[:], ALU.mult).then_inc(s["product"], 1)
                    for u in range(U):
                        i = U * g + u
                        dve.wait_ge(s["product"], i + 1)
                        nc.vector.tensor_tensor(tile3(r.acc, i), tile3(r.acc, i), tile3(r.nodes, i), ALU.add).then_inc(s["sum_ready"], 1)
                    dve.wait_ge(s["sum_ready"], U * g + U)
                    dve.sem_inc(s["passed"], 1)
                    for u in range(U):
                        nc.vector.bn_stats(stats[:, u, :], tile3(r.acc, U * g + u)).then_inc(s["sum_stats"], 1)
                    dve.wait_ge(s["sum_stats"], U * g + U)
                    dve.sem_inc(s["passed"], 1)
                    for u in range(U):
                        nc.vector.bn_aggr(moments[:, u, :], stats[:, u, :]).then_inc(s["sum_moments"], 1)
                    dve.wait_ge(s["sum_root"], g + 1)
                    nc.vector.reciprocal(root[:], root[:]).then_inc(s["sum_inverse"], 1)
                    dve.wait_ge(s["sum_inverse"], g + 1)
                    dve.wait_ge(s["x_stored"], 32 * g + 32)
                    for u in range(U):
                        i = U * g + u
                        nc.vector.tensor_scalar(x[:, u, :], tile3(r.acc, i), moments[:, u, 0:1], root[:, u:u + 1],
                                                ALU.subtract, ALU.mult).then_inc(s["x_ready"], 1)
                    dve.wait_ge(s["logits_ready"], U * g + U)
                    nc.vector.tensor_tensor(p.logits[:, ds(U * g, U), :], logit_ps.rearrange("p (u n) -> p u n", u=U),
                                            gate_b[:].unsqueeze(1).broadcast_to([T, U, E_FFN]), ALU.add).then_inc(s["logits_kept"], 1)

            @block.scalar
            def _(act):
                with act.Fori(0, NG) as g:
                    for u in range(U):
                        i = U * g + u
                        act.wait_ge(s["centred"], i + 1)
                        act.wait_ge(s["squares_free"], i + 1)
                        nc.scalar.activation(squares[:, u, :], tile3(r.nodes, i), ACT.Square).then_inc(s["squared"], 1)
                act.wait_ge(s["step"], 1)
                nc.scalar.activation(spread[:], spread[:], ACT.Sqrt, bias=r.eps[0:T, :]).then_inc(s["roots"], 1)
                with act.Fori(0, NG) as g:
                    act.wait_ge(s["sum_moments"], U * g + U)
                    nc.scalar.activation(root[:], moments[:, :, 1], ACT.Sqrt, bias=r.eps[0:T, :]).then_inc(s["sum_root"], 1)
                    act.wait_ge(s["xT_ready"], U * g + U)
                    for u in range(U):
                        nc.scalar.activation(xT[:, u], turned[u].rearrange("p (c t) -> p c t", c=DC), ACT.Copy).then_inc(s["xT_kept"], 1)

            @block.tensor
            def _(pe):
                pe.sem_inc(s["squares_free"], U)
                nc.tensor.matmul(sums, r.zeros[0:T, 0:T], r.zeros[0:T, 0:D], start=True, stop=False)
                with pe.Fori(0, NG) as g:
                    for u in range(U):
                        pe.wait_ge(s["squared"], U * g + u + 1)
                        nc.tensor.matmul(sums, r.ones[:], squares[:, u, :], start=False, stop=False).then_inc(s["squares_free"], 1)
                nc.tensor.matmul(sums, r.zeros[0:T, 0:T], r.zeros[0:T, 0:D], start=False, stop=True).then_inc(s["squared_sum"], 1)
                pe.wait_ge(s["loaded"], 80)
                with pe.Fori(0, NG) as g:
                    for u in range(U):
                        pe.wait_ge(s["x_ready"], U * g + u + 1)
                        for c in range(DC):
                            done = nc.tensor.transpose(turned[u][:, c * T:(c + 1) * T], x[:, u, c * 128:(c + 1) * 128], r.ident[0:T, 0:T])
                        done.then_inc(s["xT_ready"], 1)
                    for u in range(U):
                        pe.wait_ge(s["xT_kept"], U * g + u + 1)
                        for c in range(DC):
                            done = nc.tensor.matmul(logit_ps[:, u * E_FFN:(u + 1) * E_FFN], xT[:, u, c, :], gate_w[:, c, :], start=c == 0, stop=c == DC - 1)
                        done.then_inc(s["logits_ready"], 1)


def program(nc, d, out):
    with ExitStack() as scope:
        r = resident(nc, scope)
        constants(nc, r)
        sb = lambda where, n, shape, dt=F32: where.enter_context(nc.sbuf_tensor(n, shape, dt))

        def layer(where, name, experts):
            cut = CUTS[experts]
            kept = Bag()
            kept.logits = sb(where, f"{name}_logits", [T, NT, experts])
            kept.gates = sb(where, f"{name}_gates", [T, NT, 2])
            kept.slots = sb(where, f"{name}_slots", [T, NT, 2], I32)
            kept.token_of = sb(where, f"{name}_token_of", [B, cut.blocks + cut.wide * cut.unroll], I32)
            kept.expert_of = sb(where, f"{name}_expert_of", [1, cut.loads + cut.unroll], I32)
            kept.steps = sb(where, f"{name}_steps", [1, 1], I32)
            kept.tokens = nc.dram_tensor(f"{name}_tokens", (N, D), F32, kind="Internal").ap()
            kept.outputs = nc.dram_tensor(f"{name}_outputs", (cut.blocks * B, D), F32, kind="Internal").ap()
            return kept
        with ExitStack() as graph_scope:
            q = layer(graph_scope, "graph", E_GNN)
            p = layer(graph_scope, "dense", E_FFN)
            q.mean = sb(graph_scope, "column_mean", [T, D])
            with ExitStack() as mix_scope:
                m = lambda n, shape, dt=F32: sb(mix_scope, n, shape, dt)
                a = Bag()
                a.hn, a.xnT, a.qk = m("hn", [T, NT, D]), m("xnT", [128, DC, N]), m("qk", [T, NT, 2 * HR])
                a.src_idx, a.dst_t = m("src_idx", [T, EC + EPAD], I32), m("dst_t", [T, EC + EPAD])
                a.visit_tab, a.rs_out = m("visit_tab", [1, 3, NT], I32), m("rs_out", [T, NT])
                a.wx, a.wv, a.wo = m("wx", [128, DC, D]), m("wv", [128, 128]), m("wo", [128, DC, D])
                a.w_gc, a.w_res, a.wg = m("w_gc", [128, DC, D]), m("w_res", [128, DC, D]), m("wg", [128, DC, E_GNN])
                a.cols = m("cols", [128, 22])
                a.bx_row, a.g1_bc, a.b1_bc = m("bx_row", [1, D]), m("g1_bc", [HR, D]), m("b1_bc", [HR, D])
                a.b2_bc, a.bg_bc, a.beta_bc = m("b2_bc", [T, D]), m("bg_bc", [T, E_GNN]), m("beta_bc", [T, D])
                a.m_aug = m("m_aug", [HR + 1, D])
                a.h_dram = nc.dram_tensor("scaled_nodes", (N, D), F32, kind="Internal").ap()
                prepare(nc, d, r, a, (q, p))
                a.w1, a.w2 = m("w1", [128, DC, FF]), m("w2", [128, FC, D])
                attention_state(nc, d, r, a)
                graph_and_mix(nc, d, r, a, q, p)
            route(nc, "graph_route", r, q, E_GNN, CAP, dense=False)
            run_experts(nc, "graph_experts", r, q, E_GNN, d["gnn_w1"], d["gnn_w2"], d["gnn_b1"])
            combine(nc, "graph_combine", r, q, E_GNN, d["gnn_b2"], None)
            batch_norm(nc, d, r, q, p)
            route(nc, "dense_route", r, p, E_FFN, 2 * N, dense=True)
            run_experts(nc, "dense_experts", r, p, E_FFN, d["ffn_W1"], d["ffn_W2"], d["ffn_b1"])
            combine(nc, "dense_combine", r, p, E_FFN, d["ffn_b2"], out)


_INS = ["x", "src", "dst", "gnn_W_gc", "gnn_b_gc", "gnn_W_res", "gnn_b_res", "gnn_Wg", "gnn_bg", "gnn_w1", "gnn_b1", "gnn_w2", "gnn_b2",
        "gnn_gamma", "gnn_beta", "mix_ln1_g", "mix_ln1_b", "mix_Wx", "mix_bx", "mix_Wq", "mix_Wk", "mix_Wv", "mix_Wo", "mix_bo",
        "mix_ln2_g", "mix_ln2_b", "mix_W1", "mix_b1", "mix_W2", "mix_b2",
        "ffn_gate_w", "ffn_gate_b", "ffn_W1", "ffn_b1", "ffn_W2", "ffn_b2"]


def kernel(**inputs):
    import numpy as _np
    import concourse.bacc as _bacc
    from concourse import mybir as _mybir
    from concourse.bass_utils import run_bass_kernel_spmd as _run

    nc = _bacc.Bacc("TRN2", target_bir_lowering=False, num_devices=1)
    arrays, args = {}, {}
    for name in _INS:
        a = _np.ascontiguousarray(inputs[name if name in inputs else "L0_" + name])
        arrays[f"in_{name}"] = a
        args[name] = nc.dram_tensor(f"in_{name}", a.shape, _mybir.dt.from_np(a.dtype), kind="ExternalInput").ap()
    out = nc.dram_tensor("out_0", (N, D), F32, kind="ExternalOutput").ap()
    program(nc, args, out)
    return _run(nc, [arrays], core_ids=[0]).results[0]["out_0"]
```

```python
from contextlib import ExitStack, contextmanager

import concourse.bass as bass
from concourse import mybir

F32, I32, U32, BF16 = mybir.dt.float32, mybir.dt.int32, mybir.dt.uint32, mybir.dt.bfloat16
ALU = mybir.AluOpType
ACT = mybir.ActivationFunctionType
AX = mybir.AxisListType.X
ds = bass.ds

N, D = 3125, 256
NE = 50000
T = 125
NT = N // T
U = 5
NG = NT // U
EC = NE // T
EQ = 100
EJ = EC // EQ
VU = 5
SETS = 4
SET_BITS = SETS.bit_length() - 1
EPAD = VU
HG = 20
DC = D // 128
EPS = 1e-5
MAGIC = float(3 << 22)
HEADS, DH, KR = 8, 32, 4
HR = HEADS * KR
FF = 1024
FC = FF // 128
H = 512
HC = H // 128
B = 128
E_GNN, E_FFN = 64, 8
CAP = 1024
SPLIT = 112


class Bag:
    pass


class Cut:

    def __init__(self, experts, wide, unroll):
        self.experts, self.wide, self.unroll = experts, wide, unroll
        self.reuse = unroll > 2
        slots = B * wide
        loads = (2 * N + experts * (slots - 1)) // slots
        self.steps = -(-loads // unroll)
        self.loads = self.steps * unroll
        self.blocks = self.loads * wide


CUTS = {E_GNN: Cut(E_GNN, wide=1, unroll=4), E_FFN: Cut(E_FFN, wide=2, unroll=2)}


@contextmanager
def phase(nc, name, semaphores):
    sems = {s: nc.alloc_semaphore(f"{name}_{s}") for s in semaphores.split()}
    with ExitStack() as scope:
        tools = Bag()
        tools.sb = lambda n, shape, dt=F32: scope.enter_context(nc.sbuf_tensor(f"{name}_{n}", shape, dt))
        tools.psum = scope.enter_context(nc.psum_tensor(f"{name}_psum", [128, 8 * 512], F32))[:]
        tools.s = sems
        tools.banks = [tools.psum[:, 512 * n:512 * (n + 1)] for n in range(8)]
        tools.wide = [tools.psum[:, 512 * n:512 * (n + 2)] for n in (3, 5)]
        yield tools
    nc.clear_and_free_semaphores(list(sems.values()))
    nc.all_engine_barrier(sem_only=True)


def rows_of(dram, group):
    return dram.rearrange("(g u p) d -> g p u d", p=T, u=U)[group]


def round_to_whole(nc, out, in_, scale, shift):
    return (lambda: nc.vector.tensor_scalar(out, in_, scale, shift, ALU.mult, ALU.add),
            lambda: nc.vector.tensor_scalar(out, out, MAGIC, MAGIC, ALU.add, ALU.subtract))


def resident(nc, scope):
    sb = lambda n, shape, dt=F32: scope.enter_context(nc.sbuf_tensor(n, shape, dt))
    r = Bag()
    r.acc = sb("acc", [T, NT, D])
    r.nodes = sb("nodes", [T, NT, D])
    r.ident = sb("ident", [128, 128])
    r.ones = sb("ones", [T, T])
    r.zeros = sb("zeros", [128, D + 2], BF16)
    r.tril_f = sb("tril_f", [64, 64])
    r.tril = sb("tril", [T, T], BF16)
    r.ones_b = sb("ones_b", [T, T], BF16)
    r.row = sb("row", [128, 512])
    r.col = sb("col", [128, 1])
    r.eps = sb("eps", [128, 1])
    return r


def constants(nc, r):
    with phase(nc, "constants", "filled shaped") as k:
        s = k.s
        with nc.Block() as block:
            @block.gpsimd
            def _(pool):
                nc.gpsimd.memset(r.ident[:], 0.0)
                nc.gpsimd.memset(r.ones[:], 1.0)
                nc.gpsimd.memset(r.ones_b[:], 1.0)
                nc.gpsimd.memset(r.tril[:], 1.0)
                nc.gpsimd.memset(r.tril_f[:], 1.0)
                nc.gpsimd.memset(r.zeros[:], 0.0)
                nc.gpsimd.memset(r.eps[:], EPS)
                nc.gpsimd.iota(r.row[:], pattern=[[1, 512]], base=0, channel_multiplier=0,
                               allow_small_or_imprecise_dtypes=True)
                nc.gpsimd.iota(r.col[:], pattern=[[0, 1]], base=0, channel_multiplier=1,
                               allow_small_or_imprecise_dtypes=True).then_inc(s["filled"], 1)
                pool.wait_ge(s["filled"], 1)
                nc.gpsimd.affine_select(out=r.ident[:], in_=r.ident[:], compare_op=ALU.not_equal, fill=1.0,
                                        base=0, pattern=[[-1, 128]], channel_multiplier=1).then_inc(s["shaped"], 1)
                nc.gpsimd.affine_select(out=r.tril[:], in_=r.tril[:], compare_op=ALU.is_gt, fill=0.0,
                                        base=0, pattern=[[1, T]], channel_multiplier=-1).then_inc(s["shaped"], 1)
                nc.gpsimd.affine_select(out=r.tril_f[:], in_=r.tril_f[:], compare_op=ALU.is_gt, fill=0.0,
                                        base=0, pattern=[[1, 64]], channel_multiplier=-1).then_inc(s["shaped"], 1)
                pool.wait_ge(s["shaped"], 3)


def prepare(nc, d, r, a, layers):
    names = ("edges_in x_in mix_in rest_in edges_float edge_columns ids ids_step hist_ready hist_free degree degree_root"
             " chunk_range range_bc visit_step visit_row tables blockdiag wx_turned wx_copied folded qk_weights"
             " stats1 moments1 root1 inverse1 xn_ready xn_free h_ready h_stored stats2 moments2 root2 inverse2"
             " hn_ready hn_free xnT_turned hnT_turned hT_ready qk_ready qk_kept xnT_kept passed blanked")
    with phase(nc, "prepare", names) as k:
        s, sb = k.s, k.sb
        src_n, dst_n = sb("src_n", [EQ, EJ, T], I32), sb("dst_n", [EQ, EJ, T], I32)
        src_f, dst_f = sb("src_f", [EQ, EJ, T]), sb("dst_f", [EQ, EJ, T])
        src_t, src_hi = sb("src_t", [T, EC]), sb("src_hi", [T, EC])
        hi_b, lo_b = sb("hi_b", [T, EC], BF16), sb("lo_b", [T, EC], BF16)
        count_lo, count_hi = sb("count_lo", [T, T, HG], BF16), sb("count_hi", [T, NT, HG], BF16)
        hot_lo = [sb(f"hot_lo{v}", [T, T, HG], BF16) for v in range(2)]
        hot_hi = [sb(f"hot_hi{v}", [T, NT, HG], BF16) for v in range(2)]
        degree = sb("degree", [T, NT])
        reach = sb("reach", [EQ, 2, EJ])
        lo_c, hi_c = sb("lo_c", [NT, EC]), sb("hi_c", [NT, EC])
        visit = sb("visit", [NT, 8])
        blockdiag_qk = sb("blockdiag_qk", [128, DC, 2 * HR])
        bias_rows = sb("bias_rows", [22, 128])
        wx_t = sb("wx_t", [128, DC, D])
        wqk = sb("wqk", [128, DC, 2 * HR])
        bqk = sb("bqk", [T, 2 * HR])
        stats, moments = sb("stats", [T, U, 6]), sb("moments", [T, U, 2])
        root = sb("root", [T, U])
        xn = sb("xn", [T, U, D])
        hn = sb("hn", [T, U, D])
        h_out = sb("h_out", [T, U, D])
        hT = sb("hT", [128, U, DC, T])
        blank = sb("blank", [B, D])
        turn_x = [k.banks[u // 2][:, (u % 2) * 256:(u % 2) * 256 + DC * T] for u in range(U)]
        turn_h = [k.banks[3 + u // 2][:, (u % 2) * 256:(u % 2) * 256 + DC * T] for u in range(U)]
        qk_ps = k.banks[6]
        hist = k.banks[7][0:T, 0:NT]

        with nc.Block() as block:
            @block.sync
            def _(sp):
                def load(to, what, sem):
                    sp.dma_start(to, what).then_inc(sem, 16)
                for dst, edges in ((src_n, d["src"]), (dst_n, d["dst"])):
                    load(dst[:], edges.rearrange("(j q e) -> q j e", q=EQ, e=T), s["edges_in"])
                for p0, p1 in ((0, SPLIT), (SPLIT, T)):
                    load(r.acc[p0:p1], d["x"].rearrange("(i p) d -> p i d", p=T)[p0:p1], s["x_in"])
                load(a.wx[:], d["mix_Wx"].rearrange("(c p) n -> p c n", p=128), s["mix_in"])
                for at, what in ((0, d["mix_bx"]), (2, d["mix_ln1_g"]), (4, d["mix_ln1_b"]), (6, d["mix_ln2_g"]), (8, d["mix_ln2_b"]),
                                 (10, d["mix_b1"]), (18, d["gnn_b_gc"]), (20, d["gnn_b_res"])):
                    pieces = what.rearrange("(c p) -> c p", p=128)
                    load(bias_rows[at:at + pieces.shape[0], :], pieces, s["mix_in"])
                sp.wait_ge(s["blockdiag"], 1)
                for c in range(DC):
                    for q in range(128 // DH):
                        at, head = slice(DH * q, DH * (q + 1)), 4 * c + q
                        load(blockdiag_qk[at, c, KR * head:KR * (head + 1)], d["mix_Wq"], s["mix_in"])
                        load(blockdiag_qk[at, c, HR + KR * head:HR + KR * (head + 1)], d["mix_Wk"], s["mix_in"])
                for q in range(128 // DH):
                    load(a.wv[DH * q:DH * (q + 1), DH * q:DH * (q + 1)], d["mix_Wv"], s["rest_in"])
                for p0, p1 in ((0, SPLIT), (SPLIT, T)):
                    load(a.b2_bc[p0:p1], d["mix_b2"].partition_broadcast(p1 - p0), s["rest_in"])
                    load(a.beta_bc[p0:p1], d["gnn_beta"].partition_broadcast(p1 - p0), s["rest_in"])
                    load(a.bg_bc[p0:p1], d["gnn_bg"].partition_broadcast(p1 - p0), s["rest_in"])
                load(a.g1_bc[:], d["mix_ln1_g"].partition_broadcast(HR), s["rest_in"])
                load(a.b1_bc[:], d["mix_ln1_b"].partition_broadcast(HR), s["rest_in"])
                load(a.bx_row[:], d["mix_bx"].rearrange("(o n) -> o n", o=1), s["rest_in"])
                load(a.m_aug[HR:HR + 1, :], d["mix_bo"].rearrange("(o n) -> o n", o=1), s["rest_in"])
                for to, what in ((a.wo, d["mix_Wo"]), (a.w_gc, d["gnn_W_gc"]), (a.w_res, d["gnn_W_res"]), (a.wg, d["gnn_Wg"])):
                    load(to[:], what.rearrange("(c p) n -> p c n", p=128), s["rest_in"])
                rest = 4 + 6 + 4 + 4
                for layer, used in zip(layers, (2 * CAP // B, 2 * N // B)):
                    rows_out = layer.outputs.rearrange("(m p) d -> p m d", p=B)[:, used:, :]
                    sp.dma_start(rows_out, blank[:].unsqueeze(1).broadcast_to([B, rows_out.shape[1], D])).then_inc(s["blanked"], 16)
                sp.sem_inc(s["h_stored"], 32)
                with sp.Fori(0, NG) as g:
                    sp.wait_ge(s["h_ready"], U * g + U)
                    for p0, p1 in ((0, SPLIT), (SPLIT, T)):
                        sp.dma_start(rows_of(a.h_dram, g)[p0:p1], h_out[p0:p1]).then_inc(s["h_stored"], 16)
                sp.wait_ge(s["h_stored"], 32 * NG + 32)
                sp.wait_ge(s["blanked"], 32)
                sp.wait_ge(s["mix_in"], 16 * (1 + 8 + 4 * 2 * DC))
                sp.wait_ge(s["rest_in"], 16 * rest)
                sp.wait_ge(s["x_in"], 32)
                sp.wait_ge(s["edges_in"], 32)

            @block.gpsimd
            def _(pool):
                nc.gpsimd.memset(blank[:], 0.0)
                nc.gpsimd.memset(blockdiag_qk[:], 0.0)
                nc.gpsimd.memset(a.wv[:], 0.0).then_inc(s["blockdiag"], 1)
                nc.gpsimd.iota(count_lo[:], pattern=[[1, T], [0, HG]], base=0, channel_multiplier=0,
                               allow_small_or_imprecise_dtypes=True)
                nc.gpsimd.iota(count_hi[:], pattern=[[1, NT], [0, HG]], base=0, channel_multiplier=0,
                               allow_small_or_imprecise_dtypes=True).then_inc(s["tables"], 1)
                pool.sem_inc(s["xn_free"], U)
                pool.sem_inc(s["hn_free"], U)
                with pool.Fori(0, NG) as g:
                    for u in range(U):
                        pool.wait_ge(s["xn_ready"], U * g + u + 1)
                        nc.gpsimd.tensor_copy(r.nodes[:, ds(U * g + u, 1), :], xn[:, u:u + 1, :]).then_inc(s["xn_free"], 1)

            @block.vector
            def _(dve):
                steps = [0]

                def then(ins):
                    steps[0] += 1
                    ins.then_inc(s["ids_step"], 1)
                    dve.wait_ge(s["ids_step"], steps[0])

                nc.vector.memset(a.src_idx[:], 0)
                nc.vector.memset(a.visit_tab[:], 0)
                then(nc.vector.memset(a.dst_t[:], -1.0))
                dve.wait_ge(s["edges_in"], 32)
                nc.vector.tensor_copy(src_f[:], src_n[:]).then_inc(s["edges_float"], 1)
                nc.vector.tensor_copy(dst_f[:], dst_n[:]).then_inc(s["edges_float"], 1)
                dve.wait_ge(s["edge_columns"], 2)
                nc.vector.tensor_copy(a.src_idx[:, 0:EC], k.banks[0][0:T, 0:EC])
                nc.vector.tensor_copy(src_t[:], k.banks[0][0:T, 0:EC])
                then(nc.vector.tensor_copy(a.dst_t[:, 0:EC], k.banks[1][0:T, 0:EC]))
                for ins in round_to_whole(nc, src_hi[:], src_t[:], 1.0 / T, -(T // 2) / T):
                    then(ins())
                nc.vector.tensor_copy(hi_b[:], src_hi[:])
                nc.vector.scalar_tensor_tensor(lo_b[:], src_hi[:], -float(T), src_t[:], ALU.mult, ALU.add).then_inc(s["ids"], 1)
                dve.wait_ge(s["ids"], 1)
                dve.wait_ge(s["tables"], 1)
                with dve.Fori(0, EC // HG // 2) as i:
                    for v in range(2):
                        at = ds((2 * i + v) * HG, HG)
                        dve.wait_ge(s["hist_free"], 2 * i + v + 1)
                        nc.vector.tensor_tensor(hot_lo[v][:], count_lo[:], lo_b[:, at].unsqueeze(1).broadcast_to([T, T, HG]), ALU.is_equal)
                        nc.vector.tensor_tensor(hot_hi[v][:], count_hi[:], hi_b[:, at].unsqueeze(1).broadcast_to([T, NT, HG]),
                                                ALU.is_equal).then_inc(s["hist_ready"], 1)
                dve.wait_ge(s["hist_free"], EC // HG + 2 + 1)
                nc.vector.tensor_scalar(degree[:], hist, 1.0, None, ALU.max).then_inc(s["degree"], 1)
                dve.wait_ge(s["degree_root"], 1)
                then(nc.vector.reciprocal(a.rs_out[:], degree[:]))
                nc.vector.tensor_reduce(reach[:, 0, :], dst_f[:], AX, ALU.min)
                then(nc.vector.tensor_reduce(reach[:, 1, :], dst_f[:], AX, ALU.max))
                for ins in round_to_whole(nc, reach[:], reach[:], 1.0 / T, -(T // 2) / T):
                    then(ins())
                nc.vector.tensor_copy(visit[:, 7:8], r.col[0:NT, :]).then_inc(s["chunk_range"], 1)
                dve.wait_ge(s["range_bc"], 1)
                block_no = r.col[0:NT, :]
                nc.vector.tensor_scalar(lo_c[:], k.banks[2][0:NT, 0:EC], block_no, None, ALU.is_le)
                then(nc.vector.tensor_scalar(hi_c[:], k.banks[3][0:NT, 0:EC], block_no, None, ALU.is_ge))
                then(nc.vector.tensor_tensor(lo_c[:], lo_c[:], hi_c[:], ALU.mult))
                then(nc.vector.scalar_tensor_tensor(hi_c[:], r.row[0:NT, 0:EC], -float(EC), lo_c[:], ALU.add, ALU.mult))
                then(nc.vector.tensor_reduce(visit[:, 0:1], hi_c[:], AX, ALU.min))
                then(nc.vector.tensor_scalar(visit[:, 0:1], visit[:, 0:1], float(EC), float(EC - 1), ALU.add, ALU.min))
                then(nc.vector.scalar_tensor_tensor(hi_c[:], r.row[0:NT, 0:EC], 1.0, lo_c[:], ALU.add, ALU.mult))
                then(nc.vector.tensor_reduce(visit[:, 1:2], hi_c[:], AX, ALU.max))
                then(nc.vector.tensor_tensor(visit[:, 1:2], visit[:, 1:2], visit[:, 0:1], ALU.subtract))
                then(nc.vector.tensor_scalar(visit[:, 1:2], visit[:, 1:2], 1.0, None, ALU.max))
                for ins in round_to_whole(nc, visit[:, 2:3], visit[:, 1:2], 1.0 / VU, (VU - 1) / (2.0 * VU)):
                    then(ins())
                nc.vector.tensor_copy(visit[:, 3:4], visit[:, 2:3]).then_inc(s["visit_step"], 1)
                dve.wait_ge(s["visit_row"], 1)
                nc.vector.tensor_copy(visit[:, 4:5], k.banks[4][0:NT, 0:1]).then_inc(s["visit_step"], 1)
                dve.wait_ge(s["visit_row"], 2)
                nc.vector.tensor_copy(a.visit_tab[0:1, 0, 0:NT], k.banks[5][0:1, 0:NT])
                nc.vector.tensor_copy(a.visit_tab[0:1, 1, 0:NT], k.banks[5][0:1, NT:2 * NT])
                nc.vector.tensor_copy(a.visit_tab[0:1, 2, 0:NT], k.banks[5][0:1, 2 * NT:3 * NT])
                dve.wait_ge(s["wx_turned"], 1)
                nc.vector.tensor_copy(a.cols[:], k.banks[0][:, 0:22])
                nc.vector.tensor_copy(wx_t[:], k.banks[6][:, 0:DC * D].rearrange("p (c n) -> p c n", c=DC)).then_inc(s["wx_copied"], 1)
                dve.wait_ge(s["folded"], 1)
                nc.vector.tensor_copy(wqk[:], k.banks[1][:, 0:DC * 2 * HR].rearrange("p (c n) -> p c n", c=DC))
                nc.vector.tensor_copy(bqk[:], k.banks[1][0:T, 256:256 + 2 * HR]).then_inc(s["qk_weights"], 1)
                dve.wait_ge(s["qk_weights"], 1)
                dve.wait_ge(s["x_in"], 32)

                def norm(g, tile, stats_sem, moments_sem, root_sem, inverse_sem):
                    for u in range(U):
                        nc.vector.bn_stats(stats[:, u, :], tile(u)).then_inc(stats_sem, 1)
                    dve.wait_ge(stats_sem, U * g + U)
                    dve.sem_inc(s["passed"], 1)
                    for u in range(U):
                        nc.vector.bn_aggr(moments[:, u, :], stats[:, u, :]).then_inc(moments_sem, 1)
                    dve.wait_ge(root_sem, g + 1)
                    nc.vector.reciprocal(root[:], root[:]).then_inc(inverse_sem, 1)
                    dve.wait_ge(inverse_sem, g + 1)

                def first_norm(g):
                    norm(g, lambda u: r.acc[:, ds(U * g + u, 1), :].rearrange("p o d -> p (o d)"), s["stats1"], s["moments1"], s["root1"], s["inverse1"])
                    dve.wait_ge(s["hnT_turned"], U * g + 1)
                    for u in range(U):
                        dve.wait_ge(s["xn_free"], U * g + u + 1)
                        nc.vector.tensor_scalar(xn[:, u:u + 1, :], r.acc[:, ds(U * g + u, 1), :], moments[:, u, 0:1], root[:, u:u + 1],
                                                ALU.subtract, ALU.mult).then_inc(s["xn_ready"], 1)

                def second_norm(g):
                    dve.wait_ge(s["xn_ready"], U * g + U)
                    norm(g, lambda u: xn[:, u, :], s["stats2"], s["moments2"], s["root2"], s["inverse2"])
                    for u in range(U):
                        dve.wait_ge(s["hn_free"], U * g + u + 1)
                        nc.vector.tensor_scalar(hn[:, u, :], xn[:, u, :], moments[:, u, 0:1], root[:, u:u + 1],
                                                ALU.subtract, ALU.mult).then_inc(s["hn_ready"], 1)

                def keep_turned(g):
                    dve.wait_ge(s["xnT_turned"], U * g + U)
                    for u in range(U):
                        nc.vector.tensor_copy(a.xnT[:, :, ds((U * g + u) * T, T)],
                                              turn_x[u].rearrange("p (c t) -> p c t", c=DC)).then_inc(s["xnT_kept"], 1)

                def keep_qk(g):
                    dve.wait_ge(s["qk_ready"], U * g + U)
                    nc.vector.tensor_tensor(a.qk[:, ds(U * g, U), :], qk_ps[0:T, 0:U * 2 * HR].rearrange("p (u n) -> p u n", u=U),
                                            bqk[:].unsqueeze(1).broadcast_to([T, U, 2 * HR]), ALU.add).then_inc(s["qk_kept"], 1)

                first_norm(0)
                second_norm(0)
                with dve.Fori(1, NG) as g:
                    first_norm(g)
                    keep_turned(g - 1)
                    second_norm(g)
                    keep_qk(g - 1)
                keep_turned(NG - 1)
                keep_qk(NG - 1)

            @block.scalar
            def _(act):
                act.wait_ge(s["degree"], 1)
                nc.scalar.activation(degree[:], degree[:], ACT.Sqrt).then_inc(s["degree_root"], 1)
                with act.Fori(0, NG) as g:
                    act.wait_ge(s["moments1"], U * g + U)
                    nc.scalar.activation(root[:], moments[:, :, 1], ACT.Sqrt, bias=r.eps[0:T, :]).then_inc(s["root1"], 1)
                    act.wait_ge(s["h_stored"], 32 * g + 32)
                    for u in range(U):
                        act.wait_ge(s["xn_ready"], U * g + u + 1)
                        nc.scalar.activation(h_out[:, u, :], xn[:, u, :], ACT.Copy,
                                             scale=a.rs_out[:, ds(U * g + u, 1)]).then_inc(s["h_ready"], 1)
                    act.wait_ge(s["moments2"], U * g + U)
                    nc.scalar.activation(root[:], moments[:, :, 1], ACT.Sqrt, bias=r.eps[0:T, :]).then_inc(s["root2"], 1)
                    for u in range(U):
                        act.wait_ge(s["hn_ready"], U * g + u + 1)
                        nc.scalar.activation(a.hn[:, ds(U * g + u, 1), :], hn[:, u:u + 1, :], ACT.Copy).then_inc(s["hn_free"], 1)
                    act.wait_ge(s["hnT_turned"], U * g + U + 1)
                    for u in range(U):
                        for c in range(DC):
                            done = nc.scalar.activation(hT[:, u, c, :], turn_h[u][:, c * T:(c + 1) * T], ACT.Identity,
                                                        scale=a.cols[:, 2 + c:3 + c], bias=a.cols[:, 4 + c:5 + c])
                        done.then_inc(s["hT_ready"], 1)

            @block.tensor
            def _(pe):
                for n, (edges, bank) in enumerate(((src_f, k.banks[0]), (dst_f, k.banks[1]))):
                    pe.wait_ge(s["edges_float"], n + 1)
                    for j in range(EJ):
                        done = nc.tensor.transpose(bank[0:T, j * EQ:(j + 1) * EQ], edges[:, j, :], r.ident[0:EQ, 0:EQ])
                    done.then_inc(s["edge_columns"], 1)
                pe.sem_inc(s["hist_free"], 2)
                nc.tensor.matmul(hist, r.zeros[0:T, 0:T], r.zeros[0:T, 0:NT], start=True, stop=False)
                with pe.Fori(0, EC // HG // 2) as i:
                    for v in range(2):
                        pe.wait_ge(s["hist_ready"], 2 * i + v + 1)
                        for j in range(HG):
                            done = nc.tensor.matmul(hist, hot_lo[v][:, :, j], hot_hi[v][:, :, j], start=False, stop=False)
                        done.then_inc(s["hist_free"], 1)
                nc.tensor.matmul(hist, r.zeros[0:T, 0:T], r.zeros[0:T, 0:NT], start=False, stop=True).then_inc(s["hist_free"], 1)
                pe.wait_ge(s["chunk_range"], 1)
                for way in range(2):
                    for j in range(EJ):
                        done = nc.tensor.matmul(k.banks[2 + way][0:NT, j * EQ:(j + 1) * EQ],
                                                reach[:, way, j:j + 1].broadcast_to([EQ, NT]), r.ident[0:EQ, 0:EQ], start=True, stop=True)
                done.then_inc(s["range_bc"], 1)
                pe.wait_ge(s["visit_step"], 1)
                nc.tensor.matmul(k.banks[4][0:NT, 0:1], r.tril_f[0:NT, 0:NT], visit[:, 2:3], start=True, stop=True).then_inc(s["visit_row"], 1)
                pe.wait_ge(s["visit_step"], 2)
                for n, what in enumerate((visit[:, 4:5], visit[:, 0:1], visit[:, 2:3])):
                    done = nc.tensor.matmul(k.banks[5][0:1, n * NT:(n + 1) * NT], what, r.ident[0:NT, 0:NT], start=True, stop=True)
                done.then_inc(s["visit_row"], 1)
                pe.wait_ge(s["mix_in"], 16 * (1 + 8 + 4 * 2 * DC))
                nc.tensor.transpose(k.banks[0][:, 0:22], bias_rows[:], r.ident[0:22, 0:22])
                for n in range(DC):
                    for c in range(DC):
                        done = nc.tensor.transpose(k.banks[6][:, n * D + c * 128:n * D + (c + 1) * 128], a.wx[:, c, n * 128:(n + 1) * 128], r.ident[:])
                done.then_inc(s["wx_turned"], 1)
                pe.wait_ge(s["wx_copied"], 1)
                for c in range(DC):
                    for n in range(DC):
                        nc.tensor.matmul(k.banks[1][:, c * 64:(c + 1) * 64], wx_t[:, n, c * 128:(c + 1) * 128], blockdiag_qk[:, n, :],
                                         start=n == 0, stop=n == DC - 1)
                for n in range(DC):
                    done = nc.tensor.matmul(k.banks[1][0:T, 256:256 + 2 * HR], a.cols[:, n:n + 1].broadcast_to([128, T]), blockdiag_qk[:, n, :],
                                            start=n == 0, stop=n == DC - 1)
                done.then_inc(s["folded"], 1)
                pe.wait_ge(s["qk_weights"], 1)
                pe.sem_inc(s["xnT_kept"], U)
                pe.sem_inc(s["qk_kept"], 1)
                pe.sem_inc(s["hnT_turned"], 1)
                with pe.Fori(0, NG) as g:
                    pe.wait_ge(s["xnT_kept"], U * g + U)
                    pe.sem_inc(s["passed"], 1)
                    for u in range(U):
                        pe.wait_ge(s["xn_ready"], U * g + u + 1)
                        for c in range(DC):
                            done = nc.tensor.transpose(turn_x[u][:, c * T:(c + 1) * T], xn[:, u, c * 128:(c + 1) * 128], r.ident[0:T, 0:T])
                        done.then_inc(s["xnT_turned"], 1)
                    for u in range(U):
                        pe.wait_ge(s["hn_ready"], U * g + u + 1)
                        for c in range(DC):
                            done = nc.tensor.transpose(turn_h[u][:, c * T:(c + 1) * T], hn[:, u, c * 128:(c + 1) * 128], r.ident[0:T, 0:T])
                        done.then_inc(s["hnT_turned"], 1)
                    pe.wait_ge(s["qk_kept"], g + 1)
                    pe.sem_inc(s["passed"], 1)
                    for u in range(U):
                        pe.wait_ge(s["hT_ready"], U * g + u + 1)
                        for c in range(DC):
                            done = nc.tensor.matmul(qk_ps[0:T, 64 * u:64 * u + 64], hT[:, u, c, :], wqk[:, c, :], start=c == 0, stop=c == DC - 1)
                        done.then_inc(s["qk_ready"], 1)


def attention_state(nc, d, r, a):
    names = ("step act_step pe_step summed bias_added weights_in")
    with phase(nc, "state", names) as k:
        s, sb = k.s, k.sb
        q_max, q_sum = sb("q_max", [T, NT, HEADS]), sb("q_sum", [T, NT, HEADS])
        k_max, k_sum = sb("k_max", [T, HR]), sb("k_sum", [T, HR])
        k_top = sb("k_top", [HR, 1])
        k_max_bc = sb("k_max_bc", [T, HR])
        sum_col, inv_col, sum_row = sb("sum_col", [HR, 1]), sb("inv_col", [HR, 1]), sb("sum_row", [1, HR])
        gt = sb("gt", [HR, D])
        gh, xm, kv = (sb(n, [128, DC, HR]) for n in ("gh", "xm", "kv"))
        own = sb("own", [128, DC, HR])
        state = k.banks[0][0:HR, 0:D]
        q_part = a.qk[:, :, 0:HR].rearrange("p i (h r) -> p i h r", h=HEADS)
        k_part = a.qk[:, :, HR:2 * HR]
        by_head = lambda t: t[:].unsqueeze(3).broadcast_to([T, NT, HEADS, KR])

        with nc.Block() as block:
            @block.sync
            def _(sp):
                for to, what in ((a.w1, d["mix_W1"]), (a.w2, d["mix_W2"])):
                    sp.dma_start(to[:], what.rearrange("(c p) n -> p c n", p=128)).then_inc(s["weights_in"], 16)
                sp.wait_ge(s["weights_in"], 32)

            @block.gpsimd
            def _(pool):
                nc.gpsimd.tensor_tensor(a.b2_bc[:], a.b2_bc[:], a.beta_bc[:], ALU.add).then_inc(s["bias_added"], 1)
                pool.wait_ge(s["bias_added"], 1)
                nc.gpsimd.tensor_tensor(r.acc[:], r.acc[:], a.b2_bc[:].unsqueeze(1).broadcast_to([T, NT, D]), ALU.add).then_inc(s["bias_added"], 1)

            @block.vector
            def _(dve):
                steps = [0]

                def then(ins):
                    steps[0] += 1
                    ins.then_inc(s["step"], 1)
                    dve.wait_ge(s["step"], steps[0])

                nc.vector.tensor_reduce(q_max[:], q_part, AX, ALU.max)
                then(nc.vector.tensor_reduce(k_max[:], k_part.rearrange("p i n -> p n i"), AX, ALU.max))
                nc.vector.tensor_tensor(q_part, q_part, by_head(q_max), ALU.subtract)
                dve.wait_ge(s["pe_step"], 1)
                then(nc.vector.tensor_reduce(k_top[:], k.banks[1][0:HR, 0:T], AX, ALU.max))
                dve.wait_ge(s["pe_step"], 2)
                then(nc.vector.tensor_copy(k_max_bc[:], k.banks[2][0:T, 0:HR]))
                then(nc.vector.tensor_tensor(k_part, k_part, k_max_bc[:].unsqueeze(1).broadcast_to([T, NT, HR]), ALU.subtract))
                nc.vector.memset(own[:], 0.0)
                dve.wait_ge(s["act_step"], 1)
                then(nc.vector.tensor_reduce(k_sum[:], k_part.rearrange("p i n -> p n i"), AX, ALU.add))
                then(nc.vector.tensor_reduce(q_sum[:], q_part, AX, ALU.add))
                then(nc.vector.reciprocal(q_sum[:], q_sum[:]))
                for c in range(DC):
                    for q in range(128 // DH):
                        head = 4 * c + q
                        nc.vector.memset(own[DH * q:DH * (q + 1), c, KR * head:KR * (head + 1)], 1.0)
                then(nc.vector.tensor_tensor(q_part, q_part, by_head(q_sum), ALU.mult))
                dve.wait_ge(s["summed"], 1)
                nc.vector.tensor_copy(sum_col[:], k.banks[1][0:HR, 128:129])
                nc.vector.tensor_copy(sum_row[:], k.banks[1][0:1, 256:256 + HR])
                then(nc.vector.tensor_tensor(gt[:], state, a.g1_bc[:], ALU.mult))
                nc.vector.reciprocal(inv_col[:], sum_col[:])
                then(nc.vector.scalar_tensor_tensor(gt[:], a.b1_bc[:], sum_col[:], gt[:], ALU.mult, ALU.add))
                for n, to in ((3, gh), (4, xm)):
                    dve.wait_ge(s["pe_step"], n)
                    then(nc.vector.tensor_copy(to[:], k.banks[n][:, 0:DC * HR].rearrange("p (c n) -> p c n", c=DC)))
                dve.wait_ge(s["pe_step"], 5)
                then(nc.vector.tensor_tensor(kv[:], k.banks[5][:, 0:DC * HR].rearrange("p (c n) -> p c n", c=DC), own[:], ALU.mult))
                dve.wait_ge(s["pe_step"], 6)
                then(nc.vector.tensor_scalar(a.m_aug[0:HR, :], k.banks[6][0:HR, 0:D], inv_col[:], None, ALU.mult))

            @block.scalar
            def _(act):
                act.wait_ge(s["step"], 4)
                nc.scalar.activation(a.qk[:], a.qk[:], ACT.Exp).then_inc(s["act_step"], 1)

            @block.tensor
            def _(pe):
                pe.wait_ge(s["step"], 1)
                nc.tensor.transpose(k.banks[1][0:HR, 0:T], k_max[:], r.ident[0:T, 0:T]).then_inc(s["pe_step"], 1)
                pe.wait_ge(s["step"], 2)
                nc.tensor.matmul(k.banks[2][0:T, 0:HR], k_top[:].broadcast_to([HR, T]), r.ident[0:HR, 0:HR],
                                 start=True, stop=True).then_inc(s["pe_step"], 1)
                pe.wait_ge(s["act_step"], 1)
                for i in range(NT):
                    nc.tensor.matmul(state, a.qk[:, i, HR:2 * HR], a.hn[:, i, :], start=i == 0, stop=i == NT - 1)
                pe.wait_ge(s["step"], 5)
                nc.tensor.matmul(k.banks[1][0:HR, 128:129], k_sum[:], r.ones[:, 0:1], start=True, stop=True)
                nc.tensor.matmul(k.banks[1][0:1, 256:256 + HR], r.ones[:, 0:1], k_sum[:], start=True, stop=True).then_inc(s["summed"], 1)
                pe.wait_ge(s["step"], 10)
                for c in range(DC):
                    done = nc.tensor.transpose(k.banks[3][:, c * HR:(c + 1) * HR], gt[:, c * 128:(c + 1) * 128], r.ident[0:HR, 0:HR])
                done.then_inc(s["pe_step"], 1)
                pe.wait_ge(s["step"], 11)
                for n in range(DC):
                    out = k.banks[4][:, n * HR:(n + 1) * HR]
                    for c in range(DC):
                        nc.tensor.matmul(out, a.wx[:, c, n * 128:(n + 1) * 128], gh[:, c, :], start=c == 0, stop=False)
                    done = nc.tensor.matmul(out, a.bx_row[0:1, n * 128:(n + 1) * 128], sum_row[0:1, :], start=False, stop=True)
                done.then_inc(s["pe_step"], 1)
                pe.wait_ge(s["step"], 12)
                for n in range(DC):
                    done = nc.tensor.matmul(k.banks[5][:, n * HR:(n + 1) * HR], a.wv[:], xm[:, n, :], start=True, stop=True)
                done.then_inc(s["pe_step"], 1)
                pe.wait_ge(s["step"], 13)
                for n in range(DC):
                    done = nc.tensor.matmul(k.banks[6][0:HR, 0:D], kv[:, n, :], a.wo[:, n, :], start=n == 0, stop=n == DC - 1)
                done.then_inc(s["pe_step"], 1)


def by_set(eng, step, body):
    def choose(bit, found):
        if bit == SETS:
            body(found)
            return
        with eng.If(eng.snap(step & bit) == 0):
            choose(2 * bit, found)
        with eng.Else():
            choose(2 * bit, found + bit)
    choose(1, 0)


def chunk_at(first, step):
    return (first + VU * step).with_bounds(min_val=0, max_val=EC - 1)


def graph_and_mix(nc, d, r, a, q, p):
    names = ("idx_ready passed visited hot_ready mix_added"
             " ones_in sums_ready inv_degree deg_clipped deg_root mean_ready meanT_ready meanT_kept xgT_ready xgT_kept"
             " xg_kept xg_stored logits_ready logits_kept top_found id_found chosen"
             " q_staged qT_ready qT_kept attn_ready fx_ready fx_stats fx_moments fx_root fx_inverse h2_ready h2T_ready h2T_kept"
             " up_ready hidden_ready down_ready down_added") + "".join(f" row_in{n}" for n in range(SETS * VU))
    with phase(nc, "graph", names) as k:
        s, sb = k.s, k.sb
        gathered = [s[f"row_in{n}"] for n in range(SETS * VU)]
        rows = a.hn[:].rearrange("p i d -> p (i d)")[:, 0:SETS * VU * (D + 2)].rearrange("p (n d) -> p n d", n=SETS * VU)
        hot = [sb(f"hot{n}", [T, VU, T]) for n in range(SETS)]
        idx = [sb(f"idx{n}", [T, VU], I32) for n in range(SETS)]
        base = sb("base", [T, NT])
        bias_gc = sb("bias_gc", [128, DC])
        inv_deg = sb("inv_deg", [T, 1])
        deg_root = sb("deg_root", [T, 1])
        mean = sb("mean", [T, D])
        meanT = sb("meanT", [128, DC, T])
        xgT = sb("xgT", [128, DC, T])
        qs = sb("qs", [T, U, HR + 1])
        qT = sb("qT", [HR + 1, U, T])
        fx = sb("fx", [T, U, D])
        h2T = sb("h2T", [128, DC, U * T])
        hidden_all = sb("hidden", [128, FC * U * T])
        hidden = hidden_all[:].rearrange("p (m t) -> p m t", m=FC)
        h2 = hidden_all[0:T, 0:U * D].rearrange("p (u d) -> p u d", u=U)
        stats, moments, root = sb("stats", [T, U, 6]), sb("moments", [T, U, 2]), sb("root", [T, U])
        logits_s, top_s, top_id_s = sb("logits_s", [T, U, E_GNN]), sb("top_s", [T, U, 8]), sb("top_id_s", [T, U, 8], U32)
        sums = [k.banks[n][0:T, 0:D + 2] for n in (0, 1, 0, 1, 7)]
        meanT_ps, xg_ps = k.banks[2][:, 0:DC * T], k.banks[2][0:T, 0:D]
        xgT_ps, logit_ps = k.banks[2][:, 256:256 + DC * T], k.banks[2][0:T, 256:256 + E_GNN]
        slot = [k.banks[(5, 5, 6, 6, 4)[u]][:, (0, 256, 0, 256, 256)[u]:][:, 0:256] for u in range(U)]
        wide = [k.wide[0][:], k.wide[1][:]]
        turn_q = [k.banks[3][0:HR + 1, u * T:(u + 1) * T] for u in range(4)] + [k.banks[4][0:HR + 1, 0:T]]
        tile3 = lambda t, i: t[:, ds(i, 1), :].rearrange("p o d -> p (o d)")

        with nc.Block() as block:
            @block.sync
            def _(sp):
                sp.sem_inc(s["xg_stored"], 32)
                with sp.Fori(0, NG) as g:
                    sp.wait_ge(s["xg_kept"], U * g + U)
                    for p0, p1 in ((0, SPLIT), (SPLIT, T)):
                        sp.dma_start(rows_of(q.tokens, g)[p0:p1], r.nodes[p0:p1, ds(U * g, U), :]).then_inc(s["xg_stored"], 16)
                sp.wait_ge(s["xg_stored"], 32 * NG + 32)

            @block.gpsimd
            def _(pool):
                pool.wait_ge(s["ones_in"], 1)
                with pool.Fori(0, NT) as b:
                    before = pool.value_load(a.visit_tab[0:1, 0, ds(b, 1)], min_val=0, max_val=NT * EC)
                    first = pool.value_load(a.visit_tab[0:1, 1, ds(b, 1)], min_val=0, max_val=EC - 1)
                    steps = pool.value_load(a.visit_tab[0:1, 2, ds(b, 1)], min_val=1, max_val=-(-EC // VU))
                    with pool.Fori(0, steps) as j:
                        v = pool.snap(before + j)
                        pool.wait_ge(s["visited"], v + 1)
                        pool.sem_inc(s["passed"], 1)

                        def fetch(n):
                            nc.gpsimd.tensor_copy(idx[n][:], a.src_idx[:, ds(chunk_at(first, j), VU)]).then_inc(s["idx_ready"], 1)
                            pool.wait_ge(s["idx_ready"], v + 1)
                            pool.sem_inc(s["passed"], 1)
                            for u in range(VU):
                                nc.gpsimd.indirect_dma_start(
                                    out=rows[:, VU * n + u, 0:D], out_offset=None, in_=a.h_dram[:, :],
                                    in_offset=bass.IndirectOffsetOnAxis(ap=idx[n][:, u:u + 1], axis=0)).then_inc(gathered[VU * n + u], 16)
                        by_set(pool, v, fetch)

            @block.vector
            def _(dve):
                nc.vector.memset(rows[:, :, D:D + 2], 1.0).then_inc(s["ones_in"], 1)
                nc.vector.memset(qs[:], 1.0)
                nc.vector.tensor_scalar(base[:], r.row[0:T, 0:NT], float(T), None, ALU.mult)
                nc.vector.tensor_tensor(bias_gc[:], a.cols[:, 18:20], a.cols[:, 20:22], ALU.add).then_inc(s["ones_in"], 1)
                dve.wait_ge(s["ones_in"], 2)
                dve.sem_inc(s["down_added"], 1)

                def hot_of_block(g, u):
                    b = U * g + u
                    before = dve.value_load(a.visit_tab[0:1, 0, ds(b, 1)], min_val=0, max_val=NT * EC)
                    first = dve.value_load(a.visit_tab[0:1, 1, ds(b, 1)], min_val=0, max_val=EC - 1)
                    steps = dve.value_load(a.visit_tab[0:1, 2, ds(b, 1)], min_val=1, max_val=-(-EC // VU))
                    with dve.Fori(0, steps) as j:
                        v = dve.snap(before + j)
                        dve.wait_ge(s["visited"], v + 1)

                        def mark(n):
                            nc.vector.scalar_tensor_tensor(
                                hot[n][:], r.row[0:T, 0:T].unsqueeze(1).broadcast_to([T, VU, T]), base[:, ds(b, 1)],
                                a.dst_t[:, ds(chunk_at(first, j), VU)].unsqueeze(2).broadcast_to([T, VU, T]),
                                ALU.add, ALU.is_equal).then_inc(s["hot_ready"], 1)
                        by_set(dve, v, mark)

                def mean_of_block(g, u):
                    i = U * g + u
                    dve.wait_ge(s["sums_ready"], i + 1)
                    nc.vector.tensor_scalar(inv_deg[:], sums[u][:, D:D + 1], 1.0, None, ALU.max).then_inc(s["deg_clipped"], 1)
                    dve.wait_ge(s["deg_root"], i + 1)
                    nc.vector.reciprocal(inv_deg[:], deg_root[:]).then_inc(s["inv_degree"], 1)
                    dve.wait_ge(s["inv_degree"], i + 1)
                    nc.vector.tensor_scalar(mean[:], sums[u][:, 0:D], inv_deg[:], None, ALU.mult).then_inc(s["mean_ready"], 1)

                def turned_mean_of_block(g, u):
                    i = U * g + u
                    dve.wait_ge(s["meanT_ready"], i + 1)
                    nc.vector.tensor_copy(meanT[:].rearrange("p c t -> p (c t)"), meanT_ps).then_inc(s["meanT_kept"], 1)

                def tokens_of_block(g, u):
                    i = U * g + u
                    dve.wait_ge(s["logits_ready"], i + 1)
                    dve.sem_inc(s["passed"], 1)
                    nc.vector.tensor_copy(tile3(r.nodes, i), xg_ps).then_inc(s["xg_kept"], 1)
                    nc.vector.tensor_tensor(logits_s[:, u, :], logit_ps, a.bg_bc[:], ALU.add).then_inc(s["logits_kept"], 1)
                    dve.wait_ge(s["logits_kept"], i + 1)
                    dve.sem_inc(s["passed"], 1)
                    nc.vector.max(top_s[:, u, :], logits_s[:, u, :]).then_inc(s["top_found"], 1)
                    dve.wait_ge(s["top_found"], i + 1)
                    dve.sem_inc(s["passed"], 1)
                    nc.vector.max_index(top_id_s[:, u, :], top_s[:, u, :], logits_s[:, u, :]).then_inc(s["id_found"], 1)
                    dve.wait_ge(s["id_found"], i + 1)
                    dve.sem_inc(s["passed"], 1)
                    nc.vector.tensor_copy(tile3(q.top, i), top_s[:, u, 0:2])
                    nc.vector.tensor_copy(tile3(q.choice, i), top_id_s[:, u, 0:2]).then_inc(s["chosen"], 1)

                def stage_q(g):
                    for u in range(U):
                        nc.vector.tensor_copy(qs[:, u, 0:HR], a.qk[:, ds(U * g + u, 1), 0:HR].rearrange("p o n -> p (o n)")).then_inc(s["q_staged"], 1)

                def keep_q(g):
                    dve.wait_ge(s["qT_ready"], U * g + U)
                    for u in range(U):
                        nc.vector.tensor_copy(qT[:, u, :], turn_q[u]).then_inc(s["qT_kept"], 1)

                def residual(g):
                    dve.wait_ge(s["attn_ready"], U * g + U)
                    for u in range(U):
                        i = U * g + u
                        nc.vector.tensor_tensor(fx[:, u, :], slot[u][0:T, :], tile3(r.nodes, i), ALU.add).then_inc(s["fx_ready"], 1)
                    dve.wait_ge(s["fx_ready"], U * g + U)
                    dve.sem_inc(s["passed"], 1)
                    for u in range(U):
                        nc.vector.bn_stats(stats[:, u, :], fx[:, u, :]).then_inc(s["fx_stats"], 1)
                    dve.wait_ge(s["fx_stats"], U * g + U)
                    dve.sem_inc(s["passed"], 1)
                    for u in range(U):
                        nc.vector.bn_aggr(moments[:, u, :], stats[:, u, :]).then_inc(s["fx_moments"], 1)

                def normalised(g):
                    dve.wait_ge(s["fx_root"], g + 1)
                    nc.vector.reciprocal(root[:], root[:]).then_inc(s["fx_inverse"], 1)
                    dve.wait_ge(s["fx_inverse"], g + 1)
                    for u in range(U):
                        nc.vector.tensor_scalar(h2[:, u, :], fx[:, u, :], moments[:, u, 0:1], root[:, u:u + 1],
                                                ALU.subtract, ALU.mult).then_inc(s["h2_ready"], 1)

                def other_blocks(g, following):
                    hot_of_block(g, 1)
                    mean_of_block(g, 0)
                    turned_mean_of_block(g, 0)
                    residual(g)
                    hot_of_block(g, 2)
                    tokens_of_block(g, 0)
                    normalised(g)
                    mean_of_block(g, 1)
                    turned_mean_of_block(g, 1)
                    for u in (3, 4):
                        hot_of_block(g, u)
                        tokens_of_block(g, u - 2)
                        mean_of_block(g, u - 1)
                        turned_mean_of_block(g, u - 1)
                    if following is not None:
                        stage_q(following)
                        hot_of_block(following, 0)
                    tokens_of_block(g, 3)
                    if following is not None:
                        keep_q(following)
                    mean_of_block(g, 4)
                    turned_mean_of_block(g, 4)
                    dve.wait_ge(s["down_ready"], U * g + U)
                    for u in range(U):
                        nc.vector.tensor_tensor(fx[:, u, :], slot[u][0:T, :], fx[:, u, :], ALU.add).then_inc(s["down_added"], 1)
                    for u in range(U):
                        i = U * g + u
                        dve.wait_ge(s["down_added"], i + 2)
                        nc.vector.tensor_tensor(tile3(r.acc, i), tile3(r.acc, i), fx[:, u, :], ALU.add).then_inc(s["mix_added"], 1)
                    tokens_of_block(g, 4)

                stage_q(0)
                keep_q(0)
                hot_of_block(0, 0)
                with dve.Fori(0, NG - 1) as g:
                    other_blocks(g, g + 1)
                other_blocks(NG - 1, None)

            @block.scalar
            def _(act):
                with act.Fori(0, NG) as g:
                    def degree_root(u):
                        act.wait_ge(s["deg_clipped"], U * g + u + 1)
                        nc.scalar.activation(deg_root[:], inv_deg[:], ACT.Sqrt).then_inc(s["deg_root"], 1)

                    def tokens_of_block(u):
                        act.wait_ge(s["xgT_ready"], U * g + u + 1)
                        for c in range(DC):
                            done = nc.scalar.activation(xgT[:, c, :], xgT_ps[:, c * T:(c + 1) * T], ACT.Identity, bias=bias_gc[:, c:c + 1])
                        done.then_inc(s["xgT_kept"], 1)

                    def hidden_chunks(chunks):
                        for m in chunks:
                            act.wait_ge(s["up_ready"], FC * g + m + 1)
                            nc.scalar.activation(hidden[:, m, :], wide[m % 2][:, 0:U * T], ACT.Gelu,
                                                 bias=a.cols[:, 10 + m:11 + m]).then_inc(s["hidden_ready"], 1)

                    degree_root(0)
                    tokens_of_block(0)
                    act.wait_ge(s["fx_moments"], U * g + U)
                    nc.scalar.activation(root[:], moments[:, :, 1], ACT.Sqrt, bias=r.eps[0:T, :]).then_inc(s["fx_root"], 1)
                    degree_root(1)
                    act.wait_ge(s["h2T_ready"], U * g + U)
                    for w in range(U):
                        for c in range(DC):
                            done = nc.scalar.activation(h2T[:, c, w * T:(w + 1) * T], slot[w][:, c * T:(c + 1) * T],
                                                        ACT.Identity, scale=a.cols[:, 6 + c:7 + c], bias=a.cols[:, 8 + c:9 + c])
                        done.then_inc(s["h2T_kept"], 1)
                    tokens_of_block(1)
                    hidden_chunks(range(0, 4))
                    degree_root(2)
                    hidden_chunks(range(4, 6))
                    tokens_of_block(2)
                    hidden_chunks(range(6, 8))
                    for u in (3, 4):
                        degree_root(u)
                        tokens_of_block(u)

            @block.tensor
            def _(pe):
                pe.wait_ge(s["ones_in"], 2)
                pe.sem_inc(s["visited"], SETS)
                def visit_block(g, u):
                    b = U * g + u
                    before = pe.value_load(a.visit_tab[0:1, 0, ds(b, 1)], min_val=0, max_val=NT * EC)
                    steps = pe.value_load(a.visit_tab[0:1, 2, ds(b, 1)], min_val=1, max_val=-(-EC // VU))
                    pe.wait_ge(s["hot_ready"], before + 1)
                    nc.tensor.matmul(sums[u], r.zeros[0:T, 0:T], r.zeros[0:T, 0:D + 2], start=True, stop=False)
                    with pe.Fori(0, steps) as j:
                        v = pe.snap(before + j)
                        pe.wait_ge(s["hot_ready"], v + 1)

                        def add(n):
                            for c in range(VU):
                                pe.wait_ge(gathered[VU * n + c], ((v >> SET_BITS) + 1) * 16)
                                done = nc.tensor.matmul(sums[u], hot[n][:, c, :], rows[:, VU * n + c, :], start=False, stop=False)
                            done.then_inc(s["visited"], 1)
                        by_set(pe, v, add)
                    nc.tensor.matmul(sums[u], r.zeros[0:T, 0:T], r.zeros[0:T, 0:D + 2], start=False, stop=True).then_inc(s["sums_ready"], 1)

                def turn_mean(g, u):
                    pe.wait_ge(s["mean_ready"], U * g + u + 1)
                    for c in range(DC):
                        done = nc.tensor.transpose(meanT_ps[:, c * T:(c + 1) * T], mean[:, c * 128:(c + 1) * 128], r.ident[0:T, 0:T])
                    done.then_inc(s["meanT_ready"], 1)

                def tokens_turned(g, u):
                    i = U * g + u
                    pe.wait_ge(s["meanT_kept"], i + 1)
                    for n in range(DC):
                        out = xgT_ps[:, n * T:(n + 1) * T]
                        for c in range(DC):
                            nc.tensor.matmul(out, a.w_res[:, c, n * 128:(n + 1) * 128], a.xnT[:, c, ds(i * T, T)], start=c == 0, stop=False)
                        for c in range(DC):
                            done = nc.tensor.matmul(out, a.w_gc[:, c, n * 128:(n + 1) * 128], meanT[:, c, :], start=False, stop=c == DC - 1)
                    done.then_inc(s["xgT_ready"], 1)

                def tokens_and_logits(g, u):
                    pe.wait_ge(s["xgT_kept"], U * g + u + 1)
                    for c in range(DC):
                        nc.tensor.transpose(xg_ps[:, c * 128:(c + 1) * 128], xgT[:, c, :], r.ident[:])
                    for c in range(DC):
                        done = nc.tensor.matmul(logit_ps, xgT[:, c, :], a.wg[:, c, :], start=c == 0, stop=c == DC - 1)
                    done.then_inc(s["logits_ready"], 1)

                def up(g, chunks):
                    for m in chunks:
                        if m >= 2:
                            pe.wait_ge(s["hidden_ready"], FC * g + m - 1)
                        for lo, hi in ((0, 512), (512, U * T)):
                            for c in range(DC):
                                done = nc.tensor.matmul(wide[m % 2][:, lo:hi], a.w1[:, c, m * 128:(m + 1) * 128], h2T[:, c, lo:hi],
                                                        start=c == 0, stop=c == DC - 1)
                        done.then_inc(s["up_ready"], 1)

                def down(g, tiles):
                    for u in tiles:
                        for m in range(FC):
                            done = nc.tensor.matmul(slot[u][0:T, :], hidden[:, m, u * T:(u + 1) * T], a.w2[:, m, :], start=m == 0, stop=m == FC - 1)
                        done.then_inc(s["down_ready"], 1)

                def turn_q_of(g):
                    for u in range(U):
                        pe.wait_ge(s["q_staged"], U * g + u + 1)
                        pe.sem_inc(s["passed"], 1)
                        nc.tensor.transpose(turn_q[u], qs[:, u, :], r.ident[0:T, 0:T]).then_inc(s["qT_ready"], 1)

                def attention(g):
                    pe.wait_ge(s["down_added"], U * g + 1)
                    pe.sem_inc(s["passed"], 1)
                    for u in range(U):
                        pe.wait_ge(s["qT_kept"], U * g + u + 1)
                        nc.tensor.matmul(slot[u][0:T, :], qT[:, u, :], a.m_aug[:], start=True, stop=True).then_inc(s["attn_ready"], 1)

                def other_blocks(g, following):
                    visit_block(g, 1)
                    turn_mean(g, 0)
                    tokens_turned(g, 0)
                    tokens_and_logits(g, 0)
                    visit_block(g, 2)
                    for u in range(U):
                        pe.wait_ge(s["h2_ready"], U * g + u + 1)
                        for c in range(DC):
                            done = nc.tensor.transpose(slot[u][:, c * T:(c + 1) * T], h2[:, u, c * 128:(c + 1) * 128], r.ident[0:T, 0:T])
                        done.then_inc(s["h2T_ready"], 1)
                    turn_mean(g, 1)
                    tokens_turned(g, 1)
                    pe.wait_ge(s["h2T_kept"], U * g + U)
                    up(g, range(0, 2))
                    tokens_and_logits(g, 1)
                    up(g, range(2, 4))
                    visit_block(g, 3)
                    turn_mean(g, 2)
                    up(g, range(4, 6))
                    tokens_turned(g, 2)
                    up(g, range(6, 8))
                    tokens_and_logits(g, 2)
                    visit_block(g, 4)
                    turn_mean(g, 3)
                    pe.wait_ge(s["hidden_ready"], FC * g + FC)
                    down(g, [0])
                    tokens_turned(g, 3)
                    down(g, [1])
                    tokens_and_logits(g, 3)
                    down(g, [2])
                    if following is not None:
                        turn_q_of(following)
                        visit_block(following, 0)
                    turn_mean(g, 4)
                    down(g, [3])
                    tokens_turned(g, 4)
                    if following is not None:
                        pe.wait_ge(s["qT_kept"], U * following + U)
                    down(g, [4])
                    tokens_and_logits(g, 4)
                    if following is not None:
                        attention(following)

                turn_q_of(0)
                visit_block(0, 0)
                attention(0)
                with pe.Fori(0, NG - 1) as g:
                    other_blocks(g, g + 1)
                other_blocks(NG - 1, None)


def route(nc, name, r, q, experts, cap, dense):
    names = "passed step act_step pe_step top_found id_found chosen marked placed halves_ready halves_free gated gates_spread counted hi_ready rows_ready rows_kept"
    cut = CUTS[experts]
    blocks, wide = cut.blocks, cut.wide
    loads = cut.loads + cut.unroll
    E = experts
    with phase(nc, name, names) as k:
        s, sb = k.s, k.sb
        top, choice = q.top, q.choice
        if dense:
            top_s, top_id_s = sb("top_s", [T, NT, 8]), sb("top_id_s", [T, NT, 8], U32)
        hot = [sb(f"hot{v}", [T, NT, E], BF16) for v in range(2)]
        both = sb("both", [T, NT, E], BF16)
        run = [sb(f"run{v}", [T, NT, E], BF16) for v in range(2)]
        rank, part = sb("rank", [T, NT, E]), sb("part", [T, NT, E])
        start_bc = sb("start_bc", [T, E])
        col = sb("col", [E, 8])
        ended = sb("ended", [E, loads])
        place = sb("place", [T, NT, 2])
        first, order, fits, slot = (sb(n, [T, NT, 2]) for n in ("first", "order", "fits", "slot"))
        slot_hi = sb("slot_hi", [T, 2 * NT])
        hi_b, lo_b, tile_b = (sb(n, [T, 2 * NT], BF16) for n in ("hi_b", "lo_b", "tile_b"))
        line = sb("line", [1, loads])
        count_lo, count_hi = sb("count_lo", [T, B, U], BF16), sb("count_hi", [T, blocks, U], BF16)
        hot_lo = [sb(f"hot_lo{v}", [T, B, U], BF16) for v in range(2)]
        is_hi = [sb(f"is_hi{v}", [T, blocks, U], BF16) for v in range(2)]
        hot_hi = [sb(f"hot_hi{v}", [T, 2, blocks, U], BF16) for v in range(2)]
        token_rows = sb("token_rows", [B, blocks])
        big = sb("big", [T, NT])
        ranks = k.psum[0:T, 0:NT * E]
        table = k.banks[4][:, 0:2 * blocks]
        flat = lambda t: t[:].rearrange("p i e -> p (i e)")
        over = lambda t: t.unsqueeze(2).broadcast_to([T, NT, E])
        pick = lambda t, n: t[:, :, n:n + 1].broadcast_to([T, NT, E])

        with nc.Block() as block:
            @block.vector
            def _(dve):
                steps = [0]

                def then(ins):
                    steps[0] += 1
                    ins.then_inc(s["step"], 1)
                    dve.wait_ge(s["step"], steps[0])

                if dense:
                    then(nc.vector.tensor_reduce(big[:], q.logits[:], AX, ALU.max))
                    then(nc.vector.tensor_tensor(q.logits[:], q.logits[:], over(big[:]), ALU.subtract))
                    dve.wait_ge(s["act_step"], 1)
                    then(nc.vector.tensor_reduce(big[:], q.logits[:], AX, ALU.add))
                    then(nc.vector.reciprocal(big[:], big[:]))
                    then(nc.vector.tensor_tensor(q.logits[:], q.logits[:], over(big[:]), ALU.mult))
                    for i in range(NT):
                        nc.vector.max(top_s[:, i, :], q.logits[:, i, :]).then_inc(s["top_found"], 1)
                    dve.wait_ge(s["top_found"], NT)
                    for i in range(NT):
                        nc.vector.max_index(top_id_s[:, i, :], top_s[:, i, :], q.logits[:, i, :]).then_inc(s["id_found"], 1)
                    nc.vector.tensor_copy(top[:], top_s[:, :, 0:2]).then_inc(s["chosen"], 1)
                    dve.wait_ge(s["id_found"], NT)
                    nc.vector.tensor_copy(choice[:], top_id_s[:, :, 0:2]).then_inc(s["chosen"], 1)
                    dve.wait_ge(s["chosen"], 2)
                row = r.row[0:T, 0:E].unsqueeze(1).broadcast_to([T, NT, E])
                for n in range(2):
                    then(nc.vector.tensor_tensor(hot[n][:], row, pick(choice, n), ALU.is_equal))
                then(nc.vector.tensor_tensor(both[:], hot[0][:], hot[1][:], ALU.add))
                now = both
                for n, reach in enumerate((1, 2, 4, 8, 16)):
                    new = run[n % 2]
                    nc.vector.tensor_copy(new[:, 0:reach, :], now[:, 0:reach, :])
                    then(nc.vector.tensor_tensor(new[:, reach:, :], now[:, reach:, :], now[:, 0:NT - reach, :], ALU.add))
                    now = new
                nc.vector.tensor_copy(tile_b[:].rearrange("p (i n) -> p i n", n=2),
                                      r.row[0:T, 0:NT].unsqueeze(2).broadcast_to([T, NT, 2])).then_inc(s["marked"], 1)
                if dense:
                    nc.vector.tensor_copy(q.gates[:], top[:, :, 0:2])
                else:
                    then(nc.vector.tensor_tensor(q.gates[:, :, 1:2], top[:, :, 1:2], top[:, :, 0:1], ALU.subtract))
                    gate_step = steps[0]
                    dve.wait_ge(s["act_step"], 1)
                    then(nc.vector.tensor_scalar(q.gates[:, :, 0:1], q.gates[:, :, 1:2], 1.0, None, ALU.add))
                    then(nc.vector.reciprocal(q.gates[:, :, 0:1], q.gates[:, :, 0:1]))
                    then(nc.vector.tensor_tensor(q.gates[:, :, 1:2], q.gates[:, :, 1:2], q.gates[:, :, 0:1], ALU.mult))
                    q.gate_step = gate_step
                dve.wait_ge(s["pe_step"], 1)
                then(nc.vector.tensor_scalar(col[:, 0:1], k.banks[5][0:E, 0:1], float(cap), None, ALU.min))
                for ins in round_to_whole(nc, col[:, 1:2], col[:, 0:1], 1.0 / (B * wide), (B * wide - 1) / (2.0 * B * wide)):
                    then(ins())
                nc.vector.tensor_copy(col[:, 7:8], col[:, 1:2]).then_inc(s["placed"], 1)
                dve.wait_ge(s["pe_step"], 2)
                then(nc.vector.tensor_copy(col[:, 2:3], k.banks[5][0:E, 8:9]))
                then(nc.vector.tensor_tensor(col[:, 3:4], col[:, 2:3], col[:, 1:2], ALU.add))
                nc.vector.tensor_scalar(ended[:], r.row[0:E, 0:loads], col[:, 3:4], None, ALU.is_ge).then_inc(s["placed"], 1)
                dve.wait_ge(s["pe_step"], 3)
                then(nc.vector.tensor_copy(start_bc[:], k.banks[6][0:T, 0:E]))
                then(nc.vector.scalar_tensor_tensor(rank[:], start_bc[:].unsqueeze(1).broadcast_to([T, NT, E]), 8192.0,
                                                    ranks.rearrange("p (i e) -> p i e", e=E), ALU.mult, ALU.add))
                for n in range(2):
                    then(nc.vector.tensor_tensor(part[:], rank[:], hot[n][:], ALU.mult))
                    then(nc.vector.tensor_reduce(place[:, :, n], part[:], AX, ALU.add))
                for ins in round_to_whole(nc, first[:], place[:], 1.0 / 8192, -4095.5 / 8192):
                    then(ins())
                then(nc.vector.scalar_tensor_tensor(order[:], first[:], -8192.0, place[:], ALU.mult, ALU.add))
                then(nc.vector.tensor_scalar(fits[:], order[:], float(cap), None, ALU.is_lt))
                then(nc.vector.scalar_tensor_tensor(slot[:], first[:], float(B * wide), order[:], ALU.mult, ALU.add))
                then(nc.vector.scalar_tensor_tensor(slot[:], slot[:], 1.0, fits[:], ALU.add, ALU.mult))
                then(nc.vector.tensor_scalar(slot[:], slot[:], -1.0, None, ALU.add))
                nc.vector.tensor_tensor(q.gates[:], q.gates[:], fits[:], ALU.mult).then_inc(s["gated"], 1)
                nc.vector.tensor_scalar(q.slots[:], slot[:], 0.0, None, ALU.max)
                for ins in round_to_whole(nc, slot_hi[:], slot[:].rearrange("p i n -> p (i n)"), 1.0 / B, -(B / 2 - 0.5) / B):
                    then(ins())
                nc.vector.tensor_copy(hi_b[:], slot_hi[:])
                then(nc.vector.scalar_tensor_tensor(lo_b[:], slot_hi[:], -float(B), slot[:].rearrange("p i n -> p (i n)"), ALU.mult, ALU.add))
                dve.wait_ge(s["counted"], 1)
                with dve.Fori(0, NG) as g:
                    for v in range(2):
                        step = 2 * g + v
                        at = ds(U * step, U)
                        over_slots = lambda x, n: x[:, at].unsqueeze(1).broadcast_to([T, n, U])
                        dve.wait_ge(s["halves_free"], step + 1)
                        nc.vector.tensor_tensor(is_hi[v][:], count_hi[:], over_slots(hi_b, blocks), ALU.is_equal).then_inc(s["hi_ready"], 1)
                        nc.vector.tensor_tensor(hot_lo[v][:], count_lo[:], over_slots(lo_b, B), ALU.is_equal)
                        dve.wait_ge(s["hi_ready"], step + 1)
                        nc.vector.tensor_tensor(hot_hi[v][:, 0], is_hi[v][:], over_slots(tile_b, blocks), ALU.mult).then_inc(s["halves_ready"], 1)
                dve.wait_ge(s["pe_step"], 4)
                nc.vector.memset(q.token_of[:], 0)
                nc.vector.memset(q.same_of[:], 0)
                then(nc.vector.tensor_scalar(line[:], k.banks[7][0:1, 0:loads], float(E - 1), None, ALU.min))
                then(nc.vector.tensor_copy(q.expert_of[:], line[:]))
                nc.vector.tensor_tensor(q.same_of[:, 1:loads], line[:, 1:loads], line[:, 0:loads - 1], ALU.is_equal)
                nc.vector.tensor_scalar(token_rows[:], table[:, 0:blocks], float(T), None, ALU.mult).then_inc(s["rows_kept"], 1)
                dve.wait_ge(s["rows_kept"], 1)
                then(nc.vector.tensor_tensor(q.token_of[:, 0:blocks], token_rows[:], table[:, blocks:2 * blocks], ALU.add))
                for ins in round_to_whole(nc, line[:, 0:1], k.banks[6][0:1, 64:65], 1.0 / cut.unroll, (cut.unroll - 1) / (2.0 * cut.unroll)):
                    then(ins())
                then(nc.vector.tensor_copy(q.steps[:], line[:, 0:1]))

            @block.gpsimd
            def _(pool):
                nc.gpsimd.iota(count_lo[:], pattern=[[1, B], [0, U]], base=0, channel_multiplier=0,
                               allow_small_or_imprecise_dtypes=True)
                nc.gpsimd.iota(count_hi[:], pattern=[[1, blocks], [0, U]], base=0, channel_multiplier=0,
                               allow_small_or_imprecise_dtypes=True).then_inc(s["counted"], 1)
                pool.wait_ge(s["gated"], 1)
                nc.gpsimd.tensor_tensor(part[:], hot[0][:], pick(q.gates, 0), ALU.mult).then_inc(s["gates_spread"], 1)
                nc.gpsimd.tensor_tensor(rank[:], hot[1][:], pick(q.gates, 1), ALU.mult).then_inc(s["gates_spread"], 1)
                pool.wait_ge(s["gates_spread"], 2)
                nc.gpsimd.tensor_tensor(q.logits[:], part[:], rank[:], ALU.add).then_inc(s["gates_spread"], 1)
                pool.wait_ge(s["gates_spread"], 3)

            @block.scalar
            def _(act):
                if dense:
                    act.wait_ge(s["step"], 2)
                    nc.scalar.activation(q.logits[:], q.logits[:], ACT.Exp).then_inc(s["act_step"], 1)
                else:
                    act.wait_ge(s["step"], q.gate_step)
                    nc.scalar.activation(q.gates[:, :, 1:2], q.gates[:, :, 1:2], ACT.Exp).then_inc(s["act_step"], 1)
                with act.Fori(0, NG) as g:
                    for v in range(2):
                        act.wait_ge(s["hi_ready"], 2 * g + v + 1)
                        nc.scalar.activation(hot_hi[v][:, 1], is_hi[v][:], ACT.Copy, scale=r.col[0:T, :]).then_inc(s["rows_ready"], 1)

            @block.tensor
            def _(pe):
                pe.sem_inc(s["halves_free"], 2)
                pe.wait_ge(s["marked"], 1)
                counts = run[0]
                per = 512 // E
                for t0 in range(0, NT, per):
                    t1 = min(t0 + per, NT)
                    nc.tensor.matmul(ranks[:, t0 * E:t1 * E], r.tril[:], flat(both)[:, t0 * E:t1 * E], start=True, stop=False)
                    a0 = max(t0, 1)
                    nc.tensor.matmul(ranks[:, a0 * E:t1 * E], r.ones_b[:], flat(counts)[:, (a0 - 1) * E:(t1 - 1) * E], start=False, stop=True)
                nc.tensor.matmul(k.banks[5][0:E, 0:1], counts[:, NT - 1, :], r.ones_b[:, 0:1], start=True, stop=True).then_inc(s["pe_step"], 1)
                pe.wait_ge(s["placed"], 1)
                nc.tensor.matmul(k.banks[5][0:E, 8:9], r.tril_f[0:E, 0:E], col[:, 1:2], start=True, stop=True).then_inc(s["pe_step"], 1)
                pe.wait_ge(s["placed"], 2)
                nc.tensor.matmul(k.banks[6][0:T, 0:E], col[:, 2:3].broadcast_to([E, T]), r.ident[0:E, 0:E], start=True, stop=True)
                nc.tensor.matmul(k.banks[6][0:1, 64:65], r.ones[0:E, 0:1], col[:, 1:2], start=True, stop=True)
                nc.tensor.matmul(k.banks[7][0:1, 0:loads], r.ones[0:E, 0:1], ended[:], start=True, stop=True).then_inc(s["pe_step"], 1)
                nc.tensor.matmul(table, r.zeros[0:T, 0:B], r.zeros[0:T, 0:2 * blocks], start=True, stop=False)
                with pe.Fori(0, NG) as g:
                    for v in range(2):
                        pe.wait_ge(s["halves_ready"], 2 * g + v + 1)
                        pe.wait_ge(s["rows_ready"], 2 * g + v + 1)
                        for w in range(U):
                            done = nc.tensor.matmul(table, hot_lo[v][:, :, w], hot_hi[v][:, :, :, w], start=False, stop=False)
                        done.then_inc(s["halves_free"], 1)
                nc.tensor.matmul(table, r.zeros[0:T, 0:B], r.zeros[0:T, 0:2 * blocks], start=False, stop=True).then_inc(s["pe_step"], 1)


def run_experts(nc, name, r, q, experts, w1, w2, b1):
    cut = CUTS[experts]
    E, MU, W = experts, cut.unroll, cut.wide
    names = ("b1_in b1_turned b1_kept x_turned xT_kept up_ready hidden_ready down_ready y_kept idx_ready passed"
             + "".join(f" x_in{n} w1_in{n} w2_in{n}" for n in range(MU)) + " y_stored0 y_stored1")
    with phase(nc, name, names) as k:
        s, sb = k.s, k.sb
        x_in, w1_in, w2_in = ([s[f"{w}{n}"] for n in range(MU)] for w in ("x_in", "w1_in", "w2_in"))
        y_stored = [s["y_stored0"], s["y_stored1"]]
        w1s, w2s = sb("w1s", [128, MU, DC, H]), sb("w2s", [128, MU, HC, D])
        idx = sb("idx", [B, MU * W], I32)
        x = sb("x", [B, MU * W, D])
        xT = sb("xT", [128, 2, DC, W * B])
        hidden = sb("hidden", [128, 2, HC, W * B])
        y = sb("y", [B, 2, W, D])
        b1_rows, b1T = sb("b1_rows", [E, H]), sb("b1T", [128, HC, E])
        xT_ps = [k.banks[v][:, 0:DC * W * B] for v in range(2)]
        up_ps = [k.psum[:, 512 * (2 + 2 * v):512 * (2 + 2 * v) + HC * W * B] for v in range(2)]
        down_ps = [k.banks[6 + v][:, 0:W * D] for v in range(2)]
        w1_rows, w2_rows = w1.rearrange("e (c p) h -> e p c h", p=128), w2.rearrange("e (c p) h -> e p c h", p=128)
        expert = lambda eng, m: eng.value_load(q.expert_of[0:1, ds(m, 1)], min_val=0, max_val=E - 1)
        same = lambda eng, m: eng.value_load(q.same_of[0:1, ds(m, 1)], min_val=0, max_val=1)
        reuse = int(cut.reuse)
        loop_steps = lambda eng: eng.value_load(q.steps[0:1, 0:1], min_val=1, max_val=cut.steps)
        y_rows = q.outputs.rearrange("(m w p) d -> m p w d", p=B, w=W)

        with nc.Block() as block:
            @block.sync
            def _(sp):
                sp.dma_start(b1_rows[:], b1).then_inc(s["b1_in"], 16)

                def fetch(m, n):
                    e = expert(sp, m)
                    sp.wait_ge(s["up_ready"], m + 1 + reuse)
                    sp.dma_start(w1s[:, n], w1_rows[ds(e, 1)].rearrange("o p c h -> p (o c) h")).then_inc(w1_in[n], 16)
                    sp.wait_ge(s["down_ready"], m + 1 + reuse)
                    sp.dma_start(w2s[:, n], w2_rows[ds(e, 1)].rearrange("o p c h -> p (o c) h")).then_inc(w2_in[n], 16)

                def load(m, n):
                    if reuse:
                        with sp.If(same(sp, m) == 0):
                            fetch(m, n)
                    else:
                        fetch(m, n)
                fetch(0, 0)
                with sp.Fori(0, loop_steps(sp)) as i:
                    for u in range(MU):
                        load(MU * i + u + 1, (u + 1) % MU)
                n = loop_steps(sp)
                for w in (w1_in, w2_in):
                    for u in range(MU):
                        sp.wait_ge(w[u], 16 * n + (16 if u == 0 else 0))
                sp.sem_inc(s["passed"], 1)
                sp.wait_ge(s["b1_in"], 16)

            @block.gpsimd
            def _(pool):
                def gather(m, n):
                    pool.wait_ge(s["x_turned"], m + 1)
                    pool.sem_inc(s["passed"], 1)
                    nc.gpsimd.tensor_copy(idx[:, W * n:W * n + W], q.token_of[:, ds(W * m, W)]).then_inc(s["idx_ready"], 1)
                    pool.wait_ge(s["idx_ready"], m + 1)
                    pool.sem_inc(s["passed"], 1)
                    for w in range(W * n, W * n + W):
                        nc.gpsimd.indirect_dma_start(out=x[:, w, :], out_offset=None, in_=q.tokens[:, :],
                                                     in_offset=bass.IndirectOffsetOnAxis(ap=idx[:, w:w + 1], axis=0)).then_inc(x_in[n], 16)
                gather(0, 0)
                gather(1, 1)
                with pool.Fori(0, loop_steps(pool)) as i:
                    for u in range(MU):
                        gather(MU * i + u + 2, (u + 2) % MU)

            @block.vector
            def _(dve):
                dve.wait_ge(s["b1_turned"], 1)
                nc.vector.tensor_copy(b1T[:], k.banks[7][:, 0:HC * E].rearrange("p (c e) -> p c e", c=HC)).then_inc(s["b1_kept"], 1)
                dve.wait_ge(s["b1_kept"], 1)
                dve.sem_inc(s["xT_kept"], 2)
                dve.sem_inc(s["y_kept"], 2)

                def keep_x(m, v):
                    dve.wait_ge(s["x_turned"], m + 1 + MU)
                    dve.wait_ge(s["up_ready"], m + MU - 1)
                    nc.vector.tensor_copy(xT[:, v], xT_ps[v].rearrange("p (c t) -> p c t", c=DC)).then_inc(s["xT_kept"], 1)

                def keep_y(m, v, uses):
                    dve.wait_ge(s["down_ready"], m + 1 + MU)
                    dve.wait_ge(y_stored[v], 16 * uses + 16)
                    nc.vector.tensor_copy(y[:, v].rearrange("p w d -> p (w d)"), down_ps[v]).then_inc(s["y_kept"], 1)

                def copy_weights(m, n, ready, w_in, ws, landed):
                    if reuse:
                        with dve.If(same(dve, m) == 1):
                            dve.wait_ge(ready, m + 1)
                            dve.wait_ge(w_in[(n - 1) % MU], landed)
                            nc.vector.tensor_copy(ws[:, n], ws[:, (n - 1) % MU]).then_inc(w_in[n], 16)
                keep_x(0, 0)
                keep_x(1, 1)
                copy_weights(1, 1, s["up_ready"], w1_in, w1s, 16)
                with dve.Fori(0, loop_steps(dve)) as i:
                    for u in range(MU):
                        m = MU * i + u
                        keep_x(m + 2, u % 2)
                        copy_weights(m + 2, (u + 2) % MU, s["up_ready"], w1_in, w1s, 16 * i + 16 * (1 + (u + 1) // MU))
                        copy_weights(m + 1, (u + 1) % MU, s["down_ready"], w2_in, w2s, 16 * i + 16)
                        keep_y(m, u % 2, MU // 2 * i + u // 2)

            @block.scalar
            def _(act):
                act.sem_inc(s["hidden_ready"], 2)
                act.sem_inc(y_stored[0], 16)
                act.sem_inc(y_stored[1], 16)
                act.wait_ge(s["b1_kept"], 1)

                def activate(m, v):
                    e = expert(act, m)
                    act.wait_ge(s["up_ready"], m + 1 + MU)
                    act.wait_ge(s["down_ready"], m + MU - 1)
                    for j in range(HC):
                        done = nc.scalar.activation(hidden[:, v, j, :], up_ps[v][:, j * W * B:(j + 1) * W * B], ACT.Gelu,
                                                    bias=b1T[:, j, ds(e, 1)])
                    done.then_inc(s["hidden_ready"], 1)
                activate(0, 0)
                with act.Fori(0, loop_steps(act)) as i:
                    for u in range(MU):
                        activate(MU * i + u + 1, (u + 1) % 2)
                        act.wait_ge(s["y_kept"], MU * i + u + 1 + 2)
                        act.dma_start(y_rows[ds(MU * i + u, 1)].rearrange("o p w d -> p (o w) d"), y[:, u % 2]).then_inc(y_stored[u % 2], 16)
                n = loop_steps(act)
                for v in range(2):
                    act.wait_ge(y_stored[v], MU // 2 * 16 * n + 16)
                act.sem_inc(s["passed"], 1)

            @block.tensor
            def _(pe):
                pe.wait_ge(s["b1_in"], 16)
                for c in range(HC):
                    done = nc.tensor.transpose(k.banks[7][:, c * E:(c + 1) * E], b1_rows[:, c * 128:(c + 1) * 128], r.ident[0:E, 0:E])
                done.then_inc(s["b1_turned"], 1)
                for primed in (s["x_turned"], s["up_ready"], s["down_ready"]):
                    pe.sem_inc(primed, MU)

                def turn(m, v, n, landed):
                    pe.wait_ge(x_in[n], landed)
                    pe.wait_ge(s["xT_kept"], m + 1)
                    for c in range(DC):
                        for w in range(W):
                            done = nc.tensor.transpose(xT_ps[v][:, (c * W + w) * B:(c * W + w + 1) * B],
                                                       x[:, W * n + w, c * 128:(c + 1) * 128], r.ident[:])
                    done.then_inc(s["x_turned"], 1)

                def up(m, v, n, landed):
                    pe.wait_ge(w1_in[n], landed)
                    pe.wait_ge(s["hidden_ready"], m + 1)
                    pe.wait_ge(s["xT_kept"], m + 3)
                    for j in range(HC):
                        for c in range(DC):
                            done = nc.tensor.matmul(up_ps[v][:, j * W * B:(j + 1) * W * B], w1s[:, n, c, j * 128:(j + 1) * 128], xT[:, v, c, :],
                                                    start=c == 0, stop=c == DC - 1)
                    done.then_inc(s["up_ready"], 1)

                def down(m, v, n, landed):
                    pe.wait_ge(w2_in[n], landed)
                    pe.wait_ge(s["y_kept"], m + 1)
                    pe.wait_ge(s["hidden_ready"], m + 3)
                    for w in range(W):
                        for j in range(HC):
                            done = nc.tensor.matmul(down_ps[v][:, w * D:(w + 1) * D], hidden[:, v, j, w * B:(w + 1) * B], w2s[:, n, j, :],
                                                    start=j == 0, stop=j == HC - 1)
                    done.then_inc(s["down_ready"], 1)
                turn(0, 0, 0, 16 * W)
                turn(1, 1, 1, 16 * W)
                up(0, 0, 0, 16)
                with pe.Fori(0, loop_steps(pe)) as i:
                    for u in range(MU):
                        turn(MU * i + u + 2, u % 2, (u + 2) % MU, 16 * W * i + 16 * W * (1 + (u + 2) // MU))
                        up(MU * i + u + 1, (u + 1) % 2, (u + 1) % MU, 16 * i + 16 * (1 + (u + 1) // MU))
                        down(MU * i + u, u % 2, u, 16 * i + 16)


def combine(nc, name, r, q, experts, b2, out):
    names = ("b2_in idx_ready passed joined1 joined2 joined3 gates_staged gates_turned gatesT_kept bias_ready summed out_stored"
             + "".join(f" y_in{n}" for n in range(2 * U)))
    E = experts
    with phase(nc, name, names) as k:
        s, sb = k.s, k.sb
        y_in = [s[f"y_in{n}"] for n in range(2 * U)]
        b2s = sb("b2", [E, D])
        idx = sb("idx", [T, 2 * U], I32)
        y = sb("y", [T, 2 * U, D])
        total = sb("total", [T, U, D])
        gates_s, gatesT = sb("gates_s", [T, U, E]), sb("gatesT", [E, U, T])
        turned = [k.banks[u // 4][0:E, (u % 4) * T:(u % 4 + 1) * T] for u in range(U)]
        bias = [k.banks[2 + u // 2][0:T, (u % 2) * 256:(u % 2) * 256 + 256] for u in range(U)]
        sums = k.banks[7][0:T, 0:D]
        home = r.nodes if out is None else r.acc
        tile3 = lambda t, i: t[:, ds(i, 1), :].rearrange("p o d -> p (o d)")
        slots = q.slots[:].rearrange("p i n -> p (i n)")
        gates = q.gates[:].rearrange("p i n -> p (i n)")
        with nc.Block() as block:
            @block.sync
            def _(sp):
                sp.dma_start(b2s[:], b2).then_inc(s["b2_in"], 16)
                if out is not None:
                    with sp.Fori(0, NG) as g:
                        sp.wait_ge(s["joined3"], U * g + 2 * U)
                        for p0, p1 in ((0, SPLIT), (SPLIT, T)):
                            sp.dma_start(rows_of(out, g)[p0:p1], home[p0:p1, ds(U * g, U), :]).then_inc(s["out_stored"], 16)
                    sp.wait_ge(s["out_stored"], 32 * NG)
                sp.wait_ge(s["b2_in"], 16)

            @block.gpsimd
            def _(pool):
                with pool.Fori(0, NG) as g:
                    for u in range(U):
                        i = U * g + u
                        pool.wait_ge(s["joined3"], i + 1)
                        nc.gpsimd.tensor_copy(idx[:, 2 * u:2 * u + 2], slots[:, ds(2 * i, 2)]).then_inc(s["idx_ready"], 1)
                        pool.wait_ge(s["idx_ready"], i + 1)
                        pool.sem_inc(s["passed"], 1)
                        for n in range(2):
                            w = 2 * u + n
                            nc.gpsimd.indirect_dma_start(out=y[:, w, :], out_offset=None, in_=q.outputs[:, :],
                                                         in_offset=bass.IndirectOffsetOnAxis(ap=idx[:, w:w + 1], axis=0)).then_inc(y_in[w], 16)

            @block.vector
            def _(dve):
                dve.sem_inc(s["joined3"], U)
                with dve.Fori(0, NG) as g:
                    for u in range(U):
                        nc.vector.tensor_copy(gates_s[:, u, :], tile3(q.logits, U * g + u)).then_inc(s["gates_staged"], 1)
                    dve.wait_ge(s["bias_ready"], U * g + U)
                    for u in range(U):
                        i = U * g + u
                        nc.vector.tensor_tensor(total[:, u, :], bias[u], tile3(home, i), ALU.add).then_inc(s["joined1"], 1)
                    for u in range(U):
                        i = U * g + u
                        dve.wait_ge(s["joined1"], i + 1)
                        dve.wait_ge(y_in[2 * u], 16 * g + 16)
                        nc.vector.scalar_tensor_tensor(total[:, u, :], y[:, 2 * u, :], gates[:, ds(2 * i, 1)], total[:, u, :],
                                                       ALU.mult, ALU.add).then_inc(s["joined2"], 1)
                    for u in range(U):
                        i = U * g + u
                        dve.wait_ge(s["joined2"], i + 1)
                        dve.wait_ge(y_in[2 * u + 1], 16 * g + 16)
                        nc.vector.scalar_tensor_tensor(tile3(home, i), y[:, 2 * u + 1, :], gates[:, ds(2 * i + 1, 1)], total[:, u, :],
                                                       ALU.mult, ALU.add).then_inc(s["joined3"], 1)

            @block.scalar
            def _(act):
                with act.Fori(0, NG) as g:
                    act.wait_ge(s["gates_turned"], U * g + U)
                    for u in range(U):
                        nc.scalar.activation(gatesT[:, u, :], turned[u], ACT.Copy).then_inc(s["gatesT_kept"], 1)

            @block.tensor
            def _(pe):
                pe.wait_ge(s["b2_in"], 16)
                if out is None:
                    nc.tensor.matmul(sums, r.zeros[0:T, 0:T], r.zeros[0:T, 0:D], start=True, stop=False)
                with pe.Fori(0, NG) as g:
                    for u in range(U):
                        pe.wait_ge(s["gates_staged"], U * g + u + 1)
                        pe.sem_inc(s["passed"], 1)
                        nc.tensor.transpose(turned[u], gates_s[:, u, :], r.ident[0:T, 0:T]).then_inc(s["gates_turned"], 1)
                    for u in range(U):
                        pe.wait_ge(s["gatesT_kept"], U * g + u + 1)
                        nc.tensor.matmul(bias[u], gatesT[:, u, :], b2s[:], start=True, stop=True).then_inc(s["bias_ready"], 1)
                    if out is None:
                        for u in range(U):
                            pe.wait_ge(s["joined3"], U * g + u + 1 + U)
                            nc.tensor.matmul(sums, r.ones[:], tile3(r.nodes, U * g + u), start=False, stop=False)
                if out is None:
                    nc.tensor.matmul(sums, r.zeros[0:T, 0:T], r.zeros[0:T, 0:D], start=False, stop=True).then_inc(s["summed"], 1)
                    pe.wait_ge(s["summed"], 1)
            if out is None:
                @block.vector
                def _(dve):
                    dve.wait_ge(s["summed"], 1)
                    nc.vector.tensor_scalar(q.mean[:], sums, 1.0 / N, None, ALU.mult).then_inc(s["joined1"], 1)
                    dve.wait_ge(s["joined1"], NT + 1)


def batch_norm(nc, d, r, q, p):
    names = ("passed loaded centred squared squares_free squared_sum step roots"
             " product sum_ready sum_stats sum_moments sum_root sum_inverse x_ready x_stored xT_ready xT_kept logits_ready logits_kept")
    with phase(nc, "norm", names) as k:
        s, sb = k.s, k.sb
        gamma, spread = sb("gamma", [T, D]), sb("spread", [T, D])
        gate_w, gate_b = sb("gate_w", [128, DC, E_FFN]), sb("gate_b", [T, E_FFN])
        squares = sb("squares", [T, U, D])
        stats, moments, root = sb("stats", [T, U, 6]), sb("moments", [T, U, 2]), sb("root", [T, U])
        x = sb("x", [T, U, D])
        xT = sb("xT", [128, U, DC, T])
        sums = k.banks[7][0:T, 0:D]
        turned = [k.banks[u // 2][:, (u % 2) * 256:(u % 2) * 256 + DC * T] for u in range(U)]
        logit_ps = k.banks[3][0:T, 0:U * E_FFN]
        tile3 = lambda t, i: t[:, ds(i, 1), :].rearrange("p o d -> p (o d)")
        with nc.Block() as block:
            @block.sync
            def _(sp):
                for p0, p1 in ((0, SPLIT), (SPLIT, T)):
                    sp.dma_start(gamma[p0:p1], d["gnn_gamma"].partition_broadcast(p1 - p0)).then_inc(s["loaded"], 16)
                    sp.dma_start(gate_b[p0:p1], d["ffn_gate_b"].partition_broadcast(p1 - p0)).then_inc(s["loaded"], 16)
                sp.dma_start(gate_w[:], d["ffn_gate_w"].rearrange("(c p) n -> p c n", p=128)).then_inc(s["loaded"], 16)
                sp.sem_inc(s["x_stored"], 32)
                with sp.Fori(0, NG) as g:
                    sp.wait_ge(s["x_ready"], U * g + U)
                    for p0, p1 in ((0, SPLIT), (SPLIT, T)):
                        sp.dma_start(rows_of(p.tokens, g)[p0:p1], x[p0:p1]).then_inc(s["x_stored"], 16)
                sp.wait_ge(s["x_stored"], 32 * NG + 32)
                sp.wait_ge(s["loaded"], 80)

            @block.vector
            def _(dve):
                five = lambda x: x[:].unsqueeze(1).broadcast_to([T, U, D])
                group = lambda x, g: x[:, ds(U * g, U), :]
                with dve.Fori(0, NG) as g:
                    nc.vector.tensor_tensor(group(r.nodes, g), group(r.nodes, g), five(q.mean), ALU.subtract).then_inc(s["centred"], 1)
                dve.wait_ge(s["squared_sum"], 1)
                nc.vector.tensor_scalar(spread[:], sums, 1.0 / N, None, ALU.mult).then_inc(s["step"], 1)
                dve.wait_ge(s["roots"], 1)
                nc.vector.reciprocal(spread[:], spread[:]).then_inc(s["step"], 1)
                dve.wait_ge(s["step"], 2)
                dve.wait_ge(s["loaded"], 80)
                nc.vector.tensor_tensor(spread[:], spread[:], gamma[:], ALU.mult).then_inc(s["step"], 1)
                dve.wait_ge(s["step"], 3)

                def residual(g):
                    nc.vector.tensor_tensor(group(r.nodes, g), group(r.nodes, g), five(spread), ALU.mult).then_inc(s["product"], 1)
                    dve.wait_ge(s["product"], g + 1)
                    nc.vector.tensor_tensor(group(r.acc, g), group(r.acc, g), group(r.nodes, g), ALU.add).then_inc(s["sum_ready"], 1)
                    dve.wait_ge(s["sum_ready"], g + 1)
                    dve.sem_inc(s["passed"], 1)
                    for u in range(U):
                        nc.vector.bn_stats(stats[:, u, :], tile3(r.acc, U * g + u)).then_inc(s["sum_stats"], 1)
                    dve.wait_ge(s["sum_stats"], U * g + U)
                    dve.sem_inc(s["passed"], 1)
                    for u in range(U):
                        nc.vector.bn_aggr(moments[:, u, :], stats[:, u, :]).then_inc(s["sum_moments"], 1)

                def keep_logits(g):
                    dve.wait_ge(s["logits_ready"], U * g + U)
                    nc.vector.tensor_tensor(p.logits[:, ds(U * g, U), :], logit_ps.rearrange("p (u n) -> p u n", u=U),
                                            gate_b[:].unsqueeze(1).broadcast_to([T, U, E_FFN]), ALU.add).then_inc(s["logits_kept"], 1)

                def normalised(g):
                    dve.wait_ge(s["sum_root"], g + 1)
                    nc.vector.reciprocal(root[:], root[:]).then_inc(s["sum_inverse"], 1)
                    dve.wait_ge(s["sum_inverse"], g + 1)
                    dve.wait_ge(s["x_stored"], 32 * g + 32)
                    for u in range(U):
                        i = U * g + u
                        nc.vector.tensor_scalar(x[:, u, :], tile3(r.acc, i), moments[:, u, 0:1], root[:, u:u + 1],
                                                ALU.subtract, ALU.mult).then_inc(s["x_ready"], 1)

                residual(0)
                normalised(0)
                with dve.Fori(1, NG) as g:
                    residual(g)
                    keep_logits(g - 1)
                    normalised(g)
                keep_logits(NG - 1)

            @block.scalar
            def _(act):
                with act.Fori(0, NG) as g:
                    for u in range(U):
                        i = U * g + u
                        act.wait_ge(s["centred"], g + 1)
                        act.wait_ge(s["squares_free"], i + 1)
                        nc.scalar.activation(squares[:, u, :], tile3(r.nodes, i), ACT.Square).then_inc(s["squared"], 1)
                act.wait_ge(s["step"], 1)
                nc.scalar.activation(spread[:], spread[:], ACT.Sqrt, bias=r.eps[0:T, :]).then_inc(s["roots"], 1)
                with act.Fori(0, NG) as g:
                    act.wait_ge(s["sum_moments"], U * g + U)
                    nc.scalar.activation(root[:], moments[:, :, 1], ACT.Sqrt, bias=r.eps[0:T, :]).then_inc(s["sum_root"], 1)
                    act.wait_ge(s["xT_ready"], U * g + U)
                    for u in range(U):
                        nc.scalar.activation(xT[:, u], turned[u].rearrange("p (c t) -> p c t", c=DC), ACT.Copy).then_inc(s["xT_kept"], 1)

            @block.tensor
            def _(pe):
                pe.sem_inc(s["squares_free"], U)
                nc.tensor.matmul(sums, r.zeros[0:T, 0:T], r.zeros[0:T, 0:D], start=True, stop=False)
                with pe.Fori(0, NG) as g:
                    for u in range(U):
                        pe.wait_ge(s["squared"], U * g + u + 1)
                        nc.tensor.matmul(sums, r.ones[:], squares[:, u, :], start=False, stop=False).then_inc(s["squares_free"], 1)
                nc.tensor.matmul(sums, r.zeros[0:T, 0:T], r.zeros[0:T, 0:D], start=False, stop=True).then_inc(s["squared_sum"], 1)
                pe.wait_ge(s["loaded"], 80)
                with pe.Fori(0, NG) as g:
                    for u in range(U):
                        pe.wait_ge(s["x_ready"], U * g + u + 1)
                        for c in range(DC):
                            done = nc.tensor.transpose(turned[u][:, c * T:(c + 1) * T], x[:, u, c * 128:(c + 1) * 128], r.ident[0:T, 0:T])
                        done.then_inc(s["xT_ready"], 1)
                    for u in range(U):
                        pe.wait_ge(s["xT_kept"], U * g + u + 1)
                        for c in range(DC):
                            done = nc.tensor.matmul(logit_ps[:, u * E_FFN:(u + 1) * E_FFN], xT[:, u, c, :], gate_w[:, c, :], start=c == 0, stop=c == DC - 1)
                        done.then_inc(s["logits_ready"], 1)


def program(nc, d, out):
    with ExitStack() as scope:
        r = resident(nc, scope)
        constants(nc, r)
        sb = lambda where, n, shape, dt=F32: where.enter_context(nc.sbuf_tensor(n, shape, dt))

        def layer(where, name, experts):
            cut = CUTS[experts]
            kept = Bag()
            kept.logits = sb(where, f"{name}_logits", [T, NT, experts])
            kept.top = sb(where, f"{name}_top", [T, NT, 2])
            kept.choice = sb(where, f"{name}_choice", [T, NT, 2])
            kept.gates = sb(where, f"{name}_gates", [T, NT, 2])
            kept.slots = sb(where, f"{name}_slots", [T, NT, 2], I32)
            kept.token_of = sb(where, f"{name}_token_of", [B, cut.blocks + cut.wide * cut.unroll], I32)
            kept.expert_of = sb(where, f"{name}_expert_of", [1, cut.loads + cut.unroll], I32)
            kept.same_of = sb(where, f"{name}_same_of", [1, cut.loads + cut.unroll], I32)
            kept.steps = sb(where, f"{name}_steps", [1, 1], I32)
            kept.tokens = nc.dram_tensor(f"{name}_tokens", (N, D), F32, kind="Internal").ap()
            kept.outputs = nc.dram_tensor(f"{name}_outputs", (cut.blocks * B, D), F32, kind="Internal").ap()
            return kept
        with ExitStack() as graph_scope:
            q = layer(graph_scope, "graph", E_GNN)
            p = layer(graph_scope, "dense", E_FFN)
            q.mean = sb(graph_scope, "column_mean", [T, D])
            with ExitStack() as mix_scope:
                m = lambda n, shape, dt=F32: sb(mix_scope, n, shape, dt)
                a = Bag()
                a.hn, a.xnT, a.qk = m("hn", [T, NT, D]), m("xnT", [128, DC, N]), m("qk", [T, NT, 2 * HR])
                a.src_idx, a.dst_t = m("src_idx", [T, EC + EPAD], I32), m("dst_t", [T, EC + EPAD])
                a.visit_tab, a.rs_out = m("visit_tab", [1, 3, NT], I32), m("rs_out", [T, NT])
                a.wx, a.wv, a.wo = m("wx", [128, DC, D]), m("wv", [128, 128]), m("wo", [128, DC, D])
                a.w_gc, a.w_res, a.wg = m("w_gc", [128, DC, D]), m("w_res", [128, DC, D]), m("wg", [128, DC, E_GNN])
                a.cols = m("cols", [128, 22])
                a.bx_row, a.g1_bc, a.b1_bc = m("bx_row", [1, D]), m("g1_bc", [HR, D]), m("b1_bc", [HR, D])
                a.b2_bc, a.bg_bc, a.beta_bc = m("b2_bc", [T, D]), m("bg_bc", [T, E_GNN]), m("beta_bc", [T, D])
                a.m_aug = m("m_aug", [HR + 1, D])
                a.h_dram = nc.dram_tensor("scaled_nodes", (N, D), F32, kind="Internal").ap()
                prepare(nc, d, r, a, (q, p))
                a.w1, a.w2 = m("w1", [128, DC, FF]), m("w2", [128, FC, D])
                attention_state(nc, d, r, a)
                graph_and_mix(nc, d, r, a, q, p)
            route(nc, "graph_route", r, q, E_GNN, CAP, dense=False)
            run_experts(nc, "graph_experts", r, q, E_GNN, d["gnn_w1"], d["gnn_w2"], d["gnn_b1"])
            combine(nc, "graph_combine", r, q, E_GNN, d["gnn_b2"], None)
            batch_norm(nc, d, r, q, p)
            route(nc, "dense_route", r, p, E_FFN, 2 * N, dense=True)
            run_experts(nc, "dense_experts", r, p, E_FFN, d["ffn_W1"], d["ffn_W2"], d["ffn_b1"])
            combine(nc, "dense_combine", r, p, E_FFN, d["ffn_b2"], out)


_INS = ["x", "src", "dst", "gnn_W_gc", "gnn_b_gc", "gnn_W_res", "gnn_b_res", "gnn_Wg", "gnn_bg", "gnn_w1", "gnn_b1", "gnn_w2", "gnn_b2",
        "gnn_gamma", "gnn_beta", "mix_ln1_g", "mix_ln1_b", "mix_Wx", "mix_bx", "mix_Wq", "mix_Wk", "mix_Wv", "mix_Wo", "mix_bo",
        "mix_ln2_g", "mix_ln2_b", "mix_W1", "mix_b1", "mix_W2", "mix_b2",
        "ffn_gate_w", "ffn_gate_b", "ffn_W1", "ffn_b1", "ffn_W2", "ffn_b2"]


def kernel(**inputs):
    import numpy as _np
    import concourse.bacc as _bacc
    from concourse import mybir as _mybir
    from concourse.bass_utils import run_bass_kernel_spmd as _run

    nc = _bacc.Bacc("TRN2", target_bir_lowering=False, num_devices=1)
    arrays, args = {}, {}
    for name in _INS:
        a = _np.ascontiguousarray(inputs[name if name in inputs else "L0_" + name])
        arrays[f"in_{name}"] = a
        args[name] = nc.dram_tensor(f"in_{name}", a.shape, _mybir.dt.from_np(a.dtype), kind="ExternalInput").ap()
    out = nc.dram_tensor("out_0", (N, D), F32, kind="ExternalOutput").ap()
    program(nc, args, out)
    return _run(nc, [arrays], core_ids=[0]).results[0]["out_0"]
```
